# Optimizing a Trainium2 kernel written in Bass

```python
import numpy as np
import jax
import jax.numpy as jnp

def _softmax(x, axis=-1):
    return jax.nn.softmax(x, axis=axis)

def _gelu(x):
    return jax.nn.gelu(x, approximate=True)

def _silu(x):
    return jax.nn.silu(x)

def _sigmoid(x):
    return jax.nn.sigmoid(x)

def _layernorm(x, axis=-1, eps=1e-05):
    m = jnp.mean(x, axis=axis, keepdims=True)
    v = jnp.var(x, axis=axis, keepdims=True)
    return (x - m) / jnp.sqrt(v + eps)

def _scatter_add(tgt, idx, src, axis=0):
    return tgt.at[idx].add(src)

def _segment_sum(src, seg, n):
    return jax.ops.segment_sum(src, seg, n)
kernel_name = 'mk_gnn_resnorm_d4_gnn_r64_4beec7'

def setup_inputs(seed: int=0):
    np.random.seed(seed)
    _w = jnp.asarray

    def _rec_inputs():
        import jax
        import jax.numpy as jnp
        _gk = jax.random.key(seed)
        x = -0.000202 + 1 * jax.random.normal(jax.random.fold_in(_gk, 1), (100000, 64), jnp.float32)
        src = jax.random.randint(jax.random.fold_in(_gk, 2), (50000,), 0, 100000, jnp.int32)
        dst = jax.random.randint(jax.random.fold_in(_gk, 3), (50000,), 0, 100000, jnp.int32)
        _o = jnp.argsort(dst, stable=True)
        src = src[_o]
        dst = dst[_o]
        edge_attr_32 = 0.000216709 + 1.00012 * jax.random.normal(jax.random.fold_in(_gk, 12), (50000, 32), jnp.float32)
        return (x, src, dst, edge_attr_32)
    x, src, dst, edge_attr_32 = _rec_inputs()

    def _L0_gnn_setup():
        import jax, jax.numpy as jnp
        import numpy as np
        N_NODES = 100000
        N_EDGES = 25000

        def _mean_agg(h, src, dst, deg):
            summed = jax.ops.segment_sum(h[src], dst, num_segments=N_NODES)
            return summed / deg[:, None]

        def _sage_layer(h, src, dst, deg, w_self, w_neigh, b):
            h_neigh = _mean_agg(h, src, dst, deg)
            return jax.nn.relu(h @ w_self + h_neigh @ w_neigh + b)
        key = jax.random.key(seed)
        ks = jax.random.split(key, 10)
        feat = jax.random.normal(ks[0], (N_NODES, 64), dtype=jnp.float32)
        src = jax.random.randint(ks[1], (N_EDGES,), 0, N_NODES, dtype=jnp.int32)
        dst = jax.random.randint(ks[2], (N_EDGES,), 0, N_NODES, dtype=jnp.int32)

        def lin(k, din, dout):
            return jax.random.normal(k, (din, dout), dtype=jnp.float32) * (1.0 / np.sqrt(din))
        return {'feat': feat, 'src': src, 'dst': dst, 'ws0': lin(ks[3], 64, 128), 'wn0': lin(ks[4], 64, 128), 'b0': jnp.zeros((128,), jnp.float32), 'ws1': lin(ks[5], 128, 128), 'wn1': lin(ks[6], 128, 128), 'b1': jnp.zeros((128,), jnp.float32), 'ws2': lin(ks[7], 128, 64), 'wn2': lin(ks[8], 128, 64), 'b2': jnp.zeros((64,), jnp.float32)}
    _L0_gnn_all = _L0_gnn_setup()
    _L0_gnn_in = {k: v for k, v in _L0_gnn_all.items() if k in ('ws0', 'wn0', 'b0', 'ws1', 'wn1', 'b1', 'ws2', 'wn2', 'b2')}
    del _L0_gnn_all

    def _L1_gnn_setup():
        import jax, jax.numpy as jnp
        import numpy as np
        N_NODES = 100000

        def gcn_conv(x, W, b, src, dst, num_nodes):
            xw = x @ W
            loop = jnp.arange(num_nodes, dtype=src.dtype)
            s = jnp.concatenate([src, loop])
            d = jnp.concatenate([dst, loop])
            deg = jax.ops.segment_sum(jnp.ones_like(d, dtype=xw.dtype), d, num_segments=num_nodes)
            dis = jnp.where(deg > 0, jax.lax.rsqrt(deg), 0.0)
            norm = dis[s] * dis[d]
            msg = norm[:, None] * xw[s]
            out = jax.ops.segment_sum(msg, d, num_segments=num_nodes)
            return out + b
        key = jax.random.key(seed)
        k1, k2, k3, k4 = jax.random.split(key, 4)
        F, H, E = (64, 64, 1250000)
        x = jax.random.normal(k1, (N_NODES, F), dtype=jnp.float32)
        edge_index = jax.random.randint(k2, (2, E), 0, N_NODES, dtype=jnp.int64)
        W1 = jax.random.normal(k3, (F, H), dtype=jnp.float32) * (1.0 / np.sqrt(F))
        b1 = jnp.zeros((H,), dtype=jnp.float32)
        W2 = jax.random.normal(k4, (H, F), dtype=jnp.float32) * (1.0 / np.sqrt(H))
        b2 = jnp.zeros((F,), dtype=jnp.float32)
        return {'x': x, 'edge_index': edge_index, 'W1': W1, 'b1': b1, 'W2': W2, 'b2': b2}
    _L1_gnn_all = _L1_gnn_setup()
    _L1_gnn_in = {k: v for k, v in _L1_gnn_all.items() if k in ('W1', 'b1', 'W2', 'b2')}
    del _L1_gnn_all

    def _L2_gnn_setup():
        import jax, jax.numpy as jnp
        import numpy as np
        N_NODES = 100000
        N_EDGES = 25000
        DIM = 64
        key = jax.random.key(seed)
        k = jax.random.split(key, 6)
        x = jax.random.normal(k[0], (N_NODES, DIM), dtype=jnp.float32)
        edge_index = jax.random.randint(k[1], (2, N_EDGES), 0, N_NODES, dtype=jnp.int32)
        s = 1.0 / np.sqrt(DIM)
        W1 = jax.random.normal(k[2], (DIM, DIM), dtype=jnp.float32) * s
        b1 = jnp.zeros((DIM,), dtype=jnp.float32)
        W2 = jax.random.normal(k[3], (DIM, DIM), dtype=jnp.float32) * s
        b2 = jnp.zeros((DIM,), dtype=jnp.float32)
        return {'x': x, 'edge_index': edge_index, 'W1': W1, 'b1': b1, 'W2': W2, 'b2': b2}
    _L2_gnn_all = _L2_gnn_setup()
    _L2_gnn_in = {k: v for k, v in _L2_gnn_all.items() if k in ('W1', 'b1', 'W2', 'b2')}
    del _L2_gnn_all

    def _L3_gnn_setup():
        import jax, jax.numpy as jnp
        import numpy as np
        N_NODES = 50000
        N_EDGES = 12500
        D_NODE = 64
        D_EDGE = 32
        D_HID = 128

        def _mlp(x, W1, b1, W2, b2):
            return jax.nn.relu(x @ W1 + b1) @ W2 + b2
        key = jax.random.key(seed)
        ks = jax.random.split(key, 12)
        inp = {'nodes': jax.random.normal(ks[0], (N_NODES, D_NODE), dtype=jnp.float32), 'row': jax.random.randint(ks[1], (N_EDGES,), 0, N_NODES, dtype=jnp.int32), 'col': jax.random.randint(ks[2], (N_EDGES,), 0, N_NODES, dtype=jnp.int32), 'edge_features': jax.random.normal(ks[3], (N_EDGES, D_EDGE), dtype=jnp.float32)}
        d_in_msg = 2 * D_NODE + D_EDGE
        inp['mW1'] = jax.random.normal(ks[4], (d_in_msg, D_HID), dtype=jnp.float32) / np.sqrt(d_in_msg)
        inp['mb1'] = jnp.zeros((D_HID,), dtype=jnp.float32)
        inp['mW2'] = jax.random.normal(ks[5], (D_HID, D_NODE), dtype=jnp.float32) / np.sqrt(D_HID)
        inp['mb2'] = jnp.zeros((D_NODE,), dtype=jnp.float32)
        d_in_upd = 2 * D_NODE
        inp['uW1'] = jax.random.normal(ks[6], (d_in_upd, D_HID), dtype=jnp.float32) / np.sqrt(d_in_upd)
        inp['ub1'] = jnp.zeros((D_HID,), dtype=jnp.float32)
        inp['uW2'] = jax.random.normal(ks[7], (D_HID, D_NODE), dtype=jnp.float32) / np.sqrt(D_HID)
        inp['ub2'] = jnp.zeros((D_NODE,), dtype=jnp.float32)
        return inp
    _L3_gnn_all = _L3_gnn_setup()
    _L3_gnn_in = {k: v for k, v in _L3_gnn_all.items() if k in ('mW1', 'mb1', 'mW2', 'mb2', 'uW1', 'ub1', 'uW2', 'ub2')}
    del _L3_gnn_all
    return {'x': x, 'src': src, 'dst': dst, 'edge_attr_32': edge_attr_32, 'L0_gnn_ws0': _L0_gnn_in['ws0'], 'L0_gnn_wn0': _L0_gnn_in['wn0'], 'L0_gnn_b0': _L0_gnn_in['b0'], 'L0_gnn_ws1': _L0_gnn_in['ws1'], 'L0_gnn_wn1': _L0_gnn_in['wn1'], 'L0_gnn_b1': _L0_gnn_in['b1'], 'L0_gnn_ws2': _L0_gnn_in['ws2'], 'L0_gnn_wn2': _L0_gnn_in['wn2'], 'L0_gnn_b2': _L0_gnn_in['b2'], 'L1_gnn_W1': _L1_gnn_in['W1'], 'L1_gnn_b1': _L1_gnn_in['b1'], 'L1_gnn_W2': _L1_gnn_in['W2'], 'L1_gnn_b2': _L1_gnn_in['b2'], 'L2_gnn_W1': _L2_gnn_in['W1'], 'L2_gnn_b1': _L2_gnn_in['b1'], 'L2_gnn_W2': _L2_gnn_in['W2'], 'L2_gnn_b2': _L2_gnn_in['b2'], 'L3_gnn_mW1': _L3_gnn_in['mW1'], 'L3_gnn_mb1': _L3_gnn_in['mb1'], 'L3_gnn_mW2': _L3_gnn_in['mW2'], 'L3_gnn_mb2': _L3_gnn_in['mb2'], 'L3_gnn_uW1': _L3_gnn_in['uW1'], 'L3_gnn_ub1': _L3_gnn_in['ub1'], 'L3_gnn_uW2': _L3_gnn_in['uW2'], 'L3_gnn_ub2': _L3_gnn_in['ub2']}

def reference(x, src, dst, edge_attr_32, L0_gnn_ws0, L0_gnn_wn0, L0_gnn_b0, L0_gnn_ws1, L0_gnn_wn1, L0_gnn_b1, L0_gnn_ws2, L0_gnn_wn2, L0_gnn_b2, L1_gnn_W1, L1_gnn_b1, L1_gnn_W2, L1_gnn_b2, L2_gnn_W1, L2_gnn_b1, L2_gnn_W2, L2_gnn_b2, L3_gnn_mW1, L3_gnn_mb1, L3_gnn_mW2, L3_gnn_mb2, L3_gnn_uW1, L3_gnn_ub1, L3_gnn_uW2, L3_gnn_ub2):
    import jax
    import jax.numpy as jnp

    def _L0_gnn_ref(feat, src, dst, ws0, wn0, b0, ws1, wn1, b1, ws2, wn2, b2):
        import jax, jax.numpy as jnp
        import numpy as np
        N_NODES = 100000
        N_EDGES = 25000

        def _mean_agg(h, src, dst, deg):
            summed = jax.ops.segment_sum(h[src], dst, num_segments=N_NODES)
            return summed / deg[:, None]

        def _sage_layer(h, src, dst, deg, w_self, w_neigh, b):
            h_neigh = _mean_agg(h, src, dst, deg)
            return jax.nn.relu(h @ w_self + h_neigh @ w_neigh + b)
        deg_i = jax.ops.segment_sum(jnp.ones_like(dst, dtype=jnp.float32), dst, num_segments=N_NODES)
        deg = jnp.maximum(deg_i, 1.0)
        h = _sage_layer(feat, src, dst, deg, ws0, wn0, b0)
        h = _sage_layer(h, src, dst, deg, ws1, wn1, b1)
        h = _sage_layer(h, src, dst, deg, ws2, wn2, b2)
        return h

    def _L1_gnn_ref(x, edge_index, W1, b1, W2, b2):
        import jax, jax.numpy as jnp
        import numpy as np
        N_NODES = 100000

        def gcn_conv(x, W, b, src, dst, num_nodes):
            xw = x @ W
            loop = jnp.arange(num_nodes, dtype=src.dtype)
            s = jnp.concatenate([src, loop])
            d = jnp.concatenate([dst, loop])
            deg = jax.ops.segment_sum(jnp.ones_like(d, dtype=xw.dtype), d, num_segments=num_nodes)
            dis = jnp.where(deg > 0, jax.lax.rsqrt(deg), 0.0)
            norm = dis[s] * dis[d]
            msg = norm[:, None] * xw[s]
            out = jax.ops.segment_sum(msg, d, num_segments=num_nodes)
            return out + b
        src, dst = (edge_index[0], edge_index[1])
        h = gcn_conv(x, W1, b1, src, dst, N_NODES)
        h = jax.nn.relu(h)
        out = gcn_conv(h, W2, b2, src, dst, N_NODES)
        return out

    def _L2_gnn_ref(x, edge_index, W1, b1, W2, b2):
        import jax, jax.numpy as jnp
        import numpy as np
        N_NODES = 100000
        N_EDGES = 25000
        DIM = 64
        src, dst = (edge_index[0], edge_index[1])
        agg = jax.ops.segment_sum(x[src], dst, num_segments=N_NODES)
        h = x + agg
        h = jax.nn.relu(h @ W1 + b1) @ W2 + b2
        return x + jax.nn.relu(h)

    def _L3_gnn_ref(nodes, row, col, edge_features, mW1, mb1, mW2, mb2, uW1, ub1, uW2, ub2):
        import jax, jax.numpy as jnp
        import numpy as np
        N_NODES = 50000
        N_EDGES = 12500
        D_NODE = 64
        D_EDGE = 32
        D_HID = 128

        def _mlp(x, W1, b1, W2, b2):
            return jax.nn.relu(x @ W1 + b1) @ W2 + b2
        msg_in = jnp.concatenate([nodes[row], nodes[col], edge_features], axis=-1)
        messages = _mlp(msg_in, mW1, mb1, mW2, mb2)
        aggregated = jax.ops.segment_sum(messages, col, num_segments=nodes.shape[0])
        upd_in = jnp.concatenate([nodes, aggregated], axis=-1)
        return _mlp(upd_in, uW1, ub1, uW2, ub2)
    edge_index = jnp.stack([src, dst])
    x = _layernorm(x + _L0_gnn_ref(x, src, dst, L0_gnn_ws0, L0_gnn_wn0, L0_gnn_b0, L0_gnn_ws1, L0_gnn_wn1, L0_gnn_b1, L0_gnn_ws2, L0_gnn_wn2, L0_gnn_b2), axis=-1)
    x = _layernorm(x + _L1_gnn_ref(x, edge_index, L1_gnn_W1, L1_gnn_b1, L1_gnn_W2, L1_gnn_b2), axis=-1)
    x = _layernorm(x + _L2_gnn_ref(x, edge_index, L2_gnn_W1, L2_gnn_b1, L2_gnn_W2, L2_gnn_b2), axis=-1)
    x = _layernorm(x + _L3_gnn_ref(x, src, dst, edge_attr_32, L3_gnn_mW1, L3_gnn_mb1, L3_gnn_mW2, L3_gnn_mb2, L3_gnn_uW1, L3_gnn_ub1, L3_gnn_uW2, L3_gnn_ub2), axis=-1)
    return x

_drawn_inputs = setup_inputs


def setup_inputs(seed=0):
    import zlib

    import numpy as np

    out = dict(_drawn_inputs(seed))
    spreads = {'L0_gnn_b0': (0.0, 0.1),
     'L0_gnn_b1': (0.0, 0.1),
     'L0_gnn_b2': (0.0, 0.1),
     'L1_gnn_b1': (0.0, 0.1),
     'L1_gnn_b2': (0.0, 0.1),
     'L2_gnn_b1': (0.0, 0.432),
     'L2_gnn_b2': (0.0, 0.306),
     'L3_gnn_mb1': (0.0, 0.386),
     'L3_gnn_mb2': (0.0, 0.273),
     'L3_gnn_ub1': (0.0, 0.1),
     'L3_gnn_ub2': (0.0, 0.1)}
    factors = {}
    for name, (base, spread) in spreads.items():
        noise = np.random.default_rng([zlib.crc32(name.encode()), seed]).standard_normal(out[name].shape)
        drawn = base * np.exp(spread * noise) if base else spread * noise
        out[name] = jnp.asarray(drawn.astype(out[name].dtype))
    for name, factor in factors.items():
        out[name] = (out[name] * factor).astype(out[name].dtype)
    return out
```

```python
import concourse.bass as bass
from concourse import mybir
from contextlib import ExitStack

F32, BF16, F16, I32 = mybir.dt.float32, mybir.dt.bfloat16, mybir.dt.float16, mybir.dt.int32
ALU = mybir.AluOpType
ACT = mybir.ActivationFunctionType
AX = mybir.AxisListType

P = 128
NT = 16
BN = P * NT
GT = 8
ET = 8
HT = 4
D = 64
H = 128
DE = 32
EPS = 1e-5
RB = 8
RING = RB * ET


class Sizes:

    def __init__(self, nodes, edges):
        self.nodes, self.edges = nodes, edges
        self.nb = -(-nodes // BN) + 1
        self.nb += self.nb % 2
        self.tiles = self.nb * NT
        self.etiles = self.nb * ET
        assert self.etiles * P >= edges
        self.rows = self.nb * BN
        assert nodes < self.rows - BN
        self.pad_node = (self.nb - 1) * BN
        self.wide = -(-(self.tiles + NT) // P) * P


def build(nc, z, a, out):
    ctx = ExitStack()
    NB = z.nb

    def sb(name, shape, dt=F32):
        return ctx.enter_context(nc.sbuf_tensor(name, shape, dt))

    def dram(name, shape, dt=F32):
        return nc.dram_tensor(name, shape, dt).ap()

    sets = [[ctx.enter_context(nc.semaphore(f"set{k}_{i}")) for i in range(68)] for k in range(2)]
    names, current = {}, [0]
    soft, base, first = {}, {}, [0]
    POOL_DMAS = ("wing0", "wing1", "rows0", "rows1", "pair0", "pair1", "g_rows", "g_old", "g_put")

    def kept(name):
        return f"{name}_{current[0]}" if name[0:2] == "g_" else name

    def S(name):
        if name in POOL_DMAS:
            key = kept(name)
            if key not in soft:
                soft[key] = ctx.enter_context(nc.semaphore(key))
            return soft[key]
        if name not in names:
            names[name] = sets[current[0]][len(names)]
        return names[name]

    def since(name):
        return base.get(kept(name), 0) if name in POOL_DMAS else first[0]

    def carry(name, count):
        base[kept(name)] = since(name) + count

    def next_pass(number):
        current[0], first[0] = number % 2, 1
        names.clear()
        return sets[1 - current[0]]

    def start_at_one(sp, semaphores):
        for s in semaphores:
            sp.sem_clear(s)
            sp.sem_inc(s, 1)

    def now(uses):
        return uses + (1 + first[0])

    def before(uses):
        return uses + first[0]

    def landed(name, uses, dmas=1):
        return uses * (16 * dmas) + (16 * dmas + since(name))

    s1_t, n1_t = dram("s1_t", [z.rows, H]), dram("n1_t", [z.rows, H])
    s2_t, n2_t = dram("s2_t", [z.rows, D]), dram("n2_t", [z.rows, D])
    x1_t, y1_t, y2_t = (dram(n, [z.rows, D]) for n in ("x1_t", "y1_t", "y2_t"))
    x2_t, x3_t = dram("x2_t", [z.rows, D]), dram("x3_t", [z.rows, D])
    msg_t = dram("msg_t", [z.etiles * P, D])
    sums_t, sums2_t = dram("sums_t", [z.rows, D]), dram("sums2_t", [z.rows, H])
    win_d = dram("win_d", [z.wide], I32)
    slot_d = dram("slot_d", [2, z.wide], I32)
    pref_d = dram("pref_d", [3, 32 * 32], I32)

    def block_of(table, m, width):
        return table[bass.ds(m * BN, BN), :].rearrange("(p j) f -> p (j f)", p=P)

    src_ix = sb("src_ix", [P, z.etiles], I32)
    dst_ix = sb("dst_ix", [P, z.etiles], I32)
    dst_f = sb("dst_f", [P, z.etiles])
    window = sb("window", [P, 2, z.wide])
    slots = sb("slots", [1, 2, z.tiles], I32)
    flag = sb("flag", [1, 4], I32)
    deg = sb("deg", [P, z.tiles])
    invdeg = sb("invdeg", [P, z.tiles])
    dis = sb("dis", [P, z.tiles])
    ident = sb("ident", [P, P])
    iota = sb("iota", [P, P], F16)
    ones_b = sb("ones_b", [P, 1], BF16)
    eps_c = sb("eps_c", [P, 1])
    one_c = sb("one_c", [P, 1])
    w0 = sb("w0", [P, H])
    w1 = sb("w1", [P, 2 * H])
    w2 = sb("w2", [P, H])
    wg1, wg2, wi1, wi2 = (sb(n, [P, P]) for n in ("wg1", "wg2", "wi1", "wi2"))
    wm1 = sb("wm1", [P, H])
    wm1e = sb("wm1e", [P, H])
    wm2 = sb("wm2", [P, P])
    wu1, wu2 = sb("wu1", [P, H]), sb("wu2", [P, P])
    b0c, bg1c, bi1c, bm1c, bu1c = (sb(n, [P, 1]) for n in ("b0c", "bg1c", "bi1c", "bm1c", "bu1c"))
    b1r, b2r, bg2r, bi2r, bm2r, bu2r = (
        sb(n, [P, w]) for n, w in (("b1r", H), ("b2r", D), ("bg2r", D), ("bi2r", D), ("bm2r", D), ("bu2r", D)))

    ps_all = ctx.enter_context(nc.psum_tensor("ps_all", [P, 8 * 512], F32))
    ps = [ps_all[:, 512 * i:512 * (i + 1)] for i in range(8)]

    def work(name, bytes_):
        return sb(name, [P, bytes_ // 4])

    gathered = [work(f"gathered{h}", HT * H * 4) for h in range(2)]
    rest = [work(f"rest{h}", HT * H * 4) for h in range(2)]
    ring = sb("ring", [P, RING * 3 * H], BF16)
    onehot = sb("onehot", [P, 2, GT, 2, P], BF16)
    load_a = [work(f"load_a{u}", NT * H * 4) for u in range(2)]
    load_b = [work(f"load_b{u}", NT * D * 4) for u in range(2)]
    store_a = [work(f"store_a{u}", NT * H * 4) for u in range(2)]
    store_b = [work(f"store_b{u}", NT * H * 4) for u in range(2)]
    tmp = [[work(f"tmp{k}{q}", 2048) for q in range(2)] for k in range(2)]
    tp = [work(f"tp{q}", 2048) for q in range(2)]
    tq = [work(f"tq{q}", 2048) for q in range(2)]
    stat = sb("stat", [P, 2, 4, GT])
    ix_now = sb("ix_now", [P, 4, HT], I32)
    ix_dst = sb("ix_dst", [P, 4, HT], I32)

    def setup():
        pro = ExitStack()

        def tb(name, shape, dt=F32):
            return pro.enter_context(nc.sbuf_tensor(name, shape, dt))

        E = z.etiles
        ring_i = ring[:, :].bitcast(I32)
        used = [0]

        def part(n, dt=I32):
            v = ring_i[:, used[0]:used[0] + n]
            used[0] += n
            assert used[0] <= RING * 3 * H // 2
            return v if dt == I32 else v.bitcast(dt)

        src_i, dst_i, nxt_i = part(E), part(E), part(E)
        t_i, u_i, v_i = part(E), part(E), part(E)
        hi_f, lo_f, gt_f = part(E, F32), part(E, F32), part(E, F32)
        i32_i = part(32)
        i32_f = part(32, F32)
        CH = 8
        oh = tb("oh", [P, 2, 2, CH, 32], BF16)
        tri = tb("tri", [32, 32])
        ones = tb("ones", [P, 32])
        sc = tb("sc", [32, 12, 32])
        sc_i = tb("sc_i", [32, 6, 32], I32)
        viol = tb("viol", [P, 4])
        kw = tb("kw", [P, z.wide // P], I32)
        kw2 = tb("kw2", [P, z.wide // P], I32)
        tid = tb("tid", [P, z.wide // P])
        win_g = tb("win_g", [P, 2, 2, P], I32)
        win_f = tb("win_f", [P, 2, 2, P])
        iota_i = tb("iota_i", [P, P], I32)
        tid_i = tb("tid_i", [P, z.wide // P], I32)
        zero_i = tb("zero_i", [1, 2 * NT], I32)
        steps = E // CH
        NW = z.wide // P

        with nc.Block() as block:
            n_loads = [0]

            @block.sync
            def _(sp):
                start_at_one(sp, sets[1])

                def load(dst, src):
                    sp.dma_start(dst, src).then_inc(S("weights"), 16)
                    n_loads[0] += 1

                for d, s in ((src_i, a["src_pt"]), (dst_i, a["dst_pt"]), (nxt_i, a["dstn_pt"])):
                    sp.dma_start(d, s).then_inc(S("edges"), 16)
                load(w0[0:D, :], a["L0_gnn_ws0"])
                load(w0[D:P, :], a["L0_gnn_wn0"])
                load(w1[:, 0:H], a["L0_gnn_wn1"])
                load(w1[:, H:2 * H], a["L0_gnn_ws1"])
                load(w2[:, 0:D], a["L0_gnn_ws2"])
                load(w2[:, D:H], a["L0_gnn_wn2"])
                load(wm1[:, :], a["L3_gnn_mW1"][0:P, :])
                load(wu1[:, :], a["L3_gnn_uW1"])
                sp.wait_ge(S("zeroed"), 1)
                for w, n in ((wg1, "L1_gnn_W1"), (wg2, "L1_gnn_W2"), (wi1, "L2_gnn_W1"), (wi2, "L2_gnn_W2")):
                    load(w[0:D, 0:D], a[n])
                    load(w[D:P, D:P], a[n])
                load(wm1e[0:DE, :], a["L3_gnn_mW1"][P:P + DE, :])
                load(wm2[:, 0:D], a["L3_gnn_mW2"])
                load(wu2[:, 0:D], a["L3_gnn_uW2"])
                col = lambda n: a[n].rearrange("(p o) -> p o", o=1)
                load(b0c[:, :], col("L0_gnn_b0"))
                load(bm1c[:, :], col("L3_gnn_mb1"))
                load(bu1c[:, :], col("L3_gnn_ub1"))
                for b, n in ((bg1c, "L1_gnn_b1"), (bi1c, "L2_gnn_b1")):
                    load(b[0:D, :], col(n))
                    load(b[D:P, :], col(n))
                for b, n in ((b1r, "L0_gnn_b1"), (b2r, "L0_gnn_b2"), (bg2r, "L1_gnn_b2"), (bi2r, "L2_gnn_b2"),
                             (bm2r, "L3_gnn_mb2"), (bu2r, "L3_gnn_ub2")):
                    load(b[:, :], a[n].partition_broadcast(P))
                sp.wait_ge(S("pref"), 1)
                for k in range(3):
                    sp.dma_start(pref_d[k, :].rearrange("(a b) -> a b", a=32), sc_i[:, 3 + k, :]).then_inc(S("tabs"), 16)
                sp.wait_ge(S("tabs"), 48)
                NR = z.tiles - NT
                sp.dma_start(win_d[NT:z.tiles], pref_d[0, 0:NR]).then_inc(S("tabs2"), 16)
                sp.dma_start(win_d[0:NT].rearrange("(o n) -> o n", o=1), zero_i[:, 0:NT]).then_inc(S("tabs2"), 16)
                for k in range(2):
                    sp.dma_start(slot_d[k, NT:z.tiles], pref_d[1 + k, 0:NR]).then_inc(S("tabs2"), 16)
                    sp.dma_start(slot_d[k:k + 1, 0:NT], zero_i[:, 0:NT]).then_inc(S("tabs2"), 16)
                left = z.wide - z.tiles
                for at in range(0, left, NT):
                    n = min(NT, left - at)
                    sp.dma_start(win_d[z.tiles + at:z.tiles + at + n].rearrange("(o n) -> o n", o=1), zero_i[:, 0:n]).then_inc(S("tabs2"), 16)
                sp.wait_ge(S("tabs2"), 16 * (6 + len(range(0, left, NT))))
                for k in range(2):
                    sp.dma_start(slots[:, k, :], slot_d[k:k + 1, 0:z.tiles]).then_inc(S("tabs3"), 16)
                with nc.allow_non_contiguous_dma(reason="a table of a few hundred numbers, once"):
                    sp.dma_start(kw[:, :], win_d.rearrange("(c p) -> p c", p=P)).then_inc(S("tabs4"), 16)
                sp.wait_ge(S("tabs3"), 32)
                sp.wait_ge(S("weights"), 16 * n_loads[0])

            @block.gpsimd
            def _(pool):
                pool.memset(tri[:, :], 1.0).then_inc(S("poolc"), 1)
                pool.wait_ge(S("poolc"), 1)
                pool.affine_select(out=tri[:, :], in_=tri[:, :], compare_op=ALU.is_gt, fill=0.0, base=0,
                                   pattern=[[1, 32]], channel_multiplier=-1).then_inc(S("poolc"), 1)
                pool.memset(ident[:, :], 0.0).then_inc(S("poolc"), 1)
                pool.wait_ge(S("poolc"), 3)
                pool.affine_select(out=ident[:, :], in_=ident[:, :], compare_op=ALU.not_equal, fill=1.0, base=0,
                                   pattern=[[-1, P]], channel_multiplier=1).then_inc(S("poolc"), 1)
                pool.iota(iota_i[:, :], pattern=[[1, P]], base=0, channel_multiplier=0).then_inc(S("iotas"), 1)
                pool.iota(i32_i, pattern=[[1, 32]], base=0, channel_multiplier=0).then_inc(S("iotas"), 1)
                pool.iota(sc_i[:, 0, :], pattern=[[1, 32]], base=0, channel_multiplier=32).then_inc(S("iotas"), 1)
                pool.iota(tid_i[:, :], pattern=[[P, NW]], base=0, channel_multiplier=1).then_inc(S("iotas"), 1)
                pool.wait_ge(S("tabs4"), 16)
                pool.wait_ge(S("kw2"), 1)
                for c in range(NW):
                    if c >= 2:
                        pool.wait_ge(S("winf"), c - 1)
                    for k, ix in enumerate((kw, kw2)):
                        pool.indirect_dma_start(
                            out=win_g[:, c % 2, k, :], out_offset=None, in_=a["dst_rows"],
                            in_offset=bass.IndirectOffsetOnAxis(ap=ix[:, c:c + 1], axis=0)).then_inc(S(f"wing{c % 2}"), 16)

            @block.vector
            def _(ve):
                k = [0]

                def step(ins):
                    k[0] += 1
                    ins.then_inc(S("chain"), 1)
                    ve.wait_ge(S("chain"), k[0])

                V = nc.vector
                for w in (wg1, wg2, wi1, wi2, wm1e, wm2, wu2):
                    last = V.memset(w[:, :], 0.0)
                last.then_inc(S("zeroed"), 1)
                step(V.memset(zero_i[:, :], 0))
                step(V.memset(ones[:, :], 1.0))
                step(V.memset(ones_b[:, :], 1.0))
                step(V.memset(eps_c[:, :], EPS))
                step(V.memset(one_c[:, :], 1.0))
                step(V.memset(viol[:, :], 0.0))
                step(V.memset(flag[:, :], 0))
                ve.wait_ge(S("iotas"), 4)
                step(V.tensor_copy(iota[:, :], iota_i[:, :]))
                step(V.tensor_copy(i32_f, i32_i))
                step(V.tensor_copy(tid[:, :], tid_i[:, :]))
                step(V.tensor_copy(sc[:, 11, :], sc_i[:, 0, :]))
                step(V.tensor_scalar(tid[:, :], tid[:, :], float(-P), float(P * NT), ALU.mult, ALU.add))
                ve.wait_ge(S("edges"), 48)
                step(V.tensor_copy(dst_f[:, :], dst_i))
                for d, s in ((src_ix, src_i), (dst_ix, dst_i)):
                    step(V.tensor_scalar(t_i, s, 11, 11, ALU.logical_shift_right, ALU.logical_shift_left))
                    step(V.tensor_scalar(u_i, s, 127, 4, ALU.bitwise_and, ALU.logical_shift_left))
                    step(V.tensor_scalar(v_i, s, 7, 15, ALU.logical_shift_right, ALU.bitwise_and))
                    step(V.tensor_tensor(u_i, u_i, v_i, ALU.add))
                    step(V.tensor_tensor(u_i, u_i, t_i, ALU.add))
                    step(V.tensor_scalar(d[:, :], u_i, float(BN), float(z.rows - 1), ALU.add, ALU.min))
                step(V.tensor_copy(hi_f, nxt_i))
                step(V.tensor_tensor(gt_f, dst_f[:, :], hi_f, ALU.is_gt))
                step(V.tensor_reduce(viol[:, 0:1], gt_f, AX.X, ALU.add))
                step(V.tensor_scalar(t_i, dst_i, 12, None, ALU.logical_shift_right))
                step(V.tensor_scalar(u_i, dst_i, 7, 31, ALU.logical_shift_right, ALU.bitwise_and))
                step(V.tensor_copy(hi_f, t_i))
                step(V.tensor_copy(lo_f, u_i))
                for s in range(steps):
                    if s >= 2:
                        ve.wait_ge(S("hist"), s - 1)
                    for d, v in enumerate((hi_f, lo_f)):
                        V.tensor_tensor(oh[:, s % 2, d, :, :],
                                        i32_f.unsqueeze(1).to_broadcast([P, CH, 32]),
                                        v[:, s * CH:(s + 1) * CH].unsqueeze(2).to_broadcast([P, CH, 32]),
                                        ALU.is_equal).then_inc(S("ohs"), 1)
                ve.wait_ge(S("hist"), steps)
                C, INC, EXC, ENDS, A, B, CC, DD = range(8)
                step(V.tensor_copy(sc[:, C, :], ps[0][0:32, 0:32]))
                step(V.tensor_tensor_scan(sc[:, INC, :], ones[0:32, :], sc[:, C, :], 0.0, ALU.mult, ALU.add))
                V.tensor_copy(sc[:, 10, 0:1], sc[:, INC, 31:32]).then_inc(S("tot"), 1)
                ve.wait_ge(S("rowp"), 1)
                step(V.tensor_copy(sc[:, 10, 1:2], ps[1][0:32, 0:1]))
                step(V.tensor_scalar(sc[:, ENDS, :], sc[:, INC, :], sc[:, 10, 1:2], None, ALU.add))
                step(V.tensor_tensor(sc[:, EXC, :], sc[:, ENDS, :], sc[:, C, :], ALU.subtract))
                step(V.tensor_copy(sc_i[:, 1, :], sc[:, EXC, :]))
                step(V.tensor_scalar(sc_i[:, 3, :], sc_i[:, 1, :], 7, None, ALU.logical_shift_right))
                step(V.tensor_copy(sc[:, A, :], sc_i[:, 3, :]))
                step(V.tensor_scalar(sc[:, B, :], sc[:, A, :], float(P), float(2 * P), ALU.mult, ALU.add))
                step(V.tensor_tensor(sc[:, B, :], sc[:, ENDS, :], sc[:, B, :], ALU.is_gt))
                step(V.tensor_scalar(sc_i[:, 1, :], sc_i[:, 0, :], 4, 3, ALU.logical_shift_right, ALU.logical_shift_left))
                step(V.tensor_copy(sc[:, CC, :], sc_i[:, 1, :]))
                step(V.tensor_tensor(sc[:, DD, :], sc[:, A, :], sc[:, CC, :], ALU.subtract))
                step(V.tensor_scalar(sc[:, CC, :], sc[:, DD, :], float(2 * ET - 2), None, ALU.is_gt))
                step(V.tensor_tensor(sc[:, B, :], sc[:, B, :], sc[:, CC, :], ALU.add))
                step(V.tensor_scalar(sc[:, CC, :], sc[:, DD, :], float(-ET), None, ALU.is_lt))
                step(V.tensor_tensor(sc[:, B, :], sc[:, B, :], sc[:, CC, :], ALU.add))
                step(V.tensor_scalar(sc[:, CC, :], sc[:, 11, :], float(z.tiles - NT), None, ALU.is_lt))
                step(V.tensor_tensor(sc[:, B, :], sc[:, B, :], sc[:, CC, :], ALU.mult))
                step(V.tensor_reduce(viol[0:32, 1:2], sc[:, B, :], AX.X, ALU.add))
                V.tensor_tensor(viol[:, 2:3], viol[:, 0:1], viol[:, 1:2], ALU.add).then_inc(S("viol"), 1)
                step(V.tensor_scalar(sc_i[:, 1, :], sc_i[:, 3, :], 1.0, None, ALU.add))
                step(V.tensor_scalar(sc_i[:, 4, :], sc_i[:, 3, :], RING - 1, None, ALU.bitwise_and))
                step(V.tensor_scalar(sc_i[:, 5, :], sc_i[:, 1, :], RING - 1, None, ALU.bitwise_and))
                step(V.tensor_scalar(sc[:, A, :], sc[:, A, :], float(z.etiles - 1), None, ALU.min))
                V.tensor_copy(sc_i[:, 3, :], sc[:, A, :]).then_inc(S("pref"), 1)
                ve.wait_ge(S("violp"), 1)
                step(V.tensor_scalar(sc[0:1, CC, 0:1], ps[2][0:1, 0:1], 1.0, None, ALU.min))
                step(V.tensor_copy(flag[0:1, 0:1], sc[0:1, CC, 0:1]))
                ve.wait_ge(S("tabs4"), 16)
                V.tensor_scalar(kw2[:, :], kw[:, :], 1.0, None, ALU.add).then_inc(S("kw2"), 1)
                for c in range(NW):
                    ve.wait_ge(S(f"wing{c % 2}"), 32 * (c // 2 + 1))
                    if c >= 2:
                        ve.wait_ge(S("wint"), c - 1)
                    V.tensor_scalar(win_f[:, c % 2, :, :], win_g[:, c % 2, :, :], tid[:, c:c + 1], None,
                                    ALU.add).then_inc(S("winf"), 1)
                    ve.wait_ge(S("wint"), c + 1)
                    V.tensor_copy(window[:, :, c * P:(c + 1) * P],
                                  ps[4 + c % 2][:, 0:2 * P].rearrange("p (k t) -> p k t", k=2)).then_inc(S("wins"), 1)
                ve.wait_ge(S("wins"), NW)

            @block.tensor
            def _(pe):
                for s in range(steps):
                    pe.wait_ge(S("ohs"), 2 * s + 2)
                    for k in range(CH):
                        last = pe.matmul(ps[0][0:32, 0:32], oh[:, s % 2, 0, k, :], oh[:, s % 2, 1, k, :],
                                         start=(s + k == 0), stop=(s == steps - 1 and k == CH - 1))
                    last.then_inc(S("hist"), 1)
                pe.wait_ge(S("tot"), 1)
                pe.wait_ge(S("poolc"), 4)
                pe.matmul(ps[1][0:32, 0:1], tri[:, :], sc[:, 10, 0:1], start=True, stop=True).then_inc(S("rowp"), 1)
                pe.wait_ge(S("viol"), 1)
                pe.matmul(ps[2][0:1, 0:1], viol[:, 2:3], ones[:, 0:1], start=True, stop=True).then_inc(S("violp"), 1)
                for c in range(NW):
                    pe.wait_ge(S("winf"), c + 1)
                    if c >= 2:
                        pe.wait_ge(S("wins"), c - 1)
                    for k in range(2):
                        last = pe.transpose(ps[4 + c % 2][:, k * P:(k + 1) * P], win_f[:, c % 2, k, :], ident[:, :])
                    last.then_inc(S("wint"), 1)

        pro.close()

    g_rows, g_old = work("g_rows", H * 4), work("g_old", H * 4)
    g_new, g_same, g_low = work("g_new", H * 4), work("g_same", P * 4), work("g_low", P * 4)
    g_mask = sb("g_mask", [P, P])
    g_dst = sb("g_dst", [P, P], I32)
    g_small = sb("g_small", [P, 4])
    g_ix = sb("g_ix", [P, 3], I32)
    BIG = 1 << 22

    class General:

        def __init__(self, sums, width, table=None, direct=None):
            self.sums, self.width, self.table, self.direct = sums, width, table, direct

        def sync(self, sp):
            W = self.width
            sp.wait_ge(S("g_zero"), now(0))
            with sp.Fori(0, z.nb) as m:
                sp.dma_start(block_of(self.sums, m, W), store_a[0][:, 0:NT * W]).then_inc(S("g_cleared"), 16)

            def tile(m, t):
                k = m * ET + t
                sp.wait_ge(S("g_same"), before(k))
                sp.dma_start(g_dst[:, :], a["dst_rows"][bass.ds(k, 1), :].rearrange("o e -> (o e)").partition_broadcast(P)).then_inc(S("g_dst"), 16)
                if self.direct is not None:
                    sp.wait_ge(S("g_sum"), before(k))
                    block = self.direct[bass.ds(m * ET * P, ET * P), :].rearrange("(p t) f -> p t f", t=ET)
                    sp.dma_start(g_rows[:, 0:W], block[:, t, :]).then_inc(S("g_direct"), 16)

            with sp.Fori(0, NB) as m:
                for t in range(ET):
                    tile(m, t)

        def gpsimd(self, pool):
            W = self.width
            pool.memset(g_mask[:, :], 1.0).then_inc(S("g_mask"), 1)
            pool.wait_ge(S("g_mask"), before(1))
            pool.affine_select(out=g_mask[:, :], in_=g_mask[:, :], compare_op=ALU.is_gt, fill=0.0, base=0,
                               pattern=[[-1, P]], channel_multiplier=1).then_inc(S("g_mask"), 1)
            pool.wait_ge(S("g_cleared"), before(16 * z.nb))
            with pool.Fori(0, z.etiles) as k:
                pool.wait_ge(S("g_ix"), now(k))
                gate(pool)
                if self.table is not None:
                    pool.wait_ge(S("g_sum"), before(k))
                    gate(pool)
                    pool.indirect_dma_start(out=g_rows[:, 0:W], out_offset=None, in_=self.table,
                                            in_offset=bass.IndirectOffsetOnAxis(ap=g_ix[:, 0:1], axis=0)).then_inc(S("g_rows"), 16)
                pool.indirect_dma_start(out=g_old[:, 0:W], out_offset=None, in_=self.sums,
                                        in_offset=bass.IndirectOffsetOnAxis(ap=g_ix[:, 1:2], axis=0)).then_inc(S("g_old"), 16)
                pool.wait_ge(S("g_new"), now(k))
                gate(pool)
                pool.indirect_dma_start(out=self.sums, out_offset=bass.IndirectOffsetOnAxis(ap=g_ix[:, 2:3], axis=0),
                                        in_=g_new[:, 0:W], in_offset=None, bounds_check=z.rows - 1,
                                        oob_is_err=False).then_inc(S("g_put"), 16)
                pool.wait_ge(S("g_put"), landed("g_put", k))
                pool.sem_inc(S("g_stored"), 1)
            pool.sem_inc(S("g_all"), 1)

        def vector(self, ve):
            W = self.width
            V = nc.vector
            V.memset(store_a[0][:, 0:NT * W], 0.0).then_inc(S("g_zero"), 1)
            if self.table is None and self.direct is None:
                V.memset(g_rows[:, 0:W], 1.0).then_inc(S("g_zero"), 1)
            ve.wait_ge(S("g_mask"), before(2))
            with ve.Fori(0, z.etiles) as k:
                c = [0]

                def step(ins):
                    c[0] += 1
                    ins.then_inc(S("g_chain"), 1)
                    ve.wait_ge(S("g_chain"), before(k * 6 + c[0]))

                ve.wait_ge(S("g_stored"), before(k))
                ve.wait_ge(S("g_dst"), before(k * 16 + 16))
                ve.wait_ge(S("g_sum"), before(k))
                V.tensor_scalar(g_same[:, :], g_dst[:, :], dst_f[:, bass.ds(k, 1)], None, ALU.is_equal).then_inc(S("g_same"), 1)
                ve.wait_ge(S("g_same"), now(k))
                step(V.tensor_tensor(g_low[:, :], g_same[:, :], g_mask[:, :], ALU.mult))
                step(V.tensor_reduce(g_small[:, 0:1], g_low[:, :], AX.X, ALU.max))
                step(V.tensor_scalar(g_small[:, 1:2], dst_ix[:, bass.ds(k, 1)], 0.0, None, ALU.add))
                step(V.scalar_tensor_tensor(g_small[:, 2:3], g_small[:, 0:1], float(BIG), g_small[:, 1:2], ALU.mult, ALU.add))
                step(V.tensor_scalar(g_ix[:, 0:1], src_ix[:, bass.ds(k, 1)], 0.0, None, ALU.add))
                step(V.tensor_scalar(g_ix[:, 1:2], dst_ix[:, bass.ds(k, 1)], 0.0, None, ALU.add))
                V.tensor_copy(g_ix[:, 2:3], g_small[:, 2:3]).then_inc(S("g_ix"), 1)
                ve.wait_ge(S("g_sum"), now(k))
                ve.wait_ge(S("g_old"), landed("g_old", k))
                V.tensor_tensor(g_new[:, 0:W], ps[0][:, 0:W], g_old[:, 0:W], ALU.add).then_inc(S("g_new"), 1)

        def tensor(self, pe):
            W = self.width
            if self.table is None and self.direct is None:
                pe.wait_ge(S("g_zero"), before(2))
            with pe.Fori(0, z.etiles) as k:
                pe.wait_ge(S("g_same"), now(k))
                pe.wait_ge(S("g_new"), before(k))
                if self.table is not None or self.direct is not None:
                    pe.wait_ge(S("g_rows" if self.direct is None else "g_direct"), landed("g_rows" if self.direct is None else "g_direct", k))
                pe.matmul(ps[0][:, 0:W], g_same[:, :], g_rows[:, 0:W], start=True, stop=True).then_inc(S("g_sum"), 1)

    def pass_over(p):
        if p.table is not None:
            for h in range(2):
                carry(f"rows{h}", 16 * HT * (NB + 1))
            carry("g_rows", 16 * z.etiles)
        for name in ("g_old", "g_put"):
            carry(name, 16 * z.etiles)

    def both_ways(eng, general, windows):
        way = eng.value_load(flag[0:1, 0:1], min_val=0, max_val=1)
        with eng.If(way > 0):
            general()
        with eng.Else():
            windows()

    def bodies(eng, body):
        with eng.Fori(0, NB // 2) as i:
            for u in range(2):
                body(i * 2 + u, u)

    def gate(pool):
        pool.sem_inc(S("passed"), 1)

    def gather_pool(pool, table, W, ghost=True):
        def half(m, slot, h):
            pool.wait_ge(S(f"ix{slot}"), landed(f"ix{slot}", m[1]))
            pool.wait_ge(S(f"rest{h}"), before(m[0]))
            gate(pool)
            for t in range(HT):
                pool.indirect_dma_start(
                    out=gathered[h][:, t * W:(t + 1) * W], out_offset=None, in_=table,
                    in_offset=bass.IndirectOffsetOnAxis(ap=ix_now[:, slot, t:t + 1], axis=0)).then_inc(S(f"rows{h}"), 16)

        with pool.Fori(0, NB // 2) as i:
            for u in range(2):
                for h in range(2):
                    half((i * 2 + u, i), 2 * u + h, h)
        for h in range(2):
            half((NB, NB // 2), h, h)

    class Split:

        def __init__(self, W, rows=None, name="rows"):
            self.W, self.name = W, name
            self.rows = rows or (lambda h: gathered[h][:, 0:HT * W])

        def place(self, base, h, part):
            W = self.W
            return ring[:, 0:RING * 3 * W].rearrange("p (s w) -> p s w", w=3 * W)[
                :, bass.ds(base + HT * h, HT), part * W:(part + 1) * W]

        def view(self, ap):
            return ap.rearrange("p (t w) -> p t w", t=HT)

        def hi(self, act, n, base, h, dmas=HT):
            act.wait_ge(S(f"{self.name}{h}"), landed(f"{self.name}{h}", n, dmas))
            nc.scalar.activation(self.place(base, h, 0), self.view(self.rows(h)), ACT.Copy).then_inc(S(f"hi{h}"), 1)

        def rest(self, ve, n, base, h):
            ve.wait_ge(S(f"hi{h}"), now(n))
            ve.wait_ge(S(f"mid{h}"), before(n))
            ve.wait_ge(S(f"lo{h}"), before(n))
            nc.vector.tensor_tensor(self.view(rest[h][:, 0:HT * self.W]), self.view(self.rows(h)),
                                         self.place(base, h, 0), ALU.subtract).then_inc(S(f"rest{h}"), 1)

        def mid(self, act, n, base, h):
            act.wait_ge(S(f"rest{h}"), now(n))
            nc.scalar.activation(self.place(base, h, 1), self.view(rest[h][:, 0:HT * self.W]), ACT.Copy).then_inc(S(f"mid{h}"), 1)

        def lo(self, ve, n, base, h):
            ve.wait_ge(S(f"mid{h}"), now(n))
            nc.vector.tensor_tensor(self.place(base, h, 2), self.view(rest[h][:, 0:HT * self.W]),
                                         self.place(base, h, 1), ALU.subtract).then_inc(S(f"lo{h}"), 1)

    def ring_base(m):
        return (m % RB) * ET

    def one_hots(ve, m, q, used=None):
        (used or (lambda: ve.wait_ge(S(f"agg{q}"), before(m))))()
        for j in range(GT):
            for k in range(2):
                last = nc.vector.tensor_scalar(onehot[:, q, j, k, :], iota[:, :],
                                               window[:, k, bass.ds(m * NT + q * GT + j, 1)], None, ALU.is_equal)
        last.then_inc(S(f"hot{q}"), 1)

    def sums(pe, m, tiles, out, W, degrees=None):
        first, n = tiles[0], len(tiles)
        places = [nc.values_load_multi_w_load_instructions(
            slots[0:1, k, bass.ds(m * NT + first, n)], engines=(mybir.EngineType.PE,), min_val=0, max_val=RING - 1,
            skip_runtime_bounds_check_because="the table holds remainders by RING")[1] for k in range(2)]
        for j in tiles:
            for k in range(2):
                at = places[k][j - first] * (3 * W)
                if degrees is not None:
                    pe.matmul(degrees(j), onehot[:, j // GT, j % GT, k, :], ones_b[:, :],
                              start=(k == 0), stop=(k == 1))
                for part in range(3):
                    last = pe.matmul(out(j), onehot[:, j // GT, j % GT, k, :], ring[:, bass.ds(at + part * W, W)],
                                     start=(k == 0 and part == 0), stop=(k == 1 and part == 2))
        return last

    def group(ap, q, W=D):
        return ap[:, q * GT * W:(q + 1) * GT * W]

    def tiles3(ap, W=D):
        return ap.rearrange("p (j w) -> p j w", w=W)

    def per_node(table, m, q):
        return table[:, bass.ds(m * NT + q * GT, GT)].unsqueeze(2).to_broadcast([P, GT, D])

    def row(b, W=D, n=GT):
        return b[:, :].unsqueeze(1).to_broadcast([P, n, W])

    def general_sums(u, W):
        return ring[:, :].bitcast(F32)[:, u * NT * H:u * NT * H + NT * W]

    def norm_center(ve, q, m):
        V = nc.vector
        V.tensor_reduce(stat[:, q, 0, :], tiles3(tmp[1][q][:, :]), AX.X, ALU.add).then_inc(S(f"rs{q}"), 1)
        ve.wait_ge(S(f"rs{q}"), now(m))
        V.tensor_scalar(stat[:, q, 1, :], stat[:, q, 0, :], -1.0 / D, None, ALU.mult).then_inc(S(f"nm{q}"), 1)
        ve.wait_ge(S(f"nm{q}"), now(m))
        V.tensor_tensor(tiles3(tmp[0][q][:, :]), tiles3(tmp[1][q][:, :]),
                             stat[:, q, 1, :].unsqueeze(2).to_broadcast([P, GT, D]), ALU.add).then_inc(S(f"xc{q}"), 1)

    def norm_square(act, q, m):
        act.wait_ge(S(f"xc{q}"), now(m))
        nc.scalar.activation(tq[q][:, :], tmp[0][q][:, :], ACT.Square).then_inc(S(f"sq{q}"), 1)

    def norm_var(ve, q, m):
        ve.wait_ge(S(f"sq{q}"), now(m))
        nc.vector.tensor_reduce(stat[:, q, 2, :], tiles3(tq[q][:, :]), AX.X, ALU.add).then_inc(S(f"vs{q}"), 1)

    def norm_root(act, q, m):
        act.wait_ge(S(f"vs{q}"), now(m))
        nc.scalar.activation(stat[:, q, 3, :], stat[:, q, 2, :], ACT.Sqrt, bias=eps_c[:, :], scale=1.0 / D).then_inc(S(f"sd{q}"), 1)

    def norm_out(ve, q, m, to):
        ve.wait_ge(S(f"sd{q}"), now(m))
        nc.vector.reciprocal(stat[:, q, 2, :], stat[:, q, 3, :]).then_inc(S(f"rstd{q}"), 1)
        ve.wait_ge(S(f"rstd{q}"), now(m))
        nc.vector.tensor_tensor(tiles3(to), tiles3(tmp[0][q][:, :]),
                                     stat[:, q, 2, :].unsqueeze(2).to_broadcast([P, GT, D]), ALU.mult).then_inc(S(f"out{q}"), 1)

    class Pass:
        W = D
        rows = "rows"
        dmas = HT
        loads, stores, consumed = (), (), ()
        per_body = 1

        def __init__(self, number, table, general):
            self.number, self.table, self.gen = number, table, general
            self.split = Split(self.W, name=self.rows)

        def load_block(self, sp, m, u):
            for table, buf, W in self.loads:
                sp.dma_start(buf[u][:, 0:NT * W], block_of(table, m, W)).then_inc(S(f"in{u}"), 16)

        def load_sums(self, sp, m, u):
            sp.dma_start(general_sums(u, self.W), block_of(self.gen.sums, m, self.W)).then_inc(S(f"sums{u}"), 16)

        def load_index(self, sp, m, u):
            for h in range(2):
                sp.dma_start(ix_now[:, 2 * u + h, :], src_ix[:, bass.ds(m * ET + h * HT, HT)]).then_inc(S(f"ix{2 * u + h}"), 16)

        def sync_rows_first(self, sp):
            for u in range(2):
                self.load_index(sp, u, u)

        def sync_rows(self, sp, m, u):
            for h in range(2):
                sp.wait_ge(S(f"rows{h}"), landed(f"rows{h}", m, HT))
            self.load_index(sp, (m + 2) % NB, u)

        def sync_rows_last(self, sp):
            for s in range(4):
                sp.wait_ge(S(f"ix{s}"), before(16 * (NB // 2 + 1)))

        def sync_loop(self, sp, windows):
            if windows:
                self.sync_rows_first(sp)
            for u in range(2):
                self.load_block(sp, u, u)
                if not windows:
                    self.load_sums(sp, u, u)

            def body(m, u):
                if windows:
                    self.sync_rows(sp, m, u)
                for table, buf, W, names, per in self.stores:
                    for name in names:
                        sp.wait_ge(S(name), before(m * per + per))
                    sp.dma_start(block_of(table, m, W), buf[u][:, 0:NT * W]).then_inc(S(f"put{u}"), 16)
                for name, per in self.consumed:
                    sp.wait_ge(S(name), before(m * per + per))
                self.load_block(sp, (m + 2) % NB, u)
                if not windows:
                    self.load_sums(sp, (m + 2) % NB, u)

            bodies(sp, body)
            for u in range(2):
                sp.wait_ge(S(f"in{u}"), before(16 * len(self.loads) * (NB // 2 + 1)))
                if self.stores:
                    sp.wait_ge(S(f"put{u}"), before(16 * len(self.stores) * (NB // 2)))
                if not windows:
                    sp.wait_ge(S(f"sums{u}"), before(16 * (NB // 2 + 1)))
            if windows:
                self.sync_rows_last(sp)

        def inputs_in(self, eng, i, u):
            eng.wait_ge(S(f"in{u}"), landed(f"in{u}", i, len(self.loads)))

        def stored(self, eng, i, u):
            eng.wait_ge(S(f"put{u}"), before(i * 16 * len(self.stores)))

        def sums_here(self, ve, m, i, u, q, windows):
            if windows:
                ve.wait_ge(S(f"agg{q}"), now(m))
                return ps[q][:, 0:GT * D]
            ve.wait_ge(S(f"sums{u}"), landed(f"sums{u}", i))
            return group(general_sums(u, D), q)

        def tensor_sums(self, pe, m, windows):
            if not windows:
                return
            for h in range(2):
                pe.wait_ge(S(f"lo{h}"), now(m))
            for q in range(2):
                pe.wait_ge(S(f"hot{q}"), now(m))
                pe.wait_ge(S(f"mean{q}"), before(m))
                out = lambda j, q=q: ps[q][:, (j % GT) * D:(j % GT + 1) * D]
                sums(pe, m, range(q * GT, q * GT + GT), out, D).then_inc(S(f"agg{q}"), 1)

        def split_hi(self, act, n):
            for h in range(2):
                self.split.hi(act, n, ring_base(n), h, self.dmas)

        def split_mid(self, act, n):
            for h in range(2):
                self.split.mid(act, n, ring_base(n), h)

        def split_rest(self, ve, n):
            for h in range(2):
                self.split.rest(ve, n, ring_base(n), h)

        def split_lo(self, ve, n):
            for h in range(2):
                self.split.lo(ve, n, ring_base(n), h)

        def used(self, ve, m, q):
            ve.wait_ge(S(f"agg{q}"), before(m))

        def hots(self, ve, m):
            for q in range(2):
                one_hots(ve, m, q, lambda: self.used(ve, m, q))

        def vector_loop(self, ve, windows):
            if windows:
                self.hots(ve, 0)
                self.split_rest(ve, 0)
                self.split_lo(ve, 0)
            with ve.Fori(0, NB // 2) as i:
                for u in range(2):
                    self.vector(ve, i * 2 + u, i, u, windows)

        def scalar_loop(self, act, windows):
            if windows:
                self.split_hi(act, 0)
                self.split_mid(act, 0)
            with act.Fori(0, NB // 2) as i:
                for u in range(2):
                    self.scalar(act, i * 2 + u, i, u, windows)

        def tensor_loop(self, pe, windows):
            with pe.Fori(0, NB // 2) as i:
                for u in range(2):
                    self.tensor(pe, i * 2 + u, i, u, windows)

        def gpsimd_windows(self, pool):
            gather_pool(pool, self.table, self.W)

        def prepare(self, sp):
            pass

        def emit(self):
            other = next_pass(self.number)
            with nc.Block() as block:

                @block.sync
                def _(sp):
                    start_at_one(sp, other)

                    def general():
                        self.gen.sync(sp)
                        sp.wait_ge(S("g_all"), now(0))
                        self.sync_loop(sp, False)

                    both_ways(sp, general, lambda: self.sync_loop(sp, True))

                @block.gpsimd
                def _(pool):
                    both_ways(pool, lambda: self.gen.gpsimd(pool), lambda: self.gpsimd_windows(pool))

                @block.vector
                def _(ve):
                    def general():
                        self.gen.vector(ve)
                        self.vector_loop(ve, False)

                    both_ways(ve, general, lambda: self.vector_loop(ve, True))

                @block.scalar
                def _(act):
                    both_ways(act, lambda: self.scalar_loop(act, False), lambda: self.scalar_loop(act, True))

                @block.tensor
                def _(pe):
                    def general():
                        self.gen.tensor(pe)
                        self.tensor_loop(pe, False)

                    both_ways(pe, general, lambda: self.tensor_loop(pe, True))

            pass_over(self)

    def pair_transposes(pe, src, bank):
        for r in range(GT // 2):
            last = pe.transpose(bank[:, r * P:(r + 1) * P], src[:, r * P:(r + 1) * P], ident[:, :])
        return last

    def pair_products(pe, lhs, w, bank):
        for r in range(GT // 2):
            last = pe.matmul(bank[:, r * P:(r + 1) * P], lhs[:, r * P:(r + 1) * P], w[:, :], start=True, stop=True)
        return last

    class Sage2(Pass):
        loads = ((s2_t, load_a, D), (a["x_rows"], load_b, D))
        stores = ((x1_t, store_a, D, ("out0", "out1"), 1), (y1_t, store_b, D, ("y0", "y1"), 1))
        consumed = (("pre0", 1), ("pre1", 1))

        def vector(self, ve, m, i, u, windows):
            V = nc.vector
            if windows:
                self.split_rest(ve, m + 1)
            for q in range(2):
                agg = self.sums_here(ve, m, i, u, q, windows)
                V.tensor_tensor(tiles3(tmp[0][q][:, :]), tiles3(agg), per_node(invdeg, m, q), ALU.mult).then_inc(S(f"mean{q}"), 1)
            self.inputs_in(ve, i, u)
            for q in range(2):
                ve.wait_ge(S(f"mean{q}"), now(m))
                V.tensor_tensor(tmp[0][q][:, :], tmp[0][q][:, :], group(load_a[u], q), ALU.add).then_inc(S(f"sum{q}"), 1)
            for q in range(2):
                ve.wait_ge(S(f"sum{q}"), now(m))
                V.scalar_tensor_tensor(tmp[1][q][:, :], tmp[0][q][:, :], 0.0, group(load_b[u], q), ALU.max, ALU.add).then_inc(S(f"pre{q}"), 1)
            for q in range(2):
                ve.wait_ge(S(f"pre{q}"), now(m))
                norm_center(ve, q, m)
            if windows:
                self.split_lo(ve, m + 1)
            for q in range(2):
                norm_var(ve, q, m)
            self.stored(ve, i, u)
            for q in range(2):
                norm_out(ve, q, m, group(store_a[u], q))
            if windows:
                self.hots(ve, m + 1)
            for q in range(2):
                ve.wait_ge(S(f"mm{q}"), now(m))
                V.tensor_tensor(tiles3(group(store_b[u], q)), tiles3(ps[4 + q]), per_node(dis, m, q), ALU.mult).then_inc(S(f"y{q}"), 1)

        def scalar(self, act, m, i, u, windows):
            if windows:
                self.split_hi(act, m + 1)
                self.split_mid(act, m + 1)
            for q in range(2):
                norm_square(act, q, m)
            for q in range(2):
                norm_root(act, q, m)
            for q in range(2):
                act.wait_ge(S(f"tr{q}"), now(m))
                nc.scalar.activation(tp[q][:, :], ps[2 + q], ACT.Copy).then_inc(S(f"ev{q}"), 1)

        def tensor(self, pe, m, i, u, windows):
            self.tensor_sums(pe, m, windows)
            for q in range(2):
                pe.wait_ge(S(f"out{q}"), now(m))
                pe.wait_ge(S(f"ev{q}"), before(m))
                pair_transposes(pe, group(store_a[u], q), ps[2 + q]).then_inc(S(f"tr{q}"), 1)
            for q in range(2):
                pe.wait_ge(S(f"ev{q}"), now(m))
                pe.wait_ge(S(f"y{q}"), before(m))
                pair_products(pe, tp[q], wg1, ps[4 + q]).then_inc(S(f"mm{q}"), 1)

    class Gcn1(Pass):
        loads = ((y1_t, load_b, D),)
        stores = ((y2_t, store_b, D, ("y0", "y1"), 1),)
        consumed = (("mean0", 1), ("mean1", 1))

        def vector(self, ve, m, i, u, windows):
            V = nc.vector
            if windows:
                self.split_rest(ve, m + 1)
            self.inputs_in(ve, i, u)
            for q in range(2):
                agg = self.sums_here(ve, m, i, u, q, windows)
                V.tensor_tensor(tmp[0][q][:, :], agg, group(load_b[u], q), ALU.add).then_inc(S(f"mean{q}"), 1)
            for q in range(2):
                ve.wait_ge(S(f"mean{q}"), now(m))
                ve.wait_ge(S(f"tr{q}"), before(m))
                V.tensor_tensor(tiles3(tmp[1][q][:, :]), tiles3(tmp[0][q][:, :]), per_node(dis, m, q), ALU.mult).then_inc(S(f"pre{q}"), 1)
            if windows:
                self.split_lo(ve, m + 1)
                self.hots(ve, m + 1)
            self.stored(ve, i, u)
            for q in range(2):
                ve.wait_ge(S(f"mm{q}"), now(m))
                V.tensor_tensor(tiles3(group(store_b[u], q)), tiles3(ps[4 + q]), per_node(dis, m, q), ALU.mult).then_inc(S(f"y{q}"), 1)

        def scalar(self, act, m, i, u, windows):
            if windows:
                self.split_hi(act, m + 1)
                self.split_mid(act, m + 1)
            for q in range(2):
                act.wait_ge(S(f"tr{q}"), now(m))
                nc.scalar.activation(tp[q][:, :], ps[2 + q], ACT.Relu, bias=bg1c[:, :]).then_inc(S(f"ev{q}"), 1)

        def tensor(self, pe, m, i, u, windows):
            self.tensor_sums(pe, m, windows)
            for q in range(2):
                pe.wait_ge(S(f"pre{q}"), now(m))
                pe.wait_ge(S(f"ev{q}"), before(m))
                pair_transposes(pe, tmp[1][q], ps[2 + q]).then_inc(S(f"tr{q}"), 1)
            for q in range(2):
                pe.wait_ge(S(f"ev{q}"), now(m))
                pe.wait_ge(S(f"y{q}"), before(m))
                pair_products(pe, tp[q], wg2, ps[4 + q]).then_inc(S(f"mm{q}"), 1)

    class Gcn2(Pass):
        loads = ((y2_t, load_a, D), (x1_t, load_b, D))
        stores = ((x2_t, store_a, D, ("out0", "out1"), 1),)
        consumed = (("mean0", 1), ("mean1", 1), ("sum0", 1), ("sum1", 1))

        def vector(self, ve, m, i, u, windows):
            V = nc.vector
            if windows:
                self.split_rest(ve, m + 1)
            self.inputs_in(ve, i, u)
            for q in range(2):
                agg = self.sums_here(ve, m, i, u, q, windows)
                ve.wait_ge(S(f"out{q}"), before(m))
                V.tensor_tensor(tmp[0][q][:, :], agg, group(load_a[u], q), ALU.add).then_inc(S(f"mean{q}"), 1)
            for q in range(2):
                ve.wait_ge(S(f"mean{q}"), now(m))
                V.tensor_tensor(tiles3(tmp[1][q][:, :]), tiles3(tmp[0][q][:, :]), per_node(dis, m, q), ALU.mult).then_inc(S(f"scaled{q}"), 1)
            for q in range(2):
                ve.wait_ge(S(f"scaled{q}"), now(m))
                V.tensor_tensor(tmp[0][q][:, :], tmp[1][q][:, :], group(load_b[u], q), ALU.add).then_inc(S(f"sum{q}"), 1)
            for q in range(2):
                ve.wait_ge(S(f"sum{q}"), now(m))
                V.tensor_tensor(tiles3(tmp[1][q][:, :]), tiles3(tmp[0][q][:, :]), row(bg2r), ALU.add).then_inc(S(f"pre{q}"), 1)
            for q in range(2):
                ve.wait_ge(S(f"pre{q}"), now(m))
                norm_center(ve, q, m)
            if windows:
                self.split_lo(ve, m + 1)
                self.hots(ve, m + 1)
            for q in range(2):
                norm_var(ve, q, m)
            self.stored(ve, i, u)
            for q in range(2):
                norm_out(ve, q, m, group(store_a[u], q))

        def scalar(self, act, m, i, u, windows):
            if windows:
                self.split_hi(act, m + 1)
                self.split_mid(act, m + 1)
            for q in range(2):
                norm_square(act, q, m)
            for q in range(2):
                norm_root(act, q, m)

        def tensor(self, pe, m, i, u, windows):
            self.tensor_sums(pe, m, windows)

    class Gin(Pass):
        loads = ((x2_t, load_b, D),)
        stores = ((x3_t, store_a, D, ("out0", "out1"), 1),)
        consumed = (("pre0", 1), ("pre1", 1))

        def vector(self, ve, m, i, u, windows):
            V = nc.vector
            if windows:
                self.split_rest(ve, m + 1)
            self.inputs_in(ve, i, u)
            for q in range(2):
                agg = self.sums_here(ve, m, i, u, q, windows)
                ve.wait_ge(S(f"out{q}"), before(m))
                V.tensor_tensor(tmp[0][q][:, :], agg, group(load_b[u], q), ALU.add).then_inc(S(f"mean{q}"), 1)
            if windows:
                self.split_lo(ve, m + 1)
                self.hots(ve, m + 1)
            for q in range(2):
                ve.wait_ge(S(f"mm{q}"), now(m))
                V.tensor_tensor(tiles3(tmp[0][q][:, :]), tiles3(ps[6 + q]), row(bi2r), ALU.add).then_inc(S(f"sum{q}"), 1)
            for q in range(2):
                ve.wait_ge(S(f"last{q}"), now(m))
                V.scalar_tensor_tensor(tmp[1][q][:, :], group(load_b[u], q), 2.0, tmp[1][q][:, :], ALU.mult, ALU.add).then_inc(S(f"pre{q}"), 1)
            for q in range(2):
                ve.wait_ge(S(f"pre{q}"), now(m))
                norm_center(ve, q, m)
            for q in range(2):
                norm_var(ve, q, m)
            self.stored(ve, i, u)
            for q in range(2):
                norm_out(ve, q, m, group(store_a[u], q))

        def scalar(self, act, m, i, u, windows):
            if windows:
                self.split_hi(act, m + 1)
                self.split_mid(act, m + 1)
            for q in range(2):
                act.wait_ge(S(f"tr{q}"), now(m))
                nc.scalar.activation(tp[q][:, :], ps[2 + q], ACT.Copy).then_inc(S(f"ev{q}"), 1)
            for q in range(2):
                act.wait_ge(S(f"hid{q}"), now(m))
                nc.scalar.activation(tq[q][:, :], ps[4 + q], ACT.Relu, bias=bi1c[:, :]).then_inc(S(f"relu{q}"), 1)
            for q in range(2):
                act.wait_ge(S(f"sum{q}"), now(m))
                nc.scalar.activation(tmp[1][q][:, :], tmp[0][q][:, :], ACT.Relu).then_inc(S(f"last{q}"), 1)
            for q in range(2):
                norm_square(act, q, m)
            for q in range(2):
                norm_root(act, q, m)

        def tensor(self, pe, m, i, u, windows):
            self.tensor_sums(pe, m, windows)
            for q in range(2):
                pe.wait_ge(S(f"mean{q}"), now(m))
                pe.wait_ge(S(f"ev{q}"), before(m))
                pair_transposes(pe, tmp[0][q], ps[2 + q]).then_inc(S(f"tr{q}"), 1)
            for q in range(2):
                pe.wait_ge(S(f"ev{q}"), now(m))
                pe.wait_ge(S(f"relu{q}"), before(m))
                pe.matmul(ps[4 + q], wi1[:, :], tp[q][:, :], start=True, stop=True).then_inc(S(f"hid{q}"), 1)
            for q in range(2):
                pe.wait_ge(S(f"relu{q}"), now(m))
                pe.wait_ge(S(f"sum{q}"), before(m))
                pair_products(pe, tq[q], wi2, ps[6 + q]).then_inc(S(f"mm{q}"), 1)

    CT = 4

    def tile_transposes(pe, src, bank):
        for r in range(CT):
            last = pe.transpose(bank[:, r * P:(r + 1) * P], src[:, r * P:(r + 1) * P], ident[:, :])
        return last

    def tile_products(pe, lhs, w, bank):
        for r in range(CT):
            last = pe.matmul(bank[:, r * P:(r + 1) * P], lhs[:, r * P:(r + 1) * P], w, start=True, stop=True)
        return last

    class Sage0(Pass):
        loads = (None,)
        stores = ((s1_t, store_a, H, ("s1",), 4), (n1_t, store_b, H, ("n1",), 4))
        consumed = (("hid", 4),)

        def load_block(self, sp, m, u):
            sp.dma_start(load_a[u][0:D, :], a["x_cols"][:, bass.ds(m * BN, BN)]).then_inc(S(f"in{u}"), 16)

        def tensor_sums(self, pe, m, windows):
            if not windows:
                return
            for h in range(2):
                pe.wait_ge(S(f"lo{h}"), now(m))
            for q in range(2):
                pe.wait_ge(S(f"hot{q}"), now(m))
                pe.wait_ge(S(f"mean{q}"), before(m))
                out = lambda j, q=q: ps[q][:, (j % GT) * D:(j % GT + 1) * D]
                count = lambda j, q=q: ps[6 + q][:, j % GT:j % GT + 1]
                sums(pe, m, range(q * GT, q * GT + GT), out, D, count).then_inc(S(f"agg{q}"), 1)

        def vector_loop(self, ve, windows):
            for q in range(2):
                nc.vector.memset(load_b[q][:, :], 0.0).then_inc(S("zeros"), 1)
            ve.wait_ge(S("zeros"), before(2))
            super().vector_loop(ve, windows)

        def vector(self, ve, m, i, u, windows):
            V = nc.vector
            cols = lambda t, q: t[:, bass.ds(m * NT + q * GT, GT)]
            if windows:
                self.split_rest(ve, m + 1)
            for q in range(2):
                agg = self.sums_here(ve, m, i, u, q, windows)
                if windows:
                    V.tensor_scalar(cols(deg, q), ps[6 + q][:, 0:GT], 0.0, None, ALU.add).then_inc(S(f"deg{q}"), 1)
                    ve.wait_ge(S(f"deg{q}"), now(m))
                V.tensor_scalar(stat[:, q, 0, :], cols(deg, q), 1.0, None, ALU.max).then_inc(S(f"least{q}"), 1)
                ve.wait_ge(S(f"least{q}"), now(m))
                V.reciprocal(cols(invdeg, q), stat[:, q, 0, :]).then_inc(S(f"inv{q}"), 1)
                ve.wait_ge(S(f"inv{q}"), now(m))
                ve.wait_ge(S("tr"), before(m * 4))
                V.tensor_tensor(tiles3(load_b[q][:, :], P)[:, :, D:P], tiles3(agg), per_node(invdeg, m, q), ALU.mult).then_inc(S(f"mean{q}"), 1)
            for q in range(2):
                ve.wait_ge(S(f"root{q}"), now(m))
                V.reciprocal(cols(dis, q), stat[:, q, 3, :]).then_inc(S(f"dis{q}"), 1)
            if windows:
                self.split_lo(ve, m + 1)
            self.stored(ve, i, u)
            for c in range(4):
                if c == 2 and windows:
                    self.hots(ve, m + 1)
                ve.wait_ge(S(f"nmm{c % 2}"), before(m * 2 + c // 2 + 1))
                V.tensor_tensor(tiles3(store_a[u][:, c * 512:(c + 1) * 512], H), tiles3(ps[5], H), row(b1r, H, CT), ALU.add).then_inc(S("s1"), 1)

        def scalar(self, act, m, i, u, windows):
            A = nc.scalar
            if windows:
                self.split_hi(act, m + 1)
                self.split_mid(act, m + 1)
            for q in range(2):
                if windows:
                    act.wait_ge(S(f"deg{q}"), now(m))
                act.wait_ge(S(f"dis{q}"), before(m))
                A.activation(stat[:, q, 3, :], deg[:, bass.ds(m * NT + q * GT, GT)], ACT.Sqrt, bias=one_c[:, :]).then_inc(S(f"root{q}"), 1)
            self.stored(act, i, u)

            def evacuate(c):
                act.wait_ge(S("tr"), before(m * 4 + c + 1))
                A.activation(load_a[u][D:P, c * 512:(c + 1) * 512], ps[2][D:P, :], ACT.Copy).then_inc(S("ev"), 1)

            def hidden(c):
                act.wait_ge(S("hid"), before(m * 4 + c + 1))
                act.wait_ge(S(f"nmm{c % 2}"), before(m * 2 + c // 2))
                A.activation(tp[c % 2][:, :], ps[3], ACT.Relu, bias=b0c[:, :]).then_inc(S("rel"), 1)

            def neighbours(c):
                act.wait_ge(S(f"nmm{c % 2}"), before(m * 2 + c // 2 + 1))
                A.activation(store_b[u][:, c * 512:(c + 1) * 512], ps[4], ACT.Copy).then_inc(S("n1"), 1)

            evacuate(0)
            for c in range(4):
                if c < 3:
                    evacuate(c + 1)
                hidden(c)
                if c >= 1:
                    neighbours(c - 1)
            neighbours(3)

        def tensor(self, pe, m, i, u, windows):
            self.tensor_sums(pe, m, windows)

            def turn(c):
                if c % 2 == 0:
                    pe.wait_ge(S(f"mean{c // 2}"), now(m))
                pe.wait_ge(S("ev"), before(m * 4 + c))
                tile_transposes(pe, load_b[c // 2][:, (c % 2) * 512:(c % 2 + 1) * 512], ps[2]).then_inc(S("tr"), 1)

            def hidden(c):
                pe.wait_ge(S("ev"), before(m * 4 + c + 1))
                pe.wait_ge(S("rel"), before(m * 4 + c))
                pe.matmul(ps[3], w0[:, :], load_a[u][:, c * 512:(c + 1) * 512], start=True, stop=True).then_inc(S("hid"), 1)

            def products(c):
                pe.wait_ge(S("rel"), before(m * 4 + c + 1))
                pe.wait_ge(S("n1"), before(m * 4 + c))
                tile_products(pe, tp[c % 2], w1[:, 0:H], ps[4])
                pe.wait_ge(S("s1"), before(m * 4 + c))
                tile_products(pe, tp[c % 2], w1[:, H:2 * H], ps[5]).then_inc(S(f"nmm{c % 2}"), 1)

            turn(0)
            self.inputs_in(pe, i, u)
            for c in range(4):
                if c < 3:
                    turn(c + 1)
                hidden(c)
                if c >= 1:
                    products(c - 1)
            products(3)

    class Sage1(Pass):
        W = H
        loads = ((s1_t, load_a, H),)
        stores = ((s2_t, store_a, D, ("s20", "s21"), 2), (n2_t, store_b, D, ("n20", "n21"), 2))
        consumed = (("pre0", 2), ("pre1", 2))

        def used(self, ve, m, q):
            if isinstance(m, int) and m == 0:
                return
            for s in range(2):
                ve.wait_ge(S(f"agg{s}"), before(m * 2 + q - 1))

        def vector(self, ve, m, i, u, windows):
            V = nc.vector
            if windows:
                self.split_rest(ve, m + 1)
            self.inputs_in(ve, i, u)

            def combine(c):
                s, n = c % 2, m * 2 + c // 2
                if windows:
                    ve.wait_ge(S(f"agg{s}"), now(n))
                    agg = ps[s]
                else:
                    ve.wait_ge(S(f"sums{u}"), landed(f"sums{u}", i))
                    agg = general_sums(u, H)[:, c * 512:(c + 1) * 512]
                ve.wait_ge(S(f"tr{s}"), before(n))
                for r in range(CT):
                    last = V.scalar_tensor_tensor(
                        tmp[0][s][:, r * P:(r + 1) * P], agg[:, r * P:(r + 1) * P],
                        invdeg[:, bass.ds(m * NT + c * CT + r, 1)], load_a[u][:, (c * CT + r) * P:(c * CT + r + 1) * P],
                        ALU.mult, ALU.add)
                last.then_inc(S(f"pre{s}"), 1)

            def own(c):
                s, n = c % 2, m * 2 + c // 2
                ve.wait_ge(S(f"mm{s}"), now(n))
                V.tensor_tensor(tiles3(store_a[u][:, c * 256:(c + 1) * 256]), tiles3(ps[4 + s], H)[:, :, 0:D], row(b2r, D, CT), ALU.add).then_inc(S(f"s2{s}"), 1)

            self.stored(ve, i, u)
            combine(0)
            combine(1)
            if windows:
                self.split_lo(ve, m + 1)
            for c in range(2):
                combine(c + 2)
                own(c)
            if windows:
                self.hots(ve, m + 1)
            own(2)
            own(3)

        def scalar(self, act, m, i, u, windows):
            A = nc.scalar
            if windows:
                self.split_hi(act, m + 1)
                self.split_mid(act, m + 1)
            self.stored(act, i, u)

            def hidden(c):
                s, n = c % 2, m * 2 + c // 2
                act.wait_ge(S(f"tr{s}"), now(n))
                act.wait_ge(S(f"mm{s}"), before(n))
                A.activation(tp[s][:, :], ps[2 + s], ACT.Relu).then_inc(S(f"rel{s}"), 1)

            def neighbours(c):
                s, n = c % 2, m * 2 + c // 2
                act.wait_ge(S(f"s2{s}"), now(n))
                A.activation(tiles3(store_b[u][:, c * 256:(c + 1) * 256]), tiles3(ps[4 + s], H)[:, :, D:H], ACT.Copy).then_inc(S(f"n2{s}"), 1)

            hidden(0)
            for c in range(1, 4):
                hidden(c)
                neighbours(c - 1)
            neighbours(3)

        def tensor(self, pe, m, i, u, windows):
            if windows:
                for h in range(2):
                    pe.wait_ge(S(f"lo{h}"), now(m))

            def collect(c):
                s, n = c % 2, m * 2 + c // 2
                if c % 2 == 0:
                    pe.wait_ge(S(f"hot{c // 2}"), now(m))
                pe.wait_ge(S(f"pre{s}"), before(n))
                out = lambda j: ps[s][:, (j % CT) * H:(j % CT + 1) * H]
                sums(pe, m, range(c * CT, c * CT + CT), out, H).then_inc(S(f"agg{s}"), 1)

            def turn(c):
                s, n = c % 2, m * 2 + c // 2
                pe.wait_ge(S(f"pre{s}"), now(n))
                pe.wait_ge(S(f"rel{s}"), before(n))
                tile_transposes(pe, tmp[0][s], ps[2 + s]).then_inc(S(f"tr{s}"), 1)

            def products(c):
                s, n = c % 2, m * 2 + c // 2
                pe.wait_ge(S(f"rel{s}"), now(n))
                pe.wait_ge(S(f"n2{s}"), before(n))
                tile_products(pe, tp[s], w2[:, :], ps[4 + s]).then_inc(S(f"mm{s}"), 1)

            if windows:
                collect(0)
                collect(1)
            for c in range(4):
                turn(c)
                if windows and c < 2:
                    collect(c + 2)
                if c >= 1:
                    products(c - 1)
            products(3)

    class Messages(Pass):

        def emit(self):
            other = next_pass(self.number)
            with nc.Block() as block:

                @block.sync
                def _(sp):
                    start_at_one(sp, other)

                    def index(m, u):
                        for h in range(2):
                            for buf, ix in ((ix_now, src_ix), (ix_dst, dst_ix)):
                                sp.dma_start(buf[:, 2 * u + h, :], ix[:, bass.ds(m * ET + h * HT, HT)]).then_inc(S(f"ix{2 * u + h}"), 16)

                    def edges(m, u):
                        sp.dma_start(load_a[u][0:DE, 0:ET * P], a["edge_cols"][:, bass.ds(m * ET * P, ET * P)]).then_inc(S(f"in{u}"), 16)

                    sp.wait_ge(S("zeros"), now(1))
                    for u in range(2):
                        index(u, u)
                        edges(u, u)

                    def body(m, u):
                        for h in range(2):
                            sp.wait_ge(S(f"pair{h}"), landed(f"pair{h}", m, 2 * HT))
                        index((m + 2) % NB, u)
                        for h in range(2):
                            sp.wait_ge(S(f"msg{h}"), now(m))
                        sp.dma_start(msg_t[bass.ds(m * ET * P, ET * P), :].rearrange("(p t) f -> p (t f)", p=P),
                                     store_b[u][:, 0:ET * D]).then_inc(S(f"put{u}"), 16)
                        edges((m + 2) % NB, u)

                    bodies(sp, body)
                    for u in range(2):
                        sp.wait_ge(S(f"put{u}"), before(16 * (NB // 2)))
                        sp.wait_ge(S(f"in{u}"), before(16 * (NB // 2 + 1)))
                    for s in range(4):
                        sp.wait_ge(S(f"ix{s}"), before(32 * (NB // 2 + 1)))

                @block.gpsimd
                def _(pool):
                    with pool.Fori(0, NB // 2) as i:
                        for u in range(2):
                            for h in range(2):
                                m = i * 2 + u
                                pool.wait_ge(S(f"ix{2 * u + h}"), landed(f"ix{2 * u + h}", i, 2))
                                pool.wait_ge(S(f"tr{h}"), before(m))
                                gate(pool)
                                for t in range(HT):
                                    for k, ix in enumerate((ix_now, ix_dst)):
                                        at = t * P + k * D
                                        pool.indirect_dma_start(
                                            out=gathered[h][:, at:at + D], out_offset=None, in_=x3_t,
                                            in_offset=bass.IndirectOffsetOnAxis(ap=ix[:, 2 * u + h, t:t + 1], axis=0)).then_inc(S(f"pair{h}"), 16)

                @block.vector
                def _(ve):
                    for u in range(2):
                        nc.vector.memset(load_a[u][:, :], 0.0).then_inc(S("zeros"), 1)

                    def body(m, u, i):
                        self.stored_one(ve, i, u)
                        for h in range(2):
                            ve.wait_ge(S(f"mm{h}"), now(m))
                            nc.vector.tensor_tensor(tiles3(store_b[u][:, h * HT * D:(h + 1) * HT * D]),
                                                         tiles3(ps[4 + h], P)[:, :, 0:D], row(bm2r, D, HT), ALU.add).then_inc(S(f"msg{h}"), 1)

                    with ve.Fori(0, NB // 2) as i:
                        for u in range(2):
                            body(i * 2 + u, u, i)

                @block.scalar
                def _(act):
                    def body(m, u):
                        for h in range(2):
                            act.wait_ge(S(f"tr{h}"), now(m))
                            nc.scalar.activation(tp[h][:, :], ps[h], ACT.Copy).then_inc(S(f"ev{h}"), 1)
                        for h in range(2):
                            act.wait_ge(S(f"hid{h}"), now(m))
                            nc.scalar.activation(tq[h][:, :], ps[2 + h], ACT.Relu, bias=bm1c[:, :]).then_inc(S(f"rel{h}"), 1)

                    bodies(act, body)

                @block.tensor
                def _(pe):
                    def body(m, u, i):
                        for h in range(2):
                            pe.wait_ge(S(f"pair{h}"), landed(f"pair{h}", m, 2 * HT))
                            pe.wait_ge(S(f"ev{h}"), before(m))
                            tile_transposes(pe, gathered[h], ps[h]).then_inc(S(f"tr{h}"), 1)
                        pe.wait_ge(S(f"in{u}"), landed(f"in{u}", i))
                        for h in range(2):
                            pe.wait_ge(S(f"ev{h}"), now(m))
                            pe.wait_ge(S(f"rel{h}"), before(m))
                            pe.matmul(ps[2 + h], wm1[:, :], tp[h][:, :], start=True, stop=False)
                            pe.matmul(ps[2 + h], wm1e[:, :], load_a[u][:, h * 512:(h + 1) * 512], start=False, stop=True).then_inc(S(f"hid{h}"), 1)
                        for h in range(2):
                            pe.wait_ge(S(f"rel{h}"), now(m))
                            pe.wait_ge(S(f"msg{h}"), before(m))
                            tile_products(pe, tq[h], wm2[:, :], ps[4 + h]).then_inc(S(f"mm{h}"), 1)

                    with pe.Fori(0, NB // 2) as i:
                        for u in range(2):
                            body(i * 2 + u, u, i)

        def stored_one(self, eng, i, u):
            eng.wait_ge(S(f"put{u}"), before(i * 16))

    class Update(Pass):
        dmas = 1
        rows = "edges_in"
        loads = ((x3_t, load_b, D),)
        stores = ((out, store_a, D, ("out0", "out1"), 1),)
        consumed = (("pre0", 1), ("pre1", 1))

        def row_loads(self, sp, n, at):
            block = msg_t[bass.ds(at * ET * P, ET * P), :].rearrange("(p t) f -> p (t f)", p=P)
            for h in range(2):
                sp.wait_ge(S(f"rest{h}"), before(n))
                sp.dma_start(gathered[h][:, 0:HT * D], block[:, h * HT * D:(h + 1) * HT * D]).then_inc(S(f"edges_in{h}"), 16)

        def sync_rows_first(self, sp):
            self.row_loads(sp, 0, 0)

        def sync_rows(self, sp, m, u):
            self.row_loads(sp, m + 1, (m + 1) % NB)

        def sync_rows_last(self, sp):
            for h in range(2):
                sp.wait_ge(S(f"edges_in{h}"), before(16 * (NB + 1)))

        def gpsimd_windows(self, pool):
            pass

        def vector(self, ve, m, i, u, windows):
            V = nc.vector
            if windows:
                self.split_rest(ve, m + 1)
            for q in range(2):
                agg = self.sums_here(ve, m, i, u, q, windows)
                for s in range(2):
                    ve.wait_ge(S(f"tr{s}"), before(m * 2))
                V.tensor_copy(tiles3(load_a[q][:, 0:GT * P], P)[:, :, D:P], tiles3(agg)).then_inc(S(f"mean{q}"), 1)
            if windows:
                self.split_lo(ve, m + 1)
            self.inputs_in(ve, i, u)

            def add_bias(c):
                s, n, q = c % 2, m * 2 + c // 2, c // 2
                ve.wait_ge(S(f"out{q}"), before(m))
                ve.wait_ge(S(f"mm{s}"), now(n))
                V.tensor_tensor(tiles3(tmp[0][q][:, (c % 2) * 256:(c % 2 + 1) * 256]),
                                     tiles3(ps[6 + s], P)[:, :, 0:D], row(bu2r, D, CT), ALU.add).then_inc(S(f"sum{s}"), 1)

            for q in range(2):
                add_bias(2 * q)
                add_bias(2 * q + 1)
                for s in range(2):
                    ve.wait_ge(S(f"sum{s}"), now(m * 2 + q))
                V.tensor_tensor(tmp[1][q][:, :], tmp[0][q][:, :], group(load_b[u], q), ALU.add).then_inc(S(f"pre{q}"), 1)
                ve.wait_ge(S(f"pre{q}"), now(m))
                norm_center(ve, q, m)
                if windows and q == 0:
                    self.hots(ve, m + 1)
            for q in range(2):
                norm_var(ve, q, m)
            self.stored(ve, i, u)
            for q in range(2):
                norm_out(ve, q, m, group(store_a[u], q))

        def scalar(self, act, m, i, u, windows):
            A = nc.scalar
            self.inputs_in(act, i, u)
            for q in range(2):
                for s in range(2):
                    act.wait_ge(S(f"tr{s}"), before(m * 2))
                A.activation(tiles3(load_a[q][:, 0:GT * P], P)[:, :, 0:D], tiles3(group(load_b[u], q)), ACT.Copy).then_inc(S(f"own{q}"), 1)
            if windows:
                self.split_hi(act, m + 1)
                self.split_mid(act, m + 1)

            def turned(c):
                s, n = c % 2, m * 2 + c // 2
                act.wait_ge(S(f"tr{s}"), now(n))
                act.wait_ge(S(f"hid{s}"), before(n))
                A.activation(tp[s][:, :], ps[2 + s], ACT.Copy).then_inc(S(f"ev{s}"), 1)

            def hidden(c):
                s, n = c % 2, m * 2 + c // 2
                act.wait_ge(S(f"hid{s}"), now(n))
                act.wait_ge(S(f"mm{s}"), before(n))
                A.activation(store_b[s][:, 0:512], ps[4 + s], ACT.Relu, bias=bu1c[:, :]).then_inc(S(f"rel{s}"), 1)

            turned(0)
            for c in range(4):
                if c < 3:
                    turned(c + 1)
                hidden(c)
            for q in range(2):
                norm_square(act, q, m)
            for q in range(2):
                norm_root(act, q, m)

        def tensor(self, pe, m, i, u, windows):
            self.tensor_sums(pe, m, windows)

            def turn(c):
                s, n, q = c % 2, m * 2 + c // 2, c // 2
                if c % 2 == 0:
                    pe.wait_ge(S(f"mean{q}"), now(m))
                    pe.wait_ge(S(f"own{q}"), now(m))
                pe.wait_ge(S(f"ev{s}"), before(n))
                tile_transposes(pe, load_a[q][:, (c % 2) * 512:(c % 2 + 1) * 512], ps[2 + s]).then_inc(S(f"tr{s}"), 1)

            def hidden(c):
                s, n = c % 2, m * 2 + c // 2
                pe.wait_ge(S(f"ev{s}"), now(n))
                pe.wait_ge(S(f"rel{s}"), before(n))
                pe.matmul(ps[4 + s], wu1[:, :], tp[s][:, :], start=True, stop=True).then_inc(S(f"hid{s}"), 1)

            def products(c):
                s, n = c % 2, m * 2 + c // 2
                pe.wait_ge(S(f"rel{s}"), now(n))
                pe.wait_ge(S(f"sum{s}"), before(n))
                tile_products(pe, store_b[s], wu2[:, :], ps[6 + s]).then_inc(S(f"mm{s}"), 1)

            turn(0)
            for c in range(4):
                if c < 3:
                    turn(c + 1)
                hidden(c)
                if c >= 1:
                    products(c - 1)
            products(3)

    class Degrees(Pass):
        loads = ()
        stores = ()

        def emit(self):
            other = next_pass(self.number)
            with nc.Block() as block:

                @block.sync
                def _(sp):
                    start_at_one(sp, other)

                    def general():
                        self.gen.sync(sp)
                        sp.wait_ge(S("g_all"), now(0))
                        with sp.Fori(0, NB) as m:
                            sp.wait_ge(S("deg"), before(m))
                            self.load_sums(sp, m, 0)
                        sp.wait_ge(S("deg"), now(NB - 1))

                    both_ways(sp, general, lambda: None)

                @block.gpsimd
                def _(pool):
                    both_ways(pool, lambda: self.gen.gpsimd(pool), lambda: None)

                @block.vector
                def _(ve):
                    def general():
                        self.gen.vector(ve)
                        with ve.Fori(0, NB) as m:
                            ve.wait_ge(S("sums0"), landed("sums0", m))
                            nc.vector.tensor_scalar(deg[:, bass.ds(m * NT, NT)], tiles3(general_sums(0, D))[:, :, 0], 0.0, None, ALU.add).then_inc(S("deg"), 1)

                    both_ways(ve, general, lambda: None)

                @block.tensor
                def _(pe):
                    both_ways(pe, lambda: self.gen.tensor(pe), lambda: None)

            pass_over(self)

    with ctx:
        setup()
        Degrees(1, None, General(sums_t, D)).emit()
        Sage0(2, a["x_rows"], General(sums_t, D, table=a["x_rows"])).emit()
        Sage1(3, n1_t, General(sums2_t, H, table=n1_t)).emit()
        Sage2(4, n2_t, General(sums_t, D, table=n2_t)).emit()
        Gcn1(5, y1_t, General(sums_t, D, table=y1_t)).emit()
        Gcn2(6, y2_t, General(sums_t, D, table=y2_t)).emit()
        Gin(7, x2_t, General(sums_t, D, table=x2_t)).emit()
        Messages(8, x3_t, None).emit()
        Update(9, None, General(sums_t, D, direct=msg_t)).emit()


OUT_ROWS = (100000, D)
WEIGHTS = ["L0_gnn_ws0", "L0_gnn_wn0", "L0_gnn_b0", "L0_gnn_ws1", "L0_gnn_wn1", "L0_gnn_b1", "L0_gnn_ws2", "L0_gnn_wn2",
           "L0_gnn_b2", "L1_gnn_W1", "L1_gnn_b1", "L1_gnn_W2", "L1_gnn_b2", "L2_gnn_W1", "L2_gnn_b1", "L2_gnn_W2", "L2_gnn_b2",
           "L3_gnn_mW1", "L3_gnn_mb1", "L3_gnn_mW2", "L3_gnn_mb2", "L3_gnn_uW1", "L3_gnn_ub1", "L3_gnn_uW2", "L3_gnn_ub2"]


def kernel(**inputs):
    import numpy as np
    import concourse.bacc as bacc
    from concourse.bass_utils import run_bass_kernel_spmd as run

    x, src, dst, edge = (np.asarray(inputs[n]) for n in ("x", "src", "dst", "edge_attr_32"))
    z = Sizes(x.shape[0], src.shape[0])
    E = z.etiles * P
    x_pad = np.zeros((z.rows, D), x.dtype)
    x_pad[BN:BN + z.nodes] = x
    x_rows = np.ascontiguousarray(x_pad.reshape(z.nb, NT, P, D).transpose(0, 2, 1, 3)).reshape(z.rows, D)
    x_cols = np.ascontiguousarray(x_pad.T)
    src_pad = np.zeros(E, np.int32)
    src_pad[:z.edges] = src
    dst_pad = np.full(E + P, z.pad_node, np.int32)
    dst_pad[:z.edges] = dst
    by_tile = lambda v: np.ascontiguousarray(v.reshape(z.etiles, P).T)
    edge_pad = np.zeros((DE, E), edge.dtype)
    edge_pad[:, :z.edges] = edge.T
    arrays = {
        "x_rows": x_rows, "x_cols": x_cols, "edge_cols": edge_pad,
        "src_pt": by_tile(src_pad), "dst_pt": by_tile(dst_pad[:E]), "dstn_pt": by_tile(dst_pad[1:E + 1]),
        "dst_rows": dst_pad.reshape(z.etiles + 1, P),
    }
    for n in WEIGHTS:
        arrays[n] = np.ascontiguousarray(inputs[n])
    nc = bacc.Bacc("TRN2", target_bir_lowering=False, num_devices=1)
    a = {n: nc.dram_tensor(n, v.shape, mybir.dt.from_np(v.dtype), kind="ExternalInput").ap() for n, v in arrays.items()}
    out = nc.dram_tensor("out", [z.rows, D], F32, kind="ExternalOutput").ap()
    build(nc, z, a, out)
    r = run(nc, [arrays], core_ids=[0])
    got = np.asarray(r.results[0]["out"]).reshape(z.nb, P, NT, D).transpose(0, 2, 1, 3).reshape(z.rows, D)
    return np.ascontiguousarray(got[BN:BN + z.nodes])
```

```python
import concourse.bass as bass
from concourse import mybir
from contextlib import ExitStack

F32, BF16, F16, I32 = mybir.dt.float32, mybir.dt.bfloat16, mybir.dt.float16, mybir.dt.int32
ALU = mybir.AluOpType
ACT = mybir.ActivationFunctionType
AX = mybir.AxisListType

P = 128
NT = 16
BN = P * NT
GT = 8
ET = 8
HT = 4
D = 64
H = 128
DE = 32
EPS = 1e-5
RB = 8
RING = RB * ET
IX = 4 * ET


class Sizes:

    def __init__(self, nodes, edges):
        self.nodes, self.edges = nodes, edges
        self.nb = -(-nodes // BN) + 1
        self.nb += self.nb % 2
        self.tiles = self.nb * NT
        self.etiles = self.nb * ET
        assert self.etiles * P >= edges
        self.ix_columns = -(-self.etiles // IX) * IX
        self.rows = self.nb * BN
        assert nodes < self.rows - BN
        self.pad_node = (self.nb - 1) * BN
        self.wide = -(-(self.tiles + NT) // P) * P


def build(nc, z, a, out):
    ctx = ExitStack()
    NB = z.nb

    def sb(name, shape, dt=F32):
        return ctx.enter_context(nc.sbuf_tensor(name, shape, dt))

    def dram(name, shape, dt=F32):
        return nc.dram_tensor(name, shape, dt).ap()

    sets = [[ctx.enter_context(nc.semaphore(f"set{k}_{i}")) for i in range(72)] for k in range(2)]
    names, current = {}, [0]
    soft, base, first = {}, {}, [0]
    POOL_DMAS = ("wing0", "wing1", "rows0", "rows1", "pair0", "pair1", "g_rows", "g_old", "g_put")

    def kept(name):
        return f"{name}_{current[0]}" if name[0:2] == "g_" else name

    def S(name):
        if name in POOL_DMAS:
            key = kept(name)
            if key not in soft:
                soft[key] = ctx.enter_context(nc.semaphore(key))
            return soft[key]
        if name not in names:
            names[name] = sets[current[0]][len(names)]
        return names[name]

    def since(name):
        return base.get(kept(name), 0) if name in POOL_DMAS else first[0]

    def carry(name, count):
        base[kept(name)] = since(name) + count

    def next_pass(number):
        current[0], first[0] = number % 2, 1
        names.clear()
        return sets[1 - current[0]]

    def start_at_one(sp, semaphores):
        for s in semaphores:
            sp.sem_clear(s)
            sp.sem_inc(s, 1)

    def now(uses):
        return uses + (1 + first[0])

    def before(uses):
        return uses + first[0]

    def landed(name, uses, dmas=1):
        return uses * (16 * dmas) + (16 * dmas + since(name))

    s1_t, n1_t = dram("s1_t", [z.rows, H]), dram("n1_t", [z.rows, H])
    s2_t, n2_t = dram("s2_t", [z.rows, D]), dram("n2_t", [z.rows, D])
    x1_t, y1_t, y2_t = (dram(n, [z.rows, D]) for n in ("x1_t", "y1_t", "y2_t"))
    x2_t, x3_t = dram("x2_t", [z.rows, D]), dram("x3_t", [z.rows, D])
    msg_t = dram("msg_t", [z.etiles * P, D])
    sums_t, sums2_t = dram("sums_t", [z.rows, D]), dram("sums2_t", [z.rows, H])
    win_d = dram("win_d", [z.wide], I32)
    slot_d = dram("slot_d", [2, z.wide], I32)
    pref_d = dram("pref_d", [3, 32 * 32], I32)

    def block_of(table, m, width):
        return table[bass.ds(m * BN, BN), :].rearrange("(p j) f -> p (j f)", p=P)

    src_ix = sb("src_ix", [P, z.ix_columns], I32)
    dst_ix = sb("dst_ix", [P, z.ix_columns], I32)
    dst_f = sb("dst_f", [P, z.etiles])
    window = sb("window", [P, 2, z.wide])
    slots = sb("slots", [1, 2, z.tiles], I32)
    flag = sb("flag", [1, 4], I32)
    deg = sb("deg", [P, z.tiles])
    invdeg = sb("invdeg", [P, z.tiles])
    dis = sb("dis", [P, z.tiles])
    ident = sb("ident", [P, P])
    iota = sb("iota", [P, P])
    eps_c = sb("eps_c", [P, 1])
    w0 = sb("w0", [P, H])
    w1 = sb("w1", [P, 2 * H])
    w2 = sb("w2", [P, H])
    wg1, wg2, wi1, wi2 = (sb(n, [P, P]) for n in ("wg1", "wg2", "wi1", "wi2"))
    wm1 = sb("wm1", [P, H])
    wm1e = sb("wm1e", [P, H])
    wm2 = sb("wm2", [P, P])
    wu1, wu2 = sb("wu1", [P, H]), sb("wu2", [P, P])
    b0c, bg1c, bi1c, bm1c, bu1c = (sb(n, [P, 1]) for n in ("b0c", "bg1c", "bi1c", "bm1c", "bu1c"))
    b1r, b2r, bg2r, bi2r, bm2r, bu2r = (
        sb(n, [P, w]) for n, w in (("b1r", H), ("b2r", D), ("bg2r", D), ("bi2r", D), ("bm2r", D), ("bu2r", D)))

    ps_all = ctx.enter_context(nc.psum_tensor("ps_all", [P, 8 * 512], F32))
    ps = [ps_all[:, 512 * i:512 * (i + 1)] for i in range(8)]

    def work(name, bytes_):
        return sb(name, [P, bytes_ // 4])

    ring = sb("ring", [P, RING * H])
    onehot = sb("onehot", [P, 2, 2, GT, P])
    load_a = [work(f"load_a{u}", NT * H * 4) for u in range(2)]
    load_b = [work(f"load_b{u}", NT * D * 4) for u in range(2)]
    store_a = [work(f"store_a{u}", NT * H * 4) for u in range(2)]
    store_b = [work(f"store_b{u}", NT * H * 4) for u in range(2)]
    tmp = [[work(f"tmp{k}{q}", 2048) for q in range(2)] for k in range(2)]
    tp = [work(f"tp{q}", 2048) for q in range(2)]
    tq = [work(f"tq{q}", 2048) for q in range(2)]
    stat = sb("stat", [P, 2, 4, GT])
    sq = [work(f"sq{q}", 2048) for q in range(2)]
    ix_now = sb("ix_now", [P, 2 * IX], I32)
    ix_dst = sb("ix_dst", [P, 2 * IX], I32)

    def setup():
        pro = ExitStack()

        def tb(name, shape, dt=F32):
            return pro.enter_context(nc.sbuf_tensor(name, shape, dt))

        E = z.etiles
        ring_i = ring[:, :].bitcast(I32)
        used = [0]

        def part(n, dt=I32):
            v = ring_i[:, used[0]:used[0] + n]
            used[0] += n
            assert used[0] <= RING * H
            return v if dt == I32 else v.bitcast(dt)

        src_i, dst_i, nxt_i = part(E), part(E), part(E)
        t_i, u_i, v_i = part(E), part(E), part(E)
        hi_f, lo_f, gt_f = part(E, F32), part(E, F32), part(E, F32)
        i32_i = part(32)
        i32_f = part(32, F32)
        CH = 8
        oh = tb("oh", [P, 2, 2, CH, 32], BF16)
        tri = tb("tri", [32, 32])
        ones = tb("ones", [P, 32])
        sc = tb("sc", [32, 12, 32])
        sc_i = tb("sc_i", [32, 6, 32], I32)
        viol = tb("viol", [P, 4])
        kw = tb("kw", [P, z.wide // P], I32)
        kw2 = tb("kw2", [P, z.wide // P], I32)
        tid = tb("tid", [P, z.wide // P])
        win_g = tb("win_g", [P, 2, 2, P], I32)
        win_f = tb("win_f", [P, 2, 2, P])
        iota_i = tb("iota_i", [P, P], I32)
        tid_i = tb("tid_i", [P, z.wide // P], I32)
        zero_i = tb("zero_i", [1, 2 * NT], I32)
        steps = E // CH
        NW = z.wide // P

        with nc.Block() as block:
            n_loads = [0]

            @block.sync
            def _(sp):
                start_at_one(sp, sets[1])

                def load(dst, src):
                    sp.dma_start(dst, src).then_inc(S("weights"), 16)
                    n_loads[0] += 1

                for d, s in ((src_i, a["src_pt"]), (dst_i, a["dst_pt"]), (nxt_i, a["dstn_pt"])):
                    sp.dma_start(d, s).then_inc(S("edges"), 16)
                load(w0[0:D, :], a["L0_gnn_ws0"])
                load(w0[D:P, :], a["L0_gnn_wn0"])
                load(w1[:, 0:H], a["L0_gnn_wn1"])
                load(w1[:, H:2 * H], a["L0_gnn_ws1"])
                load(w2[:, 0:D], a["L0_gnn_ws2"])
                load(w2[:, D:H], a["L0_gnn_wn2"])
                load(wm1[:, :], a["L3_gnn_mW1"][0:P, :])
                load(wu1[:, :], a["L3_gnn_uW1"])
                sp.wait_ge(S("zeroed"), 1)
                for w, n in ((wg1, "L1_gnn_W1"), (wg2, "L1_gnn_W2"), (wi1, "L2_gnn_W1"), (wi2, "L2_gnn_W2")):
                    load(w[0:D, 0:D], a[n])
                    load(w[D:P, D:P], a[n])
                load(wm1e[0:DE, :], a["L3_gnn_mW1"][P:P + DE, :])
                load(wm2[:, 0:D], a["L3_gnn_mW2"])
                load(wu2[:, 0:D], a["L3_gnn_uW2"])
                col = lambda n: a[n].rearrange("(p o) -> p o", o=1)
                load(b0c[:, :], col("L0_gnn_b0"))
                load(bm1c[:, :], col("L3_gnn_mb1"))
                load(bu1c[:, :], col("L3_gnn_ub1"))
                for b, n in ((bg1c, "L1_gnn_b1"), (bi1c, "L2_gnn_b1")):
                    load(b[0:D, :], col(n))
                    load(b[D:P, :], col(n))
                for b, n in ((b1r, "L0_gnn_b1"), (b2r, "L0_gnn_b2"), (bg2r, "L1_gnn_b2"), (bi2r, "L2_gnn_b2"),
                             (bm2r, "L3_gnn_mb2"), (bu2r, "L3_gnn_ub2")):
                    load(b[:, :], a[n].partition_broadcast(P))
                sp.wait_ge(S("pref"), 1)
                for k in range(3):
                    sp.dma_start(pref_d[k, :].rearrange("(a b) -> a b", a=32), sc_i[:, 3 + k, :]).then_inc(S("tabs"), 16)
                sp.wait_ge(S("tabs"), 48)
                NR = z.tiles - NT
                sp.dma_start(win_d[NT:z.tiles], pref_d[0, 0:NR]).then_inc(S("tabs2"), 16)
                sp.dma_start(win_d[0:NT].rearrange("(o n) -> o n", o=1), zero_i[:, 0:NT]).then_inc(S("tabs2"), 16)
                for k in range(2):
                    sp.dma_start(slot_d[k, NT:z.tiles], pref_d[1 + k, 0:NR]).then_inc(S("tabs2"), 16)
                    sp.dma_start(slot_d[k:k + 1, 0:NT], zero_i[:, 0:NT]).then_inc(S("tabs2"), 16)
                left = z.wide - z.tiles
                for at in range(0, left, NT):
                    n = min(NT, left - at)
                    sp.dma_start(win_d[z.tiles + at:z.tiles + at + n].rearrange("(o n) -> o n", o=1), zero_i[:, 0:n]).then_inc(S("tabs2"), 16)
                sp.wait_ge(S("tabs2"), 16 * (6 + len(range(0, left, NT))))
                for k in range(2):
                    sp.dma_start(slots[:, k, :], slot_d[k:k + 1, 0:z.tiles]).then_inc(S("tabs3"), 16)
                with nc.allow_non_contiguous_dma(reason="a table of a few hundred numbers, once"):
                    sp.dma_start(kw[:, :], win_d.rearrange("(c p) -> p c", p=P)).then_inc(S("tabs4"), 16)
                sp.wait_ge(S("tabs3"), 32)
                sp.wait_ge(S("weights"), 16 * n_loads[0])

            @block.gpsimd
            def _(pool):
                pool.memset(tri[:, :], 1.0).then_inc(S("poolc"), 1)
                pool.wait_ge(S("poolc"), 1)
                pool.affine_select(out=tri[:, :], in_=tri[:, :], compare_op=ALU.is_gt, fill=0.0, base=0,
                                   pattern=[[1, 32]], channel_multiplier=-1).then_inc(S("poolc"), 1)
                pool.memset(ident[:, :], 0.0).then_inc(S("poolc"), 1)
                pool.wait_ge(S("poolc"), 3)
                pool.affine_select(out=ident[:, :], in_=ident[:, :], compare_op=ALU.not_equal, fill=1.0, base=0,
                                   pattern=[[-1, P]], channel_multiplier=1).then_inc(S("poolc"), 1)
                pool.iota(iota_i[:, :], pattern=[[1, P]], base=0, channel_multiplier=0).then_inc(S("iotas"), 1)
                pool.iota(i32_i, pattern=[[1, 32]], base=0, channel_multiplier=0).then_inc(S("iotas"), 1)
                pool.iota(sc_i[:, 0, :], pattern=[[1, 32]], base=0, channel_multiplier=32).then_inc(S("iotas"), 1)
                pool.iota(tid_i[:, :], pattern=[[P, NW]], base=0, channel_multiplier=1).then_inc(S("iotas"), 1)
                pool.wait_ge(S("tabs4"), 16)
                pool.wait_ge(S("kw2"), 1)
                for c in range(NW):
                    if c >= 2:
                        pool.wait_ge(S("winf"), c - 1)
                    for k, ix in enumerate((kw, kw2)):
                        pool.indirect_dma_start(
                            out=win_g[:, c % 2, k, :], out_offset=None, in_=a["dst_rows"],
                            in_offset=bass.IndirectOffsetOnAxis(ap=ix[:, c:c + 1], axis=0)).then_inc(S(f"wing{c % 2}"), 16)

            @block.vector
            def _(ve):
                k = [0]

                def step(ins):
                    k[0] += 1
                    ins.then_inc(S("chain"), 1)
                    ve.wait_ge(S("chain"), k[0])

                V = nc.vector
                for w in (wg1, wg2, wi1, wi2, wm1e, wm2, wu2):
                    last = V.memset(w[:, :], 0.0)
                last.then_inc(S("zeroed"), 1)
                step(V.memset(zero_i[:, :], 0))
                step(V.memset(ones[:, :], 1.0))
                step(V.memset(eps_c[:, :], EPS))
                step(V.memset(viol[:, :], 0.0))
                step(V.memset(flag[:, :], 0))
                for d in (src_ix, dst_ix):
                    step(V.memset(d[:, :], 0))
                ve.wait_ge(S("iotas"), 4)
                step(V.tensor_copy(iota[:, :], iota_i[:, :]))
                step(V.tensor_copy(i32_f, i32_i))
                step(V.tensor_copy(tid[:, :], tid_i[:, :]))
                step(V.tensor_copy(sc[:, 11, :], sc_i[:, 0, :]))
                step(V.tensor_scalar(tid[:, :], tid[:, :], float(-P), float(P * NT), ALU.mult, ALU.add))
                ve.wait_ge(S("edges"), 48)
                step(V.tensor_copy(dst_f[:, :], dst_i))
                for d, s in ((src_ix, src_i), (dst_ix, dst_i)):
                    step(V.tensor_scalar(t_i, s, 11, 11, ALU.logical_shift_right, ALU.logical_shift_left))
                    step(V.tensor_scalar(u_i, s, 127, 4, ALU.bitwise_and, ALU.logical_shift_left))
                    step(V.tensor_scalar(v_i, s, 7, 15, ALU.logical_shift_right, ALU.bitwise_and))
                    step(V.tensor_tensor(u_i, u_i, v_i, ALU.add))
                    step(V.tensor_tensor(u_i, u_i, t_i, ALU.add))
                    step(V.tensor_scalar(d[:, 0:E], u_i, float(BN), float(z.rows - 1), ALU.add, ALU.min))
                step(V.tensor_copy(hi_f, nxt_i))
                step(V.tensor_tensor(gt_f, dst_f[:, :], hi_f, ALU.is_gt))
                step(V.tensor_reduce(viol[:, 0:1], gt_f, AX.X, ALU.add))
                step(V.tensor_scalar(t_i, dst_i, 12, None, ALU.logical_shift_right))
                step(V.tensor_scalar(u_i, dst_i, 7, 31, ALU.logical_shift_right, ALU.bitwise_and))
                step(V.tensor_copy(hi_f, t_i))
                step(V.tensor_copy(lo_f, u_i))
                for s in range(steps):
                    if s >= 2:
                        ve.wait_ge(S("hist"), s - 1)
                    for d, v in enumerate((hi_f, lo_f)):
                        V.tensor_tensor(oh[:, s % 2, d, :, :],
                                        i32_f.unsqueeze(1).to_broadcast([P, CH, 32]),
                                        v[:, s * CH:(s + 1) * CH].unsqueeze(2).to_broadcast([P, CH, 32]),
                                        ALU.is_equal).then_inc(S("ohs"), 1)
                ve.wait_ge(S("hist"), steps)
                C, INC, EXC, ENDS, A, B, CC, DD = range(8)
                step(V.tensor_copy(sc[:, C, :], ps[0][0:32, 0:32]))
                step(V.tensor_tensor_scan(sc[:, INC, :], ones[0:32, :], sc[:, C, :], 0.0, ALU.mult, ALU.add))
                V.tensor_copy(sc[:, 10, 0:1], sc[:, INC, 31:32]).then_inc(S("tot"), 1)
                ve.wait_ge(S("rowp"), 1)
                step(V.tensor_copy(sc[:, 10, 1:2], ps[1][0:32, 0:1]))
                step(V.tensor_scalar(sc[:, ENDS, :], sc[:, INC, :], sc[:, 10, 1:2], None, ALU.add))
                step(V.tensor_tensor(sc[:, EXC, :], sc[:, ENDS, :], sc[:, C, :], ALU.subtract))
                step(V.tensor_copy(sc_i[:, 1, :], sc[:, EXC, :]))
                step(V.tensor_scalar(sc_i[:, 3, :], sc_i[:, 1, :], 7, None, ALU.logical_shift_right))
                step(V.tensor_copy(sc[:, A, :], sc_i[:, 3, :]))
                step(V.tensor_scalar(sc[:, B, :], sc[:, A, :], float(P), float(2 * P), ALU.mult, ALU.add))
                step(V.tensor_tensor(sc[:, B, :], sc[:, ENDS, :], sc[:, B, :], ALU.is_gt))
                step(V.tensor_scalar(sc_i[:, 1, :], sc_i[:, 0, :], 4, 3, ALU.logical_shift_right, ALU.logical_shift_left))
                step(V.tensor_copy(sc[:, CC, :], sc_i[:, 1, :]))
                step(V.tensor_tensor(sc[:, DD, :], sc[:, A, :], sc[:, CC, :], ALU.subtract))
                step(V.tensor_scalar(sc[:, CC, :], sc[:, DD, :], float(2 * ET - 2), None, ALU.is_gt))
                step(V.tensor_tensor(sc[:, B, :], sc[:, B, :], sc[:, CC, :], ALU.add))
                step(V.tensor_scalar(sc[:, CC, :], sc[:, DD, :], float(-ET), None, ALU.is_lt))
                step(V.tensor_tensor(sc[:, B, :], sc[:, B, :], sc[:, CC, :], ALU.add))
                step(V.tensor_scalar(sc[:, CC, :], sc[:, 11, :], float(z.tiles - NT), None, ALU.is_lt))
                step(V.tensor_tensor(sc[:, B, :], sc[:, B, :], sc[:, CC, :], ALU.mult))
                step(V.tensor_reduce(viol[0:32, 1:2], sc[:, B, :], AX.X, ALU.add))
                V.tensor_tensor(viol[:, 2:3], viol[:, 0:1], viol[:, 1:2], ALU.add).then_inc(S("viol"), 1)
                step(V.tensor_scalar(sc_i[:, 1, :], sc_i[:, 3, :], 1.0, None, ALU.add))
                step(V.tensor_scalar(sc_i[:, 4, :], sc_i[:, 3, :], RING - 1, None, ALU.bitwise_and))
                step(V.tensor_scalar(sc_i[:, 5, :], sc_i[:, 1, :], RING - 1, None, ALU.bitwise_and))
                step(V.tensor_scalar(sc[:, A, :], sc[:, A, :], float(z.etiles - 1), None, ALU.min))
                V.tensor_copy(sc_i[:, 3, :], sc[:, A, :]).then_inc(S("pref"), 1)
                ve.wait_ge(S("violp"), 1)
                step(V.tensor_scalar(sc[0:1, CC, 0:1], ps[2][0:1, 0:1], 1.0, None, ALU.min))
                step(V.tensor_copy(flag[0:1, 0:1], sc[0:1, CC, 0:1]))
                ve.wait_ge(S("tabs4"), 16)
                V.tensor_scalar(kw2[:, :], kw[:, :], 1.0, None, ALU.add).then_inc(S("kw2"), 1)
                for c in range(NW):
                    ve.wait_ge(S(f"wing{c % 2}"), 32 * (c // 2 + 1))
                    if c >= 2:
                        ve.wait_ge(S("wint"), c - 1)
                    V.tensor_scalar(win_f[:, c % 2, :, :], win_g[:, c % 2, :, :], tid[:, c:c + 1], None,
                                    ALU.add).then_inc(S("winf"), 1)
                    ve.wait_ge(S("wint"), c + 1)
                    V.tensor_copy(window[:, :, c * P:(c + 1) * P],
                                  ps[4 + c % 2][:, 0:2 * P].rearrange("p (k t) -> p k t", k=2)).then_inc(S("wins"), 1)
                ve.wait_ge(S("wins"), NW)

            @block.tensor
            def _(pe):
                for s in range(steps):
                    pe.wait_ge(S("ohs"), 2 * s + 2)
                    for k in range(CH):
                        last = pe.matmul(ps[0][0:32, 0:32], oh[:, s % 2, 0, k, :], oh[:, s % 2, 1, k, :],
                                         start=(s + k == 0), stop=(s == steps - 1 and k == CH - 1))
                    last.then_inc(S("hist"), 1)
                pe.wait_ge(S("tot"), 1)
                pe.wait_ge(S("poolc"), 4)
                pe.matmul(ps[1][0:32, 0:1], tri[:, :], sc[:, 10, 0:1], start=True, stop=True).then_inc(S("rowp"), 1)
                pe.wait_ge(S("viol"), 1)
                pe.matmul(ps[2][0:1, 0:1], viol[:, 2:3], ones[:, 0:1], start=True, stop=True).then_inc(S("violp"), 1)
                for c in range(NW):
                    pe.wait_ge(S("winf"), c + 1)
                    if c >= 2:
                        pe.wait_ge(S("wins"), c - 1)
                    for k in range(2):
                        last = pe.transpose(ps[4 + c % 2][:, k * P:(k + 1) * P], win_f[:, c % 2, k, :], ident[:, :])
                    last.then_inc(S("wint"), 1)

        pro.close()

    g_rows, g_old = work("g_rows", H * 4), work("g_old", H * 4)
    g_new, g_same, g_low = work("g_new", H * 4), work("g_same", P * 4), work("g_low", P * 4)
    g_mask = sb("g_mask", [P, P])
    g_dst = sb("g_dst", [P, P], I32)
    g_small = sb("g_small", [P, 4])
    g_ix = sb("g_ix", [P, 3], I32)
    BIG = 1 << 22

    class General:

        def __init__(self, sums, width, table=None, direct=None):
            self.sums, self.width, self.table, self.direct = sums, width, table, direct

        def sync(self, sp):
            W = self.width
            sp.wait_ge(S("g_zero"), now(0))
            with sp.Fori(0, z.nb) as m:
                sp.dma_start(block_of(self.sums, m, W), store_a[0][:, 0:NT * W]).then_inc(S("g_cleared"), 16)

            def tile(m, t):
                k = m * ET + t
                sp.wait_ge(S("g_same"), before(k))
                sp.dma_start(g_dst[:, :], a["dst_rows"][bass.ds(k, 1), :].rearrange("o e -> (o e)").partition_broadcast(P)).then_inc(S("g_dst"), 16)
                if self.direct is not None:
                    sp.wait_ge(S("g_sum"), before(k))
                    block = self.direct[bass.ds(m * ET * P, ET * P), :].rearrange("(p t) f -> p t f", t=ET)
                    sp.dma_start(g_rows[:, 0:W], block[:, t, :]).then_inc(S("g_direct"), 16)

            with sp.Fori(0, NB) as m:
                for t in range(ET):
                    tile(m, t)

        def gpsimd(self, pool):
            W = self.width
            pool.memset(g_mask[:, :], 1.0).then_inc(S("g_mask"), 1)
            pool.wait_ge(S("g_mask"), before(1))
            pool.affine_select(out=g_mask[:, :], in_=g_mask[:, :], compare_op=ALU.is_gt, fill=0.0, base=0,
                               pattern=[[-1, P]], channel_multiplier=1).then_inc(S("g_mask"), 1)
            pool.wait_ge(S("g_cleared"), before(16 * z.nb))
            with pool.Fori(0, z.etiles) as k:
                pool.wait_ge(S("g_ix"), now(k))
                gate(pool)
                if self.table is not None:
                    pool.wait_ge(S("g_sum"), before(k))
                    gate(pool)
                    pool.indirect_dma_start(out=g_rows[:, 0:W], out_offset=None, in_=self.table,
                                            in_offset=bass.IndirectOffsetOnAxis(ap=g_ix[:, 0:1], axis=0)).then_inc(S("g_rows"), 16)
                pool.indirect_dma_start(out=g_old[:, 0:W], out_offset=None, in_=self.sums,
                                        in_offset=bass.IndirectOffsetOnAxis(ap=g_ix[:, 1:2], axis=0)).then_inc(S("g_old"), 16)
                pool.wait_ge(S("g_new"), now(k))
                gate(pool)
                pool.indirect_dma_start(out=self.sums, out_offset=bass.IndirectOffsetOnAxis(ap=g_ix[:, 2:3], axis=0),
                                        in_=g_new[:, 0:W], in_offset=None, bounds_check=z.rows - 1,
                                        oob_is_err=False).then_inc(S("g_put"), 16)
                pool.wait_ge(S("g_put"), landed("g_put", k))
                pool.sem_inc(S("g_stored"), 1)
            pool.sem_inc(S("g_all"), 1)

        def vector(self, ve):
            W = self.width
            V = nc.vector
            V.memset(store_a[0][:, 0:NT * W], 0.0).then_inc(S("g_zero"), 1)
            if self.table is None and self.direct is None:
                V.memset(g_rows[:, 0:W], 1.0).then_inc(S("g_zero"), 1)
            ve.wait_ge(S("g_mask"), before(2))
            with ve.Fori(0, z.etiles) as k:
                c = [0]

                def step(ins):
                    c[0] += 1
                    ins.then_inc(S("g_chain"), 1)
                    ve.wait_ge(S("g_chain"), before(k * 6 + c[0]))

                ve.wait_ge(S("g_stored"), before(k))
                ve.wait_ge(S("g_dst"), before(k * 16 + 16))
                ve.wait_ge(S("g_sum"), before(k))
                V.tensor_scalar(g_same[:, :], g_dst[:, :], dst_f[:, bass.ds(k, 1)], None, ALU.is_equal).then_inc(S("g_same"), 1)
                ve.wait_ge(S("g_same"), now(k))
                step(V.tensor_tensor(g_low[:, :], g_same[:, :], g_mask[:, :], ALU.mult))
                step(V.tensor_reduce(g_small[:, 0:1], g_low[:, :], AX.X, ALU.max))
                step(V.tensor_scalar(g_small[:, 1:2], dst_ix[:, bass.ds(k, 1)], 0.0, None, ALU.add))
                step(V.scalar_tensor_tensor(g_small[:, 2:3], g_small[:, 0:1], float(BIG), g_small[:, 1:2], ALU.mult, ALU.add))
                step(V.tensor_scalar(g_ix[:, 0:1], src_ix[:, bass.ds(k, 1)], 0.0, None, ALU.add))
                step(V.tensor_scalar(g_ix[:, 1:2], dst_ix[:, bass.ds(k, 1)], 0.0, None, ALU.add))
                V.tensor_copy(g_ix[:, 2:3], g_small[:, 2:3]).then_inc(S("g_ix"), 1)
                ve.wait_ge(S("g_sum"), now(k))
                ve.wait_ge(S("g_old"), landed("g_old", k))
                V.tensor_tensor(g_new[:, 0:W], ps[0][:, 0:W], g_old[:, 0:W], ALU.add).then_inc(S("g_new"), 1)

        def tensor(self, pe):
            W = self.width
            if self.table is None and self.direct is None:
                pe.wait_ge(S("g_zero"), before(2))
            with pe.Fori(0, z.etiles) as k:
                pe.wait_ge(S("g_same"), now(k))
                pe.wait_ge(S("g_new"), before(k))
                if self.table is not None or self.direct is not None:
                    pe.wait_ge(S("g_rows" if self.direct is None else "g_direct"), landed("g_rows" if self.direct is None else "g_direct", k))
                pe.matmul(ps[0][:, 0:W], g_same[:, :], g_rows[:, 0:W], start=True, stop=True).then_inc(S("g_sum"), 1)

    def pass_over(p):
        if p.table is not None:
            for u in range(2):
                carry(f"rows{u}", 16 * ET * (NB // 2))
            carry("g_rows", 16 * z.etiles)
        for name in ("g_old", "g_put"):
            carry(name, 16 * z.etiles)

    def both_ways(eng, general, windows):
        way = eng.value_load(flag[0:1, 0:1], min_val=0, max_val=1)
        with eng.If(way > 0):
            general()
        with eng.Else():
            windows()

    def bodies(eng, body, by=2):
        n = (NB - 2) // by
        with eng.Fori(0, n) as it:
            for v in range(by):
                body(it * by + v, it * (by // 2) + v // 2, v % 2)
        for m in range(n * by, NB):
            body(m, m // 2, m % 2)

    def exists(m):
        return not isinstance(m, int) or m < NB

    def later(m, i, u):
        return m + 1, i + u, 1 - u

    def gate(pool):
        pool.sem_inc(S("passed"), 1)

    def slot_rows(s, W, pitch):
        return ring[:, s * pitch:s * pitch + W]

    def gather_pool(pool, table, W, pitch, last_sum):
        def block(m, v, i, c):
            if v % 4 == 0:
                pool.wait_ge(S("ix"), landed("ix", c))
            if not isinstance(m, int) or m >= 2:
                pool.wait_ge(S(f"rows{v % 2}"), landed(f"rows{v % 2}", i - 1, ET))
            if not isinstance(m, int) or m >= RB:
                pool.wait_ge(S(last_sum), before(m - 5))
            gate(pool)
            for t in range(ET):
                at = v * ET + t
                pool.indirect_dma_start(
                    out=slot_rows(at, W, pitch), out_offset=None, in_=table,
                    in_offset=bass.IndirectOffsetOnAxis(ap=ix_now[:, at:at + 1], axis=0)).then_inc(S(f"rows{v % 2}"), 16)

        for m in range(min(RB, NB)):
            block(m, m, m // 2, m // 4)
        n = max(NB - RB, 0) // RB
        if n:
            with pool.Fori(1, n + 1) as it:
                for v in range(RB):
                    block(it * RB + v, v, it * (RB // 2) + v // 2, it * 2 + v // 4)
        for m in range((n + 1) * RB, NB):
            block(m, m % RB, m // 2, m // 4)

    def one_hots(ve, m, q):
        V = nc.vector
        V.tensor_tensor(onehot[:, q, :, :, :],
                        iota[:, :].unsqueeze(1).unsqueeze(1).to_broadcast([P, 2, GT, P]),
                        window[:, :, bass.ds(m * NT + q * GT, GT)].unsqueeze(3).to_broadcast([P, 2, GT, P]),
                        ALU.is_equal).then_inc(S(f"hot{q}"), 1)

    def sums(pe, m, tiles, out, W):
        first, n = tiles[0], len(tiles)
        places = [nc.values_load_multi_w_load_instructions(
            slots[0:1, k, bass.ds(m * NT + first, n)], engines=(mybir.EngineType.PE,), min_val=0, max_val=RING - 1,
            skip_runtime_bounds_check_because="the table holds remainders by RING")[1] for k in range(2)]
        for j in tiles:
            for k in range(2):
                last = pe.matmul(out(j), onehot[:, j // GT, k, j % GT, :],
                                 ring[:, bass.ds(places[k][j - first] * W, W)], start=(k == 0), stop=(k == 1))
        return last

    def group(ap, q, W=D):
        return ap[:, q * GT * W:(q + 1) * GT * W]

    def tiles3(ap, W=D):
        return ap.rearrange("p (j w) -> p j w", w=W)

    def per_node(table, m, q):
        return table[:, bass.ds(m * NT + q * GT, GT)].unsqueeze(2).to_broadcast([P, GT, D])

    def row(b, W=D, n=GT):
        return b[:, :].unsqueeze(1).to_broadcast([P, n, W])

    def general_sums(u, W):
        return ring[:, u * NT * H:u * NT * H + NT * W]

    def norm_center(ve, q, m):
        V = nc.vector
        V.tensor_reduce(stat[:, q, 0, :], tiles3(tmp[1][q][:, :]), AX.X, ALU.add).then_inc(S(f"rs{q}"), 1)
        ve.wait_ge(S(f"rs{q}"), now(m))
        V.tensor_scalar(stat[:, q, 1, :], stat[:, q, 0, :], -1.0 / D, None, ALU.mult).then_inc(S(f"nm{q}"), 1)
        ve.wait_ge(S(f"nm{q}"), now(m))
        V.tensor_tensor(tiles3(tmp[0][q][:, :]), tiles3(tmp[1][q][:, :]),
                        stat[:, q, 1, :].unsqueeze(2).to_broadcast([P, GT, D]), ALU.add).then_inc(S(f"xc{q}"), 1)

    def norm_square(act, q, m):
        act.wait_ge(S(f"xc{q}"), now(m))
        act.wait_ge(S(f"vs{q}"), before(m))
        nc.scalar.activation(sq[q][:, :], tmp[0][q][:, :], ACT.Square).then_inc(S(f"sq{q}"), 1)

    def norm_root(act, q, m):
        act.wait_ge(S(f"vs{q}"), now(m))
        nc.scalar.activation(stat[:, q, 3, :], stat[:, q, 2, :], ACT.Sqrt, bias=eps_c[:, :], scale=1.0 / D).then_inc(S(f"sd{q}"), 1)

    def norm_var(ve, q, m):
        ve.wait_ge(S(f"sq{q}"), now(m))
        nc.vector.tensor_reduce(stat[:, q, 2, :], tiles3(sq[q][:, :]), AX.X, ALU.add).then_inc(S(f"vs{q}"), 1)

    def norm_out(ve, q, m, to):
        ve.wait_ge(S(f"sd{q}"), now(m))
        nc.vector.reciprocal(stat[:, q, 2, :], stat[:, q, 3, :]).then_inc(S(f"rstd{q}"), 1)
        ve.wait_ge(S(f"rstd{q}"), now(m))
        nc.vector.tensor_tensor(tiles3(to), tiles3(tmp[0][q][:, :]),
                                stat[:, q, 2, :].unsqueeze(2).to_broadcast([P, GT, D]), ALU.mult).then_inc(S(f"out{q}"), 1)

    class Pass:
        W = D
        pitch = D
        last_sum = "agg1"
        loads, stores, consumed = (), (), ()

        def __init__(self, number, table, general):
            self.number, self.table, self.gen = number, table, general

        def load_block(self, sp, m, u):
            for table, buf, W in self.loads:
                sp.dma_start(buf[u][:, 0:NT * W], block_of(table, m, W)).then_inc(S(f"in{u}"), 16)

        def load_sums(self, sp, m, u):
            sp.dma_start(general_sums(u, self.W), block_of(self.gen.sums, m, self.W)).then_inc(S(f"sums{u}"), 16)

        def load_index(self, sp, c):
            sp.dma_start(ix_now[:, bass.ds((c % 2) * IX, IX)], src_ix[:, bass.ds(c * IX, IX)]).then_inc(S("ix"), 16)

        def sync_rows_first(self, sp):
            self.load_index(sp, 0)

        def sync_rows(self, sp, m, i, u, v):
            if v % 4 == 0 and exists(m + 4):
                c = m // 4 if isinstance(m, int) else self.chunk
                if not isinstance(m, int) or m > 0:
                    sp.wait_ge(S(self.last_sum), before(m))
                sp.wait_ge(S("ix"), landed("ix", c))
                self.load_index(sp, c + 1)

        def sync_loop(self, sp, windows):
            if windows:
                self.sync_rows_first(sp)
            for u in range(2):
                self.load_block(sp, u, u)
                if not windows:
                    self.load_sums(sp, u, u)

            def body(m, i, u, v):
                if windows:
                    self.sync_rows(sp, m, i, u, v)
                if exists(m + 2):
                    for name in self.consumed:
                        sp.wait_ge(S(name), now(m))
                    self.load_block(sp, m + 2, u)
                    if not windows:
                        self.load_sums(sp, m + 2, u)
                for table, buf, W, signals in self.stores:
                    for name in signals:
                        sp.wait_ge(S(name), now(m))
                    sp.dma_start(block_of(table, m, W), buf[u][:, 0:NT * W]).then_inc(S(f"put{u}"), 16)

            n = (NB - 2) // 4
            with sp.Fori(0, n) as it:
                self.chunk = it
                for v in range(4):
                    body(it * 4 + v, it * 2 + v // 2, v % 2, v)
            for m in range(n * 4, NB):
                body(m, m // 2, m % 2, m)
            for u in range(2):
                sp.wait_ge(S(f"put{u}"), before(16 * len(self.stores) * (NB // 2)))

        def inputs_in(self, eng, i, u):
            eng.wait_ge(S(f"in{u}"), landed(f"in{u}", i, len(self.loads)))

        def stored(self, eng, i, u):
            eng.wait_ge(S(f"put{u}"), before(i * 16 * len(self.stores)))

        def sums_here(self, ve, m, i, u, q, windows):
            if windows:
                ve.wait_ge(S(f"agg{q}"), now(m))
                return ps[q][:, 0:GT * D]
            ve.wait_ge(S(f"sums{u}"), landed(f"sums{u}", i))
            return group(general_sums(u, D), q)

        def rows_in(self, pe, i, u):
            pe.wait_ge(S(f"rows{u}"), landed(f"rows{u}", i, ET))

        def collect(self, pe, m, i, u, q):
            if not exists(m):
                return
            if q == 0:
                self.rows_in(pe, i, u)
            pe.wait_ge(S(f"hot{q}"), now(m))
            pe.wait_ge(S(f"mean{q}"), before(m))
            sums(pe, m, range(q * GT, q * GT + GT), lambda j: ps[q][:, (j % GT) * D:(j % GT + 1) * D],
                 D).then_inc(S(f"agg{q}"), 1)

        def hots(self, ve, m, q, windows):
            if windows and exists(m):
                if not isinstance(m, int) or m > 0:
                    ve.wait_ge(S(f"agg{q}"), before(m))
                one_hots(ve, m, q)

        def take(self, ve, m, i, u, q, windows):
            pass

        def vector_loop(self, ve, windows):
            for q in range(2):
                self.hots(ve, 0, q, windows)
            for q in range(2):
                self.take(ve, 0, 0, 0, q, windows)
                self.hots(ve, 1, q, windows)
            bodies(ve, lambda m, i, u: self.vector(ve, m, i, u, windows))

        def scalar_loop(self, act, windows):
            bodies(act, lambda m, i, u: self.scalar(act, m, i, u, windows))

        def tensor_loop(self, pe, windows):
            if windows:
                for q in range(2):
                    self.collect(pe, 0, 0, 0, q)
            bodies(pe, lambda m, i, u: self.tensor(pe, m, i, u, windows))

        def gpsimd_windows(self, pool):
            gather_pool(pool, self.table, self.W, self.pitch, self.last_sum)

        def emit(self):
            other = next_pass(self.number)
            with nc.Block() as block:

                @block.sync
                def _(sp):
                    start_at_one(sp, other)

                    def general():
                        self.gen.sync(sp)
                        sp.wait_ge(S("g_all"), now(0))
                        self.sync_loop(sp, False)

                    both_ways(sp, general, lambda: self.sync_loop(sp, True))

                @block.gpsimd
                def _(pool):
                    both_ways(pool, lambda: self.gen.gpsimd(pool), lambda: self.gpsimd_windows(pool))

                @block.vector
                def _(ve):
                    def general():
                        self.gen.vector(ve)
                        self.vector_loop(ve, False)

                    both_ways(ve, general, lambda: self.vector_loop(ve, True))

                @block.scalar
                def _(act):
                    both_ways(act, lambda: self.scalar_loop(act, False), lambda: self.scalar_loop(act, True))

                @block.tensor
                def _(pe):
                    def general():
                        self.gen.tensor(pe)
                        self.tensor_loop(pe, False)

                    both_ways(pe, general, lambda: self.tensor_loop(pe, True))

            pass_over(self)

    def pair_transposes(pe, src, bank):
        for r in range(GT // 2):
            last = pe.transpose(bank[:, r * P:(r + 1) * P], src[:, r * P:(r + 1) * P], ident[:, :])
        return last

    def pair_products(pe, lhs, w, bank):
        for r in range(GT // 2):
            last = pe.matmul(bank[:, r * P:(r + 1) * P], lhs[:, r * P:(r + 1) * P], w[:, :], start=True, stop=True)
        return last

    class Sage2(Pass):
        loads = ((s2_t, load_a, D), (a["x_rows"], load_b, D))
        stores = ((x1_t, store_a, D, ("out0", "out1")), (y1_t, store_b, D, ("y0", "y1")))
        consumed = ("pre0", "pre1")

        def take(self, ve, m, i, u, q, windows):
            V = nc.vector
            if not exists(m):
                return
            agg = self.sums_here(ve, m, i, u, q, windows)
            ve.wait_ge(S(f"out{q}"), before(m))
            V.tensor_tensor(tiles3(tmp[0][q][:, :]), tiles3(agg), per_node(invdeg, m, q), ALU.mult).then_inc(S(f"mean{q}"), 1)
            self.inputs_in(ve, i, u)
            ve.wait_ge(S(f"mean{q}"), now(m))
            V.tensor_tensor(tmp[1][q][:, :], tmp[0][q][:, :], group(load_a[u], q), ALU.add).then_inc(S(f"sum{q}"), 1)
            ve.wait_ge(S(f"sum{q}"), now(m))
            V.scalar_tensor_tensor(tmp[1][q][:, :], tmp[1][q][:, :], 0.0, group(load_b[u], q), ALU.max, ALU.add).then_inc(S(f"pre{q}"), 1)
            ve.wait_ge(S(f"pre{q}"), now(m))
            norm_center(ve, q, m)

        def vector(self, ve, m, i, u, windows):
            V = nc.vector
            for q in range(2):
                if q == 0:
                    self.stored(ve, i, u)
                norm_var(ve, q, m)
                norm_out(ve, q, m, group(store_a[u], q))
                self.take(ve, *later(m, i, u), q, windows)
                self.hots(ve, m + 2, q, windows)
            for q in range(2):
                ve.wait_ge(S(f"mm{q}"), now(m))
                V.tensor_tensor(tiles3(group(store_b[u], q)), tiles3(ps[4 + q]), per_node(dis, m, q), ALU.mult).then_inc(S(f"y{q}"), 1)

        def scalar_loop(self, act, windows):
            for q in range(2):
                norm_square(act, q, 0)
            super().scalar_loop(act, windows)

        def scalar(self, act, m, i, u, windows):
            for q in range(2):
                norm_root(act, q, m)
                if exists(m + 1):
                    norm_square(act, q, m + 1)
            for q in range(2):
                act.wait_ge(S(f"tr{q}"), now(m))
                nc.scalar.activation(tp[q][:, :], ps[2 + q], ACT.Copy).then_inc(S(f"ev{q}"), 1)

        def tensor(self, pe, m, i, u, windows):
            for q in range(2):
                if windows:
                    self.collect(pe, *later(m, i, u), q)
                pe.wait_ge(S(f"out{q}"), now(m))
                pe.wait_ge(S(f"ev{q}"), before(m))
                pair_transposes(pe, group(store_a[u], q), ps[2 + q]).then_inc(S(f"tr{q}"), 1)
            for q in range(2):
                pe.wait_ge(S(f"ev{q}"), now(m))
                pe.wait_ge(S(f"y{q}"), before(m))
                pair_products(pe, tp[q], wg1, ps[4 + q]).then_inc(S(f"mm{q}"), 1)

    class Gcn1(Pass):
        loads = ((y1_t, load_b, D),)
        stores = ((y2_t, store_b, D, ("y0", "y1")),)
        consumed = ("mean0", "mean1")

        def take(self, ve, m, i, u, q, windows):
            V = nc.vector
            if not exists(m):
                return
            self.inputs_in(ve, i, u)
            agg = self.sums_here(ve, m, i, u, q, windows)
            ve.wait_ge(S(f"pre{q}"), before(m))
            V.tensor_tensor(tmp[0][q][:, :], agg, group(load_b[u], q), ALU.add).then_inc(S(f"mean{q}"), 1)
            ve.wait_ge(S(f"mean{q}"), now(m))
            ve.wait_ge(S(f"tr{q}"), before(m))
            V.tensor_tensor(tiles3(tmp[1][q][:, :]), tiles3(tmp[0][q][:, :]), per_node(dis, m, q), ALU.mult).then_inc(S(f"pre{q}"), 1)

        def vector(self, ve, m, i, u, windows):
            V = nc.vector
            for q in range(2):
                self.take(ve, *later(m, i, u), q, windows)
                self.hots(ve, m + 2, q, windows)
            self.stored(ve, i, u)
            for q in range(2):
                ve.wait_ge(S(f"mm{q}"), now(m))
                V.tensor_tensor(tiles3(group(store_b[u], q)), tiles3(ps[4 + q]), per_node(dis, m, q), ALU.mult).then_inc(S(f"y{q}"), 1)

        def scalar(self, act, m, i, u, windows):
            for q in range(2):
                act.wait_ge(S(f"tr{q}"), now(m))
                act.wait_ge(S(f"mm{q}"), before(m))
                nc.scalar.activation(tp[q][:, :], ps[2 + q], ACT.Relu, bias=bg1c[:, :]).then_inc(S(f"ev{q}"), 1)

        def tensor(self, pe, m, i, u, windows):
            for q in range(2):
                pe.wait_ge(S(f"pre{q}"), now(m))
                pe.wait_ge(S(f"ev{q}"), before(m))
                pair_transposes(pe, tmp[1][q], ps[2 + q]).then_inc(S(f"tr{q}"), 1)
                if windows:
                    self.collect(pe, *later(m, i, u), q)
            for q in range(2):
                pe.wait_ge(S(f"ev{q}"), now(m))
                pe.wait_ge(S(f"y{q}"), before(m))
                pair_products(pe, tp[q], wg2, ps[4 + q]).then_inc(S(f"mm{q}"), 1)

    class Gcn2(Pass):
        loads = ((y2_t, load_a, D), (x1_t, load_b, D))
        stores = ((x2_t, store_a, D, ("out0", "out1")),)
        consumed = ("mean0", "mean1", "sum0", "sum1")

        def take(self, ve, m, i, u, q, windows):
            V = nc.vector
            if not exists(m):
                return
            self.inputs_in(ve, i, u)
            agg = self.sums_here(ve, m, i, u, q, windows)
            ve.wait_ge(S(f"out{q}"), before(m))
            V.tensor_tensor(tmp[0][q][:, :], agg, group(load_a[u], q), ALU.add).then_inc(S(f"mean{q}"), 1)
            ve.wait_ge(S(f"mean{q}"), now(m))
            V.tensor_tensor(tiles3(tmp[1][q][:, :]), tiles3(tmp[0][q][:, :]), per_node(dis, m, q), ALU.mult).then_inc(S(f"scaled{q}"), 1)
            ve.wait_ge(S(f"scaled{q}"), now(m))
            V.tensor_tensor(tmp[0][q][:, :], tmp[1][q][:, :], group(load_b[u], q), ALU.add).then_inc(S(f"sum{q}"), 1)
            ve.wait_ge(S(f"sum{q}"), now(m))
            V.tensor_tensor(tiles3(tmp[1][q][:, :]), tiles3(tmp[0][q][:, :]), row(bg2r), ALU.add).then_inc(S(f"pre{q}"), 1)
            ve.wait_ge(S(f"pre{q}"), now(m))
            norm_center(ve, q, m)

        def vector(self, ve, m, i, u, windows):
            for q in range(2):
                if q == 0:
                    self.stored(ve, i, u)
                norm_var(ve, q, m)
                norm_out(ve, q, m, group(store_a[u], q))
                self.take(ve, *later(m, i, u), q, windows)
                self.hots(ve, m + 2, q, windows)

        def scalar_loop(self, act, windows):
            for q in range(2):
                norm_square(act, q, 0)
            super().scalar_loop(act, windows)

        def scalar(self, act, m, i, u, windows):
            for q in range(2):
                norm_root(act, q, m)
                if exists(m + 1):
                    norm_square(act, q, m + 1)

        def tensor(self, pe, m, i, u, windows):
            if windows:
                for q in range(2):
                    self.collect(pe, *later(m, i, u), q)

    class Gin(Pass):
        loads = ((x2_t, load_b, D),)
        stores = ((x3_t, store_a, D, ("out0", "out1")),)
        consumed = ("pre0", "pre1")

        def take(self, ve, m, i, u, q, windows):
            if not exists(m):
                return
            self.inputs_in(ve, i, u)
            agg = self.sums_here(ve, m, i, u, q, windows)
            ve.wait_ge(S(f"tr{q}"), before(m))
            nc.vector.tensor_tensor(load_a[q][:, 0:GT * D], agg, group(load_b[u], q), ALU.add).then_inc(S(f"mean{q}"), 1)

        def vector(self, ve, m, i, u, windows):
            V = nc.vector
            for q in range(2):
                ve.wait_ge(S(f"mm{q}"), now(m))
                ve.wait_ge(S(f"out{q}"), before(m))
                V.tensor_tensor(tiles3(tmp[0][q][:, :]), tiles3(ps[6 + q]), row(bi2r), ALU.add).then_inc(S(f"sum{q}"), 1)
            for q in range(2):
                ve.wait_ge(S(f"last{q}"), now(m))
                V.scalar_tensor_tensor(tmp[1][q][:, :], group(load_b[u], q), 2.0, tmp[1][q][:, :], ALU.mult, ALU.add).then_inc(S(f"pre{q}"), 1)
            for q in range(2):
                ve.wait_ge(S(f"pre{q}"), now(m))
                norm_center(ve, q, m)
            self.stored(ve, i, u)
            for q in range(2):
                self.take(ve, *later(m, i, u), q, windows)
                self.hots(ve, m + 2, q, windows)
                norm_var(ve, q, m)
                norm_out(ve, q, m, group(store_a[u], q))

        def scalar(self, act, m, i, u, windows):
            for q in range(2):
                act.wait_ge(S(f"tr{q}"), now(m))
                nc.scalar.activation(tp[q][:, :], ps[2 + q], ACT.Copy).then_inc(S(f"ev{q}"), 1)
            for q in range(2):
                act.wait_ge(S(f"hid{q}"), now(m))
                nc.scalar.activation(tq[q][:, :], ps[4 + q], ACT.Relu, bias=bi1c[:, :]).then_inc(S(f"relu{q}"), 1)
            for q in range(2):
                act.wait_ge(S(f"sum{q}"), now(m))
                nc.scalar.activation(tmp[1][q][:, :], tmp[0][q][:, :], ACT.Relu).then_inc(S(f"last{q}"), 1)
            for q in range(2):
                norm_square(act, q, m)
            for q in range(2):
                norm_root(act, q, m)

        def tensor(self, pe, m, i, u, windows):
            for q in range(2):
                pe.wait_ge(S(f"mean{q}"), now(m))
                pe.wait_ge(S(f"ev{q}"), before(m))
                pair_transposes(pe, load_a[q], ps[2 + q]).then_inc(S(f"tr{q}"), 1)
            for q in range(2):
                pe.wait_ge(S(f"ev{q}"), now(m))
                pe.wait_ge(S(f"relu{q}"), before(m))
                pe.matmul(ps[4 + q], wi1[:, :], tp[q][:, :], start=True, stop=True).then_inc(S(f"hid{q}"), 1)
            for q in range(2):
                pe.wait_ge(S(f"relu{q}"), now(m))
                pe.wait_ge(S(f"sum{q}"), before(m))
                pair_products(pe, tq[q], wi2, ps[6 + q]).then_inc(S(f"mm{q}"), 1)
            if windows:
                for q in range(2):
                    self.collect(pe, *later(m, i, u), q)

    CT = 4

    def tile_transposes(pe, src, bank):
        for r in range(CT):
            last = pe.transpose(bank[:, r * P:(r + 1) * P], src[:, r * P:(r + 1) * P], ident[:, :])
        return last

    def tile_products(pe, lhs, w, bank):
        for r in range(CT):
            last = pe.matmul(bank[:, r * P:(r + 1) * P], lhs[:, r * P:(r + 1) * P], w, start=True, stop=True)
        return last

    class Chunks(Pass):
        last_sum = "agg3"

        def collect_chunk(self, pe, m, i, u, c):
            if not exists(m):
                return
            if c == 0:
                self.rows_in(pe, i, u)
            if c % 2 == 0:
                pe.wait_ge(S(f"hot{c // 2}"), now(m))
            pe.wait_ge(S(f"mean{c}"), before(m))
            W = self.pitch
            sums(pe, m, range(c * CT, c * CT + CT), lambda j: ps[c][:, (j % CT) * W:(j % CT + 1) * W],
                 W).then_inc(S(f"agg{c}"), 1)

        def collect(self, pe, m, i, u, q):
            for c in (2 * q, 2 * q + 1):
                self.collect_chunk(pe, m, i, u, c)

        def hots(self, ve, m, q, windows):
            if windows and exists(m):
                if not isinstance(m, int) or m > 0:
                    ve.wait_ge(S(f"agg{2 * q + 1}"), before(m))
                one_hots(ve, m, q)

    class Sage0(Chunks):
        pitch = D + 1
        loads = (None,)
        stores = ((s1_t, store_a, H, ("s13",)), (n1_t, store_b, H, ("n13",)))
        consumed = ("hid3",)

        def load_block(self, sp, m, u):
            sp.dma_start(load_a[u][0:D, :], a["x_cols"][:, bass.ds(m * BN, BN)]).then_inc(S(f"in{u}"), 16)

        def take(self, ve, m, i, u, q, windows):
            if not exists(m):
                return
            V = nc.vector
            for c in (2 * q, 2 * q + 1):
                cols = lambda t: t[:, bass.ds(m * NT + c * CT, CT)]
                if windows:
                    ve.wait_ge(S(f"agg{c}"), now(m))
                    agg = tiles3(ps[c][:, 0:CT * (D + 1)], D + 1)
                    V.tensor_scalar(cols(deg).unsqueeze(2), agg[:, :, D:D + 1], 0.0, None, ALU.add).then_inc(S(f"deg{q}"), 1)
                    ve.wait_ge(S(f"deg{q}"), before(m * 2 + (c % 2 + 1)))
                    agg = agg[:, :, 0:D]
                else:
                    ve.wait_ge(S(f"sums{u}"), landed(f"sums{u}", i))
                    agg = tiles3(general_sums(u, D)[:, c * CT * D:(c + 1) * CT * D])
                V.tensor_scalar(stat[:, q, 0, 0:CT], cols(deg), 1.0, None, ALU.max).then_inc(S(f"least{q}"), 1)
                ve.wait_ge(S(f"least{q}"), before(m * 2 + (c % 2 + 1)))
                V.reciprocal(cols(invdeg), stat[:, q, 0, 0:CT]).then_inc(S(f"inv{q}"), 1)
                ve.wait_ge(S(f"inv{q}"), before(m * 2 + (c % 2 + 1)))
                ve.wait_ge(S(f"tr{c}"), before(m))
                V.tensor_tensor(tiles3(load_b[q][:, (c % 2) * CT * P:(c % 2 + 1) * CT * P], P)[:, :, D:P], agg,
                                cols(invdeg).unsqueeze(2).to_broadcast([P, CT, D]), ALU.mult).then_inc(S(f"mean{c}"), 1)

        def vector_loop(self, ve, windows):
            for q in range(2):
                nc.vector.memset(load_b[q][:, :], 0.0).then_inc(S("zeros"), 1)
            if windows:
                nc.vector.memset(tiles3(ring[:, 0:RING * (D + 1)], D + 1)[:, :, D:D + 1], 1.0).then_inc(S("zeros"), 1)
            ve.wait_ge(S("zeros"), before(3 if windows else 2))
            super().vector_loop(ve, windows)

        def vector(self, ve, m, i, u, windows):
            V = nc.vector

            def own(c):
                ve.wait_ge(S(f"nmm{c}"), now(m))
                V.tensor_tensor(tiles3(store_a[u][:, c * 512:(c + 1) * 512], H), tiles3(ps[7], H), row(b1r, H, CT), ALU.add).then_inc(S(f"s1{c}"), 1)

            self.stored(ve, i, u)
            for q in range(2):
                own(2 * q)
                own(2 * q + 1)
                self.take(ve, *later(m, i, u), q, windows)
                self.hots(ve, m + 2, q, windows)

        def scalar(self, act, m, i, u, windows):
            A = nc.scalar
            self.stored(act, i, u)

            def evacuate(c):
                act.wait_ge(S(f"tr{c}"), now(m))
                A.activation(load_a[u][D:P, c * 512:(c + 1) * 512], ps[4][D:P, :], ACT.Copy).then_inc(S(f"ev{c}"), 1)

            def hidden(c):
                act.wait_ge(S(f"hid{c}"), now(m))
                act.wait_ge(S(f"nmm{(c + 2) % 4}"), now(m) if c >= 2 else before(m))
                A.activation(tp[c % 2][:, :], ps[5], ACT.Relu, bias=b0c[:, :]).then_inc(S(f"rel{c}"), 1)

            def neighbours(c):
                act.wait_ge(S(f"nmm{c}"), now(m))
                A.activation(store_b[u][:, c * 512:(c + 1) * 512], ps[6], ACT.Copy).then_inc(S(f"n1{c}"), 1)

            evacuate(0)
            for c in range(4):
                if c < 3:
                    evacuate(c + 1)
                hidden(c)
                if c >= 1:
                    neighbours(c - 1)
            neighbours(3)

        def tensor(self, pe, m, i, u, windows):
            def former(name, c):
                pe.wait_ge(S(f"{name}{(c + 3) % 4}"), now(m) if c else before(m))

            def turn(c):
                pe.wait_ge(S(f"mean{c}"), now(m))
                former("ev", c)
                tile_transposes(pe, load_b[c // 2][:, (c % 2) * 512:(c % 2 + 1) * 512], ps[4]).then_inc(S(f"tr{c}"), 1)

            def hidden(c):
                pe.wait_ge(S(f"ev{c}"), now(m))
                former("rel", c)
                pe.matmul(ps[5], w0[:, :], load_a[u][:, c * 512:(c + 1) * 512], start=True, stop=True).then_inc(S(f"hid{c}"), 1)

            def products(c):
                pe.wait_ge(S(f"rel{c}"), now(m))
                former("n1", c)
                tile_products(pe, tp[c % 2], w1[:, 0:H], ps[6])
                former("s1", c)
                tile_products(pe, tp[c % 2], w1[:, H:2 * H], ps[7]).then_inc(S(f"nmm{c}"), 1)

            turn(0)
            self.inputs_in(pe, i, u)
            turn(1)
            hidden(0)
            turn(2)
            hidden(1)
            products(0)
            turn(3)
            hidden(2)
            products(1)
            if windows:
                self.collect(pe, *later(m, i, u), 0)
            hidden(3)
            products(2)
            if windows:
                self.collect_chunk(pe, *later(m, i, u), 2)
            products(3)
            if windows:
                self.collect_chunk(pe, *later(m, i, u), 3)

    class Sage1(Chunks):
        W = H
        pitch = H
        loads = ((s1_t, load_a, H),)
        stores = ((s2_t, store_a, D, ("s23",)), (n2_t, store_b, D, ("n23",)))
        consumed = ("mean3",)

        def take(self, ve, m, i, u, q, windows):
            if not exists(m):
                return
            self.inputs_in(ve, i, u)
            for c in (2 * q, 2 * q + 1):
                if windows:
                    ve.wait_ge(S(f"agg{c}"), now(m))
                    agg = ps[c]
                else:
                    ve.wait_ge(S(f"sums{u}"), landed(f"sums{u}", i))
                    agg = general_sums(u, H)[:, c * 512:(c + 1) * 512]
                ve.wait_ge(S(f"tr{c}"), before(m))
                for r in range(CT):
                    last = nc.vector.scalar_tensor_tensor(
                        tmp[c % 2][q][:, r * P:(r + 1) * P], agg[:, r * P:(r + 1) * P],
                        invdeg[:, bass.ds(m * NT + c * CT + r, 1)], load_a[u][:, (c * CT + r) * P:(c * CT + r + 1) * P],
                        ALU.mult, ALU.add)
                last.then_inc(S(f"mean{c}"), 1)

        def vector(self, ve, m, i, u, windows):
            self.stored(ve, i, u)
            for q in range(2):
                self.take(ve, *later(m, i, u), q, windows)
                self.hots(ve, m + 2, q, windows)
                for c in (2 * q, 2 * q + 1):
                    ve.wait_ge(S(f"mm{c}"), now(m))
                    nc.vector.tensor_tensor(tiles3(store_a[u][:, c * 256:(c + 1) * 256]), tiles3(ps[6 + c % 2], H)[:, :, 0:D],
                                            row(b2r, D, CT), ALU.add).then_inc(S(f"s2{c}"), 1)

        def scalar(self, act, m, i, u, windows):
            A = nc.scalar
            self.stored(act, i, u)

            def hidden(c):
                act.wait_ge(S(f"tr{c}"), now(m))
                act.wait_ge(S(f"mm{c}"), before(m))
                A.activation((tp, tq)[c // 2][c % 2][:, :], ps[4 + c % 2], ACT.Relu).then_inc(S(f"rel{c}"), 1)

            def neighbours(c):
                act.wait_ge(S(f"s2{c}"), now(m))
                A.activation(tiles3(store_b[u][:, c * 256:(c + 1) * 256]), tiles3(ps[6 + c % 2], H)[:, :, D:H], ACT.Copy).then_inc(S(f"n2{c}"), 1)

            hidden(0)
            hidden(1)
            neighbours(0)
            neighbours(1)
            hidden(2)
            hidden(3)
            neighbours(2)
            neighbours(3)

        def tensor(self, pe, m, i, u, windows):
            def former(name, c):
                pe.wait_ge(S(f"{name}{(c + 2) % 4}"), now(m) if c >= 2 else before(m))

            for q in range(2):
                for c in (2 * q, 2 * q + 1):
                    pe.wait_ge(S(f"mean{c}"), now(m))
                    former("rel", c)
                    tile_transposes(pe, tmp[c % 2][q], ps[4 + c % 2]).then_inc(S(f"tr{c}"), 1)
                if windows:
                    self.collect(pe, *later(m, i, u), q)
                for c in (2 * q, 2 * q + 1):
                    pe.wait_ge(S(f"rel{c}"), now(m))
                    former("n2", c)
                    tile_products(pe, (tp, tq)[c // 2][c % 2], w2[:, :], ps[6 + c % 2]).then_inc(S(f"mm{c}"), 1)

    class Messages(Pass):

        def emit(self):
            other = next_pass(self.number)
            gathered = store_a
            with nc.Block() as block:

                @block.sync
                def _(sp):
                    start_at_one(sp, other)

                    def index(c):
                        for buf, ix in ((ix_now, src_ix), (ix_dst, dst_ix)):
                            sp.dma_start(buf[:, bass.ds((c % 2) * IX, IX)], ix[:, bass.ds(c * IX, IX)]).then_inc(S("ix"), 16)

                    def edges(m, u):
                        sp.dma_start(load_a[u][0:DE, 0:ET * P], a["edge_cols"][:, bass.ds(m * ET * P, ET * P)]).then_inc(S(f"in{u}"), 16)

                    index(0)
                    sp.wait_ge(S("zeros"), now(1))
                    for u in range(2):
                        edges(u, u)

                    def body(m, i, u, v, c):
                        if v % 4 == 0 and exists(m + 4):
                            sp.wait_ge(S("tr1"), before(m))
                            sp.wait_ge(S("ix"), landed("ix", c, 2))
                            index(c + 1)
                        if exists(m + 2):
                            sp.wait_ge(S("hid1"), now(m))
                            edges(m + 2, u)
                        sp.wait_ge(S("msg1"), now(m))
                        sp.dma_start(msg_t[bass.ds(m * ET * P, ET * P), :].rearrange("(p t) f -> p (t f)", p=P),
                                     store_b[u][:, 0:ET * D]).then_inc(S(f"put{u}"), 16)

                    n = (NB - 2) // 4
                    with sp.Fori(0, n) as it:
                        for v in range(4):
                            body(it * 4 + v, it * 2 + v // 2, v % 2, v, it)
                    for m in range(n * 4, NB):
                        body(m, m // 2, m % 2, m, m // 4)
                    for u in range(2):
                        sp.wait_ge(S(f"put{u}"), before(16 * (NB // 2)))

                @block.gpsimd
                def _(pool):
                    def body(m, v, c):
                        if v % 4 == 0:
                            pool.wait_ge(S("ix"), landed("ix", c, 2))
                        for h in range(2):
                            pool.wait_ge(S(f"tr{h}"), before(m))
                            gate(pool)
                            for t in range(HT):
                                for k, ix in enumerate((ix_now, ix_dst)):
                                    to, at = t * P + k * D, v * ET + h * HT + t
                                    pool.indirect_dma_start(
                                        out=gathered[h][:, to:to + D], out_offset=None, in_=x3_t,
                                        in_offset=bass.IndirectOffsetOnAxis(ap=ix[:, at:at + 1], axis=0)).then_inc(S(f"pair{h}"), 16)

                    if NB >= RB:
                        with pool.Fori(0, NB // RB) as it:
                            for v in range(RB):
                                body(it * RB + v, v, it * 2 + v // 4)
                    for m in range(NB // RB * RB, NB):
                        body(m, m % RB, m // 4)

                @block.vector
                def _(ve):
                    for u in range(2):
                        nc.vector.memset(load_a[u][:, :], 0.0).then_inc(S("zeros"), 1)

                    def body(m, i, u):
                        ve.wait_ge(S(f"put{u}"), before(i * 16))
                        for h in range(2):
                            ve.wait_ge(S(f"mm{h}"), now(m))
                            nc.vector.tensor_tensor(tiles3(store_b[u][:, h * HT * D:(h + 1) * HT * D]),
                                                    tiles3(ps[4 + h], P)[:, :, 0:D], row(bm2r, D, HT), ALU.add).then_inc(S(f"msg{h}"), 1)

                    bodies(ve, body)

                @block.scalar
                def _(act):
                    def body(m, i, u):
                        for h in range(2):
                            act.wait_ge(S(f"tr{h}"), now(m))
                            nc.scalar.activation(tp[h][:, :], ps[h], ACT.Copy).then_inc(S(f"ev{h}"), 1)
                        for h in range(2):
                            act.wait_ge(S(f"hid{h}"), now(m))
                            nc.scalar.activation(tq[h][:, :], ps[2 + h], ACT.Relu, bias=bm1c[:, :]).then_inc(S(f"rel{h}"), 1)

                    bodies(act, body)

                @block.tensor
                def _(pe):
                    def body(m, i, u):
                        for h in range(2):
                            pe.wait_ge(S(f"pair{h}"), landed(f"pair{h}", m, 2 * HT))
                            pe.wait_ge(S(f"ev{h}"), before(m))
                            tile_transposes(pe, gathered[h], ps[h]).then_inc(S(f"tr{h}"), 1)
                        pe.wait_ge(S(f"in{u}"), landed(f"in{u}", i))
                        for h in range(2):
                            pe.wait_ge(S(f"ev{h}"), now(m))
                            pe.wait_ge(S(f"rel{h}"), before(m))
                            pe.matmul(ps[2 + h], wm1[:, :], tp[h][:, :], start=True, stop=False)
                            pe.matmul(ps[2 + h], wm1e[:, :], load_a[u][:, h * 512:(h + 1) * 512], start=False, stop=True).then_inc(S(f"hid{h}"), 1)
                        for h in range(2):
                            pe.wait_ge(S(f"rel{h}"), now(m))
                            pe.wait_ge(S(f"msg{h}"), before(m))
                            tile_products(pe, tq[h], wm2[:, :], ps[4 + h]).then_inc(S(f"mm{h}"), 1)

                    bodies(pe, body)

    class Update(Pass):
        loads = ((x3_t, load_b, D),)
        stores = ((out, store_a, D, ("out0", "out1")),)
        consumed = ("pre0", "pre1")

        def row_loads(self, sp, m, u):
            sp.dma_start(ring[:, bass.ds((m % RB) * (ET * D), ET * D)],
                         msg_t[bass.ds(m * ET * P, ET * P), :].rearrange("(p t) f -> p (t f)", p=P)).then_inc(S(f"edges{u}"), 16)

        def sync_rows_first(self, sp):
            for u in range(2):
                self.row_loads(sp, u, u)

        def sync_rows(self, sp, m, i, u, v):
            if exists(m + 2):
                sp.wait_ge(S("agg1"), now(m))
                self.row_loads(sp, m + 2, u)

        def rows_in(self, pe, i, u):
            pe.wait_ge(S(f"edges{u}"), landed(f"edges{u}", i))

        def gpsimd_windows(self, pool):
            pass

        def take(self, ve, m, i, u, q, windows):
            if not exists(m):
                return
            agg = self.sums_here(ve, m, i, u, q, windows)
            for s in range(2):
                ve.wait_ge(S(f"tr{q}{s}"), before(m))
            nc.vector.tensor_copy(tiles3(load_a[q][:, 0:GT * P], P)[:, :, D:P], tiles3(agg)).then_inc(S(f"mean{q}"), 1)

        def vector(self, ve, m, i, u, windows):
            V = nc.vector
            self.inputs_in(ve, i, u)
            for q in range(2):
                ve.wait_ge(S(f"out{q}"), before(m))
                for s in range(2):
                    ve.wait_ge(S(f"mm{q}{s}"), now(m))
                    V.tensor_tensor(tiles3(tmp[0][q][:, s * 256:(s + 1) * 256]),
                                    tiles3(ps[6 + s], P)[:, :, 0:D], row(bu2r, D, CT), ALU.add).then_inc(S(f"sum{q}{s}"), 1)
                ve.wait_ge(S(f"sum{q}1"), now(m))
                ve.wait_ge(S(f"xc{q}"), before(m))
                V.tensor_tensor(tmp[1][q][:, :], tmp[0][q][:, :], group(load_b[u], q), ALU.add).then_inc(S(f"pre{q}"), 1)
                ve.wait_ge(S(f"pre{q}"), now(m))
                norm_center(ve, q, m)
                self.take(ve, *later(m, i, u), q, windows)
                self.hots(ve, m + 2, q, windows)
            self.stored(ve, i, u)
            for q in range(2):
                norm_var(ve, q, m)
                norm_out(ve, q, m, group(store_a[u], q))

        def scalar(self, act, m, i, u, windows):
            A = nc.scalar
            self.inputs_in(act, i, u)
            for q in range(2):
                for s in range(2):
                    act.wait_ge(S(f"tr{q}{s}"), before(m))
                A.activation(tiles3(load_a[q][:, 0:GT * P], P)[:, :, 0:D], tiles3(group(load_b[u], q)), ACT.Copy).then_inc(S(f"own{q}"), 1)

            def turned(c):
                s, q = c % 2, c // 2
                act.wait_ge(S(f"tr{q}{s}"), now(m))
                act.wait_ge(S(f"hid{1 - q}{s}"), now(m) if q else before(m))
                A.activation(tp[s][:, :], ps[2 + s], ACT.Copy).then_inc(S(f"ev{q}{s}"), 1)

            def hidden(c):
                s, q = c % 2, c // 2
                act.wait_ge(S(f"hid{q}{s}"), now(m))
                act.wait_ge(S(f"mm{1 - q}{s}"), now(m) if q else before(m))
                A.activation(store_b[s][:, 0:512], ps[4 + s], ACT.Relu, bias=bu1c[:, :]).then_inc(S(f"rel{q}{s}"), 1)

            turned(0)
            for c in range(4):
                if c < 3:
                    turned(c + 1)
                hidden(c)
            for q in range(2):
                norm_square(act, q, m)
            for q in range(2):
                norm_root(act, q, m)

        def tensor(self, pe, m, i, u, windows):
            def former(name, q, s):
                pe.wait_ge(S(f"{name}{1 - q}{s}"), now(m) if q else before(m))

            def turn(c):
                s, q = c % 2, c // 2
                pe.wait_ge(S(f"mean{q}"), now(m))
                pe.wait_ge(S(f"own{q}"), now(m))
                former("ev", q, s)
                tile_transposes(pe, load_a[q][:, s * 512:(s + 1) * 512], ps[2 + s]).then_inc(S(f"tr{q}{s}"), 1)

            def hidden(c):
                s, q = c % 2, c // 2
                pe.wait_ge(S(f"ev{q}{s}"), now(m))
                former("rel", q, s)
                pe.matmul(ps[4 + s], wu1[:, :], tp[s][:, :], start=True, stop=True).then_inc(S(f"hid{q}{s}"), 1)

            def products(c):
                s, q = c % 2, c // 2
                pe.wait_ge(S(f"rel{q}{s}"), now(m))
                former("sum", q, s)
                tile_products(pe, store_b[s], wu2[:, :], ps[6 + s]).then_inc(S(f"mm{q}{s}"), 1)

            turn(0)
            turn(1)
            hidden(0)
            turn(2)
            hidden(1)
            products(0)
            turn(3)
            hidden(2)
            products(1)
            if windows:
                self.collect(pe, *later(m, i, u), 0)
            hidden(3)
            products(2)
            products(3)
            if windows:
                self.collect(pe, *later(m, i, u), 1)

    def roots(number):
        other = next_pass(number)
        T = z.tiles
        above, root, quot = store_a[0][:, 0:T], store_a[1][:, 0:T], store_b[0][:, 0:T]
        with nc.Block() as block:

            @block.sync
            def _(sp):
                start_at_one(sp, other)

            @block.scalar
            def _(act):
                act.wait_ge(S("above"), now(0))
                nc.scalar.activation(root, above, ACT.Sqrt).then_inc(S("root"), 1)

            @block.vector
            def _(ve):
                V = nc.vector
                V.tensor_scalar(above, deg[:, :], 1.0, None, ALU.add).then_inc(S("above"), 1)
                ve.wait_ge(S("root"), now(0))
                V.reciprocal(quot, root).then_inc(S("inverse"), 1)
                ve.wait_ge(S("inverse"), now(0))
                V.tensor_tensor(quot, quot, above, ALU.mult).then_inc(S("quotient"), 1)
                ve.wait_ge(S("quotient"), now(0))
                V.tensor_tensor(quot, quot, root, ALU.add).then_inc(S("twice"), 1)
                ve.wait_ge(S("twice"), now(0))
                V.reciprocal(above, quot).then_inc(S("half"), 1)
                ve.wait_ge(S("half"), now(0))
                V.tensor_scalar(dis[:, :], above, 2.0, None, ALU.mult).then_inc(S("dis"), 1)
                ve.wait_ge(S("dis"), now(0))

    class Degrees(Pass):
        loads = ()
        stores = ()

        def emit(self):
            other = next_pass(self.number)
            with nc.Block() as block:

                @block.sync
                def _(sp):
                    start_at_one(sp, other)

                    def general():
                        self.gen.sync(sp)
                        sp.wait_ge(S("g_all"), now(0))
                        with sp.Fori(0, NB) as m:
                            sp.wait_ge(S("deg"), before(m))
                            self.load_sums(sp, m, 0)
                        sp.wait_ge(S("deg"), now(NB - 1))

                    both_ways(sp, general, lambda: None)

                @block.gpsimd
                def _(pool):
                    both_ways(pool, lambda: self.gen.gpsimd(pool), lambda: None)

                @block.vector
                def _(ve):
                    def general():
                        self.gen.vector(ve)
                        with ve.Fori(0, NB) as m:
                            ve.wait_ge(S("sums0"), landed("sums0", m))
                            nc.vector.tensor_scalar(deg[:, bass.ds(m * NT, NT)], tiles3(general_sums(0, D))[:, :, 0], 0.0, None, ALU.add).then_inc(S("deg"), 1)

                    both_ways(ve, general, lambda: None)

                @block.tensor
                def _(pe):
                    both_ways(pe, lambda: self.gen.tensor(pe), lambda: None)

            pass_over(self)

    with ctx:
        setup()
        Degrees(1, None, General(sums_t, D)).emit()
        Sage0(2, a["x_rows"], General(sums_t, D, table=a["x_rows"])).emit()
        roots(3)
        Sage1(4, n1_t, General(sums2_t, H, table=n1_t)).emit()
        Sage2(5, n2_t, General(sums_t, D, table=n2_t)).emit()
        Gcn1(6, y1_t, General(sums_t, D, table=y1_t)).emit()
        Gcn2(7, y2_t, General(sums_t, D, table=y2_t)).emit()
        Gin(8, x2_t, General(sums_t, D, table=x2_t)).emit()
        Messages(9, x3_t, None).emit()
        Update(10, None, General(sums_t, D, direct=msg_t)).emit()


OUT_ROWS = (100000, D)
WEIGHTS = ["L0_gnn_ws0", "L0_gnn_wn0", "L0_gnn_b0", "L0_gnn_ws1", "L0_gnn_wn1", "L0_gnn_b1", "L0_gnn_ws2", "L0_gnn_wn2",
           "L0_gnn_b2", "L1_gnn_W1", "L1_gnn_b1", "L1_gnn_W2", "L1_gnn_b2", "L2_gnn_W1", "L2_gnn_b1", "L2_gnn_W2", "L2_gnn_b2",
           "L3_gnn_mW1", "L3_gnn_mb1", "L3_gnn_mW2", "L3_gnn_mb2", "L3_gnn_uW1", "L3_gnn_ub1", "L3_gnn_uW2", "L3_gnn_ub2"]


def kernel(**inputs):
    import numpy as np
    import concourse.bacc as bacc
    from concourse.bass_utils import run_bass_kernel_spmd as run

    x, src, dst, edge = (np.asarray(inputs[n]) for n in ("x", "src", "dst", "edge_attr_32"))
    z = Sizes(x.shape[0], src.shape[0])
    E = z.etiles * P
    x_pad = np.zeros((z.rows, D), x.dtype)
    x_pad[BN:BN + z.nodes] = x
    x_rows = np.ascontiguousarray(x_pad.reshape(z.nb, NT, P, D).transpose(0, 2, 1, 3)).reshape(z.rows, D)
    x_cols = np.ascontiguousarray(x_pad.T)
    src_pad = np.zeros(E, np.int32)
    src_pad[:z.edges] = src
    dst_pad = np.full(E + P, z.pad_node, np.int32)
    dst_pad[:z.edges] = dst
    by_tile = lambda v: np.ascontiguousarray(v.reshape(z.etiles, P).T)
    edge_pad = np.zeros((DE, E), edge.dtype)
    edge_pad[:, :z.edges] = edge.T
    arrays = {
        "x_rows": x_rows, "x_cols": x_cols, "edge_cols": edge_pad,
        "src_pt": by_tile(src_pad), "dst_pt": by_tile(dst_pad[:E]), "dstn_pt": by_tile(dst_pad[1:E + 1]),
        "dst_rows": dst_pad.reshape(z.etiles + 1, P),
    }
    for n in WEIGHTS:
        arrays[n] = np.ascontiguousarray(inputs[n])
    nc = bacc.Bacc("TRN2", target_bir_lowering=False, num_devices=1)
    a = {n: nc.dram_tensor(n, v.shape, mybir.dt.from_np(v.dtype), kind="ExternalInput").ap() for n, v in arrays.items()}
    out = nc.dram_tensor("out", [z.rows, D], F32, kind="ExternalOutput").ap()
    build(nc, z, a, out)
    r = run(nc, [arrays], core_ids=[0])
    got = np.asarray(r.results[0]["out"]).reshape(z.nb, P, NT, D).transpose(0, 2, 1, 3).reshape(z.rows, D)
    return np.ascontiguousarray(got[BN:BN + z.nodes])
```

```python
import concourse.bass as bass
from concourse import mybir
from contextlib import ExitStack

F32, BF16, I32 = mybir.dt.float32, mybir.dt.bfloat16, mybir.dt.int32
ALU = mybir.AluOpType
ACT = mybir.ActivationFunctionType
AX = mybir.AxisListType

P = 128
NT = 16
BN = P * NT
GT = 8
ET = 8
HT = 4
D = 64
H = 128
DE = 32
EPS = 1e-5
RB = 8
RING = RB * ET
IX = 4 * ET


class Sizes:

    def __init__(self, nodes, edges):
        self.nodes, self.edges = nodes, edges
        self.nb = -(-nodes // BN) + 1
        self.nb += self.nb % 2
        self.tiles = self.nb * NT
        self.etiles = self.nb * ET
        assert self.etiles * P >= edges
        self.ix_columns = -(-self.etiles // IX) * IX
        self.rows = self.nb * BN
        assert nodes < self.rows - BN
        self.pad_node = (self.nb - 1) * BN
        self.wide = -(-(self.tiles + NT) // P) * P


def build(nc, z, a, out):
    ctx = ExitStack()
    NB = z.nb

    def sb(name, shape, dt=F32):
        return ctx.enter_context(nc.sbuf_tensor(name, shape, dt))

    def dram(name, shape, dt=F32):
        return nc.dram_tensor(name, shape, dt).ap()

    sets = [[ctx.enter_context(nc.semaphore(f"set{k}_{i}")) for i in range((78, 66)[k])] for k in range(2)]
    names, current = {}, [0]
    soft, base, first = {}, {}, [0]
    POOL_DMAS = ("wing0", "wing1", "rows0", "rows1", "pair0", "pair1", "g_rows", "g_old", "g_put")

    def kept(name):
        return f"{name}_{current[0]}" if name[0:2] == "g_" else name

    def S(name):
        if name in POOL_DMAS:
            key = kept(name)
            if key not in soft:
                soft[key] = ctx.enter_context(nc.semaphore(key))
            return soft[key]
        if name not in names:
            names[name] = sets[current[0]][len(names)]
        return names[name]

    def since(name):
        return base.get(kept(name), 0) if name in POOL_DMAS else first[0]

    def carry(name, count):
        base[kept(name)] = since(name) + count

    def next_pass(number):
        current[0], first[0] = number % 2, 1
        names.clear()
        return sets[1 - current[0]]

    def start_at_one(sp, semaphores):
        for s in semaphores:
            sp.sem_clear(s)
            sp.sem_inc(s, 1)

    def now(uses):
        return uses + (1 + first[0])

    def before(uses):
        return uses + first[0]

    def landed(name, uses, dmas=1):
        return uses * (16 * dmas) + (16 * dmas + since(name))

    s1_t, n1_t = dram("s1_t", [z.rows, H]), dram("n1_t", [z.rows, H])
    s2_t, n2_t = dram("s2_t", [z.rows, D]), dram("n2_t", [z.rows, D])
    x1_t, y1_t, y2_t = (dram(n, [z.rows, D]) for n in ("x1_t", "y1_t", "y2_t"))
    x2_t, x3_t = dram("x2_t", [z.rows, D]), dram("x3_t", [z.rows, D])
    msg_t = dram("msg_t", [z.etiles * P, D])
    sums_t, sums2_t = dram("sums_t", [z.rows, D]), dram("sums2_t", [z.rows, H])
    win_d = dram("win_d", [z.wide], I32)
    slot_d = dram("slot_d", [2, z.wide], I32)
    pref_d = dram("pref_d", [3, 32 * 32], I32)

    def block_of(table, m, width):
        return table[bass.ds(m * BN, BN), :].rearrange("(p j) f -> p (j f)", p=P)

    src_ix = sb("src_ix", [P, z.ix_columns], I32)
    dst_ix = sb("dst_ix", [P, z.ix_columns], I32)
    dst_f = sb("dst_f", [P, z.etiles])
    window = sb("window", [P, 2, z.wide])
    slots = sb("slots", [1, 2, z.tiles], I32)
    flag = sb("flag", [1, 4], I32)
    deg = sb("deg", [P, z.tiles])
    invdeg = sb("invdeg", [P, z.tiles])
    dis = sb("dis", [P, z.tiles])
    ident = sb("ident", [P, P])
    iota = sb("iota", [P, P])
    eps_c = sb("eps_c", [P, 1])
    w0 = sb("w0", [P, H])
    w1 = sb("w1", [P, 2 * H])
    w2 = sb("w2", [P, H])
    wg1, wg2, wi1, wi2 = (sb(n, [P, P]) for n in ("wg1", "wg2", "wi1", "wi2"))
    wm1 = sb("wm1", [P, H])
    wm1e = sb("wm1e", [P, H])
    wm2 = sb("wm2", [P, P])
    wu1, wu2 = sb("wu1", [P, H]), sb("wu2", [P, P])
    b0c, bg1c, bi1c, bm1c, bu1c = (sb(n, [P, 1]) for n in ("b0c", "bg1c", "bi1c", "bm1c", "bu1c"))
    b1r, b2r, bg2r, bi2r, bm2r, bu2r = (
        sb(n, [P, w]) for n, w in (("b1r", H), ("b2r", D), ("bg2r", D), ("bi2r", D), ("bm2r", D), ("bu2r", D)))

    ps_all = ctx.enter_context(nc.psum_tensor("ps_all", [P, 8 * 512], F32))
    ps = [ps_all[:, 512 * i:512 * (i + 1)] for i in range(8)]

    def work(name, bytes_):
        return sb(name, [P, bytes_ // 4])

    HOT = 2 * 2 * GT * P
    RING_D, RING_H = RING * (D + 1), RING * H
    arena = sb("arena", [P, RING_D + 2 * HOT])
    ring = arena[:, 0:RING_H]
    load_a = [work(f"load_a{u}", NT * H * 4) for u in range(2)]
    load_b = [work(f"load_b{u}", NT * D * 4) for u in range(2)]
    store_a = [work(f"store_a{u}", NT * H * 4) for u in range(2)]
    store_b = [work(f"store_b{u}", NT * H * 4) for u in range(2)]
    tmp = [[work(f"tmp{k}{q}", 2048) for q in range(2)] for k in range(2)]
    tp = [work(f"tp{q}", 2048) for q in range(2)]
    tq = [work(f"tq{q}", 2048) for q in range(2)]
    stat = sb("stat", [P, 2, 6, GT])
    sq = [work(f"sq{q}", 2048) for q in range(2)]
    ix_now = sb("ix_now", [P, 2 * IX], I32)
    ix_dst = sb("ix_dst", [P, 2 * IX], I32)

    def setup():
        pro = ExitStack()

        def tb(name, shape, dt=F32):
            return pro.enter_context(nc.sbuf_tensor(name, shape, dt))

        E = z.etiles
        ring_i = ring[:, :].bitcast(I32)
        used = [0]

        def part(n, dt=I32):
            v = ring_i[:, used[0]:used[0] + n]
            used[0] += n
            assert used[0] <= RING_H
            return v if dt == I32 else v.bitcast(dt)

        src_i, dst_i, nxt_i = part(E), part(E), part(E)
        t_i, u_i, v_i = part(E), part(E), part(E)
        hi_f, lo_f, gt_f = part(E, F32), part(E, F32), part(E, F32)
        i32_i = part(32)
        i32_f = part(32, F32)
        CH = 8
        oh = tb("oh", [P, 2, 2, CH, 32], BF16)
        tri = tb("tri", [32, 32])
        ones = tb("ones", [P, 32])
        sc = tb("sc", [32, 12, 32])
        sc_i = tb("sc_i", [32, 6, 32], I32)
        viol = tb("viol", [P, 4])
        kw = tb("kw", [P, z.wide // P], I32)
        kw2 = tb("kw2", [P, z.wide // P], I32)
        tid = tb("tid", [P, z.wide // P])
        win_g = tb("win_g", [P, 2, 2, P], I32)
        win_f = tb("win_f", [P, 2, 2, P])
        iota_i = tb("iota_i", [P, P], I32)
        tid_i = tb("tid_i", [P, z.wide // P], I32)
        zero_i = tb("zero_i", [1, 2 * NT], I32)
        steps = E // CH
        NW = z.wide // P

        with nc.Block() as block:
            n_loads = [0]

            @block.sync
            def _(sp):
                start_at_one(sp, sets[1])

                def load(dst, src):
                    sp.dma_start(dst, src).then_inc(S("weights"), 16)
                    n_loads[0] += 1

                for d, s in ((src_i, a["src_pt"]), (dst_i, a["dst_pt"]), (nxt_i, a["dstn_pt"])):
                    sp.dma_start(d, s).then_inc(S("edges"), 16)
                load(w0[0:D, :], a["L0_gnn_ws0"])
                load(w0[D:P, :], a["L0_gnn_wn0"])
                load(w1[:, 0:H], a["L0_gnn_wn1"])
                load(w1[:, H:2 * H], a["L0_gnn_ws1"])
                load(w2[:, 0:D], a["L0_gnn_ws2"])
                load(w2[:, D:H], a["L0_gnn_wn2"])
                load(wm1[:, :], a["L3_gnn_mW1"][0:P, :])
                load(wu1[:, :], a["L3_gnn_uW1"])
                sp.wait_ge(S("zeroed"), 1)
                for w, n in ((wg1, "L1_gnn_W1"), (wg2, "L1_gnn_W2"), (wi1, "L2_gnn_W1"), (wi2, "L2_gnn_W2")):
                    load(w[0:D, 0:D], a[n])
                    load(w[D:P, D:P], a[n])
                load(wm1e[0:DE, :], a["L3_gnn_mW1"][P:P + DE, :])
                load(wm2[:, 0:D], a["L3_gnn_mW2"])
                load(wu2[:, 0:D], a["L3_gnn_uW2"])
                col = lambda n: a[n].rearrange("(p o) -> p o", o=1)
                load(b0c[:, :], col("L0_gnn_b0"))
                load(bm1c[:, :], col("L3_gnn_mb1"))
                load(bu1c[:, :], col("L3_gnn_ub1"))
                for b, n in ((bg1c, "L1_gnn_b1"), (bi1c, "L2_gnn_b1")):
                    load(b[0:D, :], col(n))
                    load(b[D:P, :], col(n))
                for b, n in ((b1r, "L0_gnn_b1"), (b2r, "L0_gnn_b2"), (bg2r, "L1_gnn_b2"), (bi2r, "L2_gnn_b2"),
                             (bm2r, "L3_gnn_mb2"), (bu2r, "L3_gnn_ub2")):
                    load(b[:, :], a[n].partition_broadcast(P))
                sp.wait_ge(S("pref"), 1)
                for k in range(3):
                    sp.dma_start(pref_d[k, :].rearrange("(a b) -> a b", a=32), sc_i[:, 3 + k, :]).then_inc(S("tabs"), 16)
                sp.wait_ge(S("tabs"), 48)
                NR = z.tiles - NT
                sp.dma_start(win_d[NT:z.tiles], pref_d[0, 0:NR]).then_inc(S("tabs2"), 16)
                sp.dma_start(win_d[0:NT].rearrange("(o n) -> o n", o=1), zero_i[:, 0:NT]).then_inc(S("tabs2"), 16)
                for k in range(2):
                    sp.dma_start(slot_d[k, NT:z.tiles], pref_d[1 + k, 0:NR]).then_inc(S("tabs2"), 16)
                    sp.dma_start(slot_d[k:k + 1, 0:NT], zero_i[:, 0:NT]).then_inc(S("tabs2"), 16)
                left = z.wide - z.tiles
                for at in range(0, left, NT):
                    n = min(NT, left - at)
                    sp.dma_start(win_d[z.tiles + at:z.tiles + at + n].rearrange("(o n) -> o n", o=1), zero_i[:, 0:n]).then_inc(S("tabs2"), 16)
                sp.wait_ge(S("tabs2"), 16 * (6 + len(range(0, left, NT))))
                for k in range(2):
                    sp.dma_start(slots[:, k, :], slot_d[k:k + 1, 0:z.tiles]).then_inc(S("tabs3"), 16)
                with nc.allow_non_contiguous_dma(reason="a table of a few hundred numbers, once"):
                    sp.dma_start(kw[:, :], win_d.rearrange("(c p) -> p c", p=P)).then_inc(S("tabs4"), 16)
                sp.wait_ge(S("tabs3"), 32)
                sp.wait_ge(S("weights"), 16 * n_loads[0])

            @block.gpsimd
            def _(pool):
                pool.memset(tri[:, :], 1.0).then_inc(S("poolc"), 1)
                pool.wait_ge(S("poolc"), 1)
                pool.affine_select(out=tri[:, :], in_=tri[:, :], compare_op=ALU.is_gt, fill=0.0, base=0,
                                   pattern=[[1, 32]], channel_multiplier=-1).then_inc(S("poolc"), 1)
                pool.memset(ident[:, :], 0.0).then_inc(S("poolc"), 1)
                pool.wait_ge(S("poolc"), 3)
                pool.affine_select(out=ident[:, :], in_=ident[:, :], compare_op=ALU.not_equal, fill=1.0, base=0,
                                   pattern=[[-1, P]], channel_multiplier=1).then_inc(S("poolc"), 1)
                pool.iota(iota_i[:, :], pattern=[[1, P]], base=0, channel_multiplier=0).then_inc(S("iotas"), 1)
                pool.iota(i32_i, pattern=[[1, 32]], base=0, channel_multiplier=0).then_inc(S("iotas"), 1)
                pool.iota(sc_i[:, 0, :], pattern=[[1, 32]], base=0, channel_multiplier=32).then_inc(S("iotas"), 1)
                pool.iota(tid_i[:, :], pattern=[[P, NW]], base=0, channel_multiplier=1).then_inc(S("iotas"), 1)
                pool.wait_ge(S("tabs4"), 16)
                pool.wait_ge(S("kw2"), 1)
                for c in range(NW):
                    if c >= 2:
                        pool.wait_ge(S("winf"), c - 1)
                    for k, ix in enumerate((kw, kw2)):
                        pool.indirect_dma_start(
                            out=win_g[:, c % 2, k, :], out_offset=None, in_=a["dst_rows"],
                            in_offset=bass.IndirectOffsetOnAxis(ap=ix[:, c:c + 1], axis=0)).then_inc(S(f"wing{c % 2}"), 16)

            @block.vector
            def _(ve):
                k = [0]

                def step(ins):
                    k[0] += 1
                    ins.then_inc(S("chain"), 1)
                    ve.wait_ge(S("chain"), k[0])

                V = nc.vector
                for w in (wg1, wg2, wi1, wi2, wm1e, wm2, wu2):
                    last = V.memset(w[:, :], 0.0)
                last.then_inc(S("zeroed"), 1)
                step(V.memset(zero_i[:, :], 0))
                step(V.memset(ones[:, :], 1.0))
                step(V.memset(eps_c[:, :], EPS))
                step(V.memset(viol[:, :], 0.0))
                step(V.memset(flag[:, :], 0))
                for d in (src_ix, dst_ix):
                    step(V.memset(d[:, :], 0))
                ve.wait_ge(S("iotas"), 4)
                step(V.tensor_copy(iota[:, :], iota_i[:, :]))
                step(V.tensor_copy(i32_f, i32_i))
                step(V.tensor_copy(tid[:, :], tid_i[:, :]))
                step(V.tensor_copy(sc[:, 11, :], sc_i[:, 0, :]))
                step(V.tensor_scalar(tid[:, :], tid[:, :], float(-P), float(P * NT), ALU.mult, ALU.add))
                ve.wait_ge(S("edges"), 48)
                step(V.tensor_copy(dst_f[:, :], dst_i))
                for d, s in ((src_ix, src_i), (dst_ix, dst_i)):
                    step(V.tensor_scalar(t_i, s, 11, 11, ALU.logical_shift_right, ALU.logical_shift_left))
                    step(V.tensor_scalar(u_i, s, 127, 4, ALU.bitwise_and, ALU.logical_shift_left))
                    step(V.tensor_scalar(v_i, s, 7, 15, ALU.logical_shift_right, ALU.bitwise_and))
                    step(V.tensor_tensor(u_i, u_i, v_i, ALU.add))
                    step(V.tensor_tensor(u_i, u_i, t_i, ALU.add))
                    step(V.tensor_scalar(d[:, 0:E], u_i, float(BN), float(z.rows - 1), ALU.add, ALU.min))
                step(V.tensor_copy(hi_f, nxt_i))
                step(V.tensor_tensor(gt_f, dst_f[:, :], hi_f, ALU.is_gt))
                step(V.tensor_reduce(viol[:, 0:1], gt_f, AX.X, ALU.add))
                step(V.tensor_scalar(t_i, dst_i, 12, None, ALU.logical_shift_right))
                step(V.tensor_scalar(u_i, dst_i, 7, 31, ALU.logical_shift_right, ALU.bitwise_and))
                step(V.tensor_copy(hi_f, t_i))
                step(V.tensor_copy(lo_f, u_i))
                for s in range(steps):
                    if s >= 2:
                        ve.wait_ge(S("hist"), s - 1)
                    for d, v in enumerate((hi_f, lo_f)):
                        V.tensor_tensor(oh[:, s % 2, d, :, :],
                                        i32_f.unsqueeze(1).to_broadcast([P, CH, 32]),
                                        v[:, s * CH:(s + 1) * CH].unsqueeze(2).to_broadcast([P, CH, 32]),
                                        ALU.is_equal).then_inc(S("ohs"), 1)
                ve.wait_ge(S("hist"), steps)
                C, INC, EXC, ENDS, A, B, CC, DD = range(8)
                step(V.tensor_copy(sc[:, C, :], ps[0][0:32, 0:32]))
                step(V.tensor_tensor_scan(sc[:, INC, :], ones[0:32, :], sc[:, C, :], 0.0, ALU.mult, ALU.add))
                V.tensor_copy(sc[:, 10, 0:1], sc[:, INC, 31:32]).then_inc(S("tot"), 1)
                ve.wait_ge(S("rowp"), 1)
                step(V.tensor_copy(sc[:, 10, 1:2], ps[1][0:32, 0:1]))
                step(V.tensor_scalar(sc[:, ENDS, :], sc[:, INC, :], sc[:, 10, 1:2], None, ALU.add))
                step(V.tensor_tensor(sc[:, EXC, :], sc[:, ENDS, :], sc[:, C, :], ALU.subtract))
                step(V.tensor_copy(sc_i[:, 1, :], sc[:, EXC, :]))
                step(V.tensor_scalar(sc_i[:, 3, :], sc_i[:, 1, :], 7, None, ALU.logical_shift_right))
                step(V.tensor_copy(sc[:, A, :], sc_i[:, 3, :]))
                step(V.tensor_scalar(sc[:, B, :], sc[:, A, :], float(P), float(2 * P), ALU.mult, ALU.add))
                step(V.tensor_tensor(sc[:, B, :], sc[:, ENDS, :], sc[:, B, :], ALU.is_gt))
                step(V.tensor_scalar(sc_i[:, 1, :], sc_i[:, 0, :], 4, 3, ALU.logical_shift_right, ALU.logical_shift_left))
                step(V.tensor_copy(sc[:, CC, :], sc_i[:, 1, :]))
                step(V.tensor_tensor(sc[:, DD, :], sc[:, A, :], sc[:, CC, :], ALU.subtract))
                step(V.tensor_scalar(sc[:, CC, :], sc[:, DD, :], float(2 * ET - 2), None, ALU.is_gt))
                step(V.tensor_tensor(sc[:, B, :], sc[:, B, :], sc[:, CC, :], ALU.add))
                step(V.tensor_scalar(sc[:, CC, :], sc[:, DD, :], float(-ET), None, ALU.is_lt))
                step(V.tensor_tensor(sc[:, B, :], sc[:, B, :], sc[:, CC, :], ALU.add))
                step(V.tensor_scalar(sc[:, CC, :], sc[:, 11, :], float(z.tiles - NT), None, ALU.is_lt))
                step(V.tensor_tensor(sc[:, B, :], sc[:, B, :], sc[:, CC, :], ALU.mult))
                step(V.tensor_reduce(viol[0:32, 1:2], sc[:, B, :], AX.X, ALU.add))
                V.tensor_tensor(viol[:, 2:3], viol[:, 0:1], viol[:, 1:2], ALU.add).then_inc(S("viol"), 1)
                step(V.tensor_scalar(sc_i[:, 1, :], sc_i[:, 3, :], 1.0, None, ALU.add))
                step(V.tensor_scalar(sc_i[:, 4, :], sc_i[:, 3, :], RING - 1, None, ALU.bitwise_and))
                step(V.tensor_scalar(sc_i[:, 5, :], sc_i[:, 1, :], RING - 1, None, ALU.bitwise_and))
                step(V.tensor_scalar(sc[:, A, :], sc[:, A, :], float(z.etiles - 1), None, ALU.min))
                V.tensor_copy(sc_i[:, 3, :], sc[:, A, :]).then_inc(S("pref"), 1)
                ve.wait_ge(S("violp"), 1)
                step(V.tensor_scalar(sc[0:1, CC, 0:1], ps[2][0:1, 0:1], 1.0, None, ALU.min))
                step(V.tensor_copy(flag[0:1, 0:1], sc[0:1, CC, 0:1]))
                ve.wait_ge(S("tabs4"), 16)
                V.tensor_scalar(kw2[:, :], kw[:, :], 1.0, None, ALU.add).then_inc(S("kw2"), 1)
                for c in range(NW):
                    ve.wait_ge(S(f"wing{c % 2}"), 32 * (c // 2 + 1))
                    if c >= 2:
                        ve.wait_ge(S("wint"), c - 1)
                    V.tensor_scalar(win_f[:, c % 2, :, :], win_g[:, c % 2, :, :], tid[:, c:c + 1], None,
                                    ALU.add).then_inc(S("winf"), 1)
                    ve.wait_ge(S("wint"), c + 1)
                    V.tensor_copy(window[:, :, c * P:(c + 1) * P],
                                  ps[4 + c % 2][:, 0:2 * P].rearrange("p (k t) -> p k t", k=2)).then_inc(S("wins"), 1)
                ve.wait_ge(S("wins"), NW)

            @block.tensor
            def _(pe):
                for s in range(steps):
                    pe.wait_ge(S("ohs"), 2 * s + 2)
                    for k in range(CH):
                        last = pe.matmul(ps[0][0:32, 0:32], oh[:, s % 2, 0, k, :], oh[:, s % 2, 1, k, :],
                                         start=(s + k == 0), stop=(s == steps - 1 and k == CH - 1))
                    last.then_inc(S("hist"), 1)
                pe.wait_ge(S("tot"), 1)
                pe.wait_ge(S("poolc"), 4)
                pe.matmul(ps[1][0:32, 0:1], tri[:, :], sc[:, 10, 0:1], start=True, stop=True).then_inc(S("rowp"), 1)
                pe.wait_ge(S("viol"), 1)
                pe.matmul(ps[2][0:1, 0:1], viol[:, 2:3], ones[:, 0:1], start=True, stop=True).then_inc(S("violp"), 1)
                for c in range(NW):
                    pe.wait_ge(S("winf"), c + 1)
                    if c >= 2:
                        pe.wait_ge(S("wins"), c - 1)
                    for k in range(2):
                        last = pe.transpose(ps[4 + c % 2][:, k * P:(k + 1) * P], win_f[:, c % 2, k, :], ident[:, :])
                    last.then_inc(S("wint"), 1)

        pro.close()

    g_rows, g_old = work("g_rows", H * 4), work("g_old", H * 4)
    g_new, g_same, g_low = work("g_new", H * 4), work("g_same", P * 4), work("g_low", P * 4)
    g_mask = sb("g_mask", [P, P])
    g_dst = sb("g_dst", [P, P], I32)
    g_small = sb("g_small", [P, 4])
    g_ix = sb("g_ix", [P, 3], I32)
    BIG = 1 << 22

    class General:

        def __init__(self, sums, width, table=None, direct=None):
            self.sums, self.width, self.table, self.direct = sums, width, table, direct

        def sync(self, sp):
            W = self.width
            sp.wait_ge(S("g_zero"), now(0))
            with sp.Fori(0, z.nb) as m:
                sp.dma_start(block_of(self.sums, m, W), store_a[0][:, 0:NT * W]).then_inc(S("g_cleared"), 16)

            def tile(m, t):
                k = m * ET + t
                sp.wait_ge(S("g_same"), before(k))
                sp.dma_start(g_dst[:, :], a["dst_rows"][bass.ds(k, 1), :].rearrange("o e -> (o e)").partition_broadcast(P)).then_inc(S("g_dst"), 16)
                if self.direct is not None:
                    sp.wait_ge(S("g_sum"), before(k))
                    block = self.direct[bass.ds(m * ET * P, ET * P), :].rearrange("(p t) f -> p t f", t=ET)
                    sp.dma_start(g_rows[:, 0:W], block[:, t, :]).then_inc(S("g_direct"), 16)

            with sp.Fori(0, NB) as m:
                for t in range(ET):
                    tile(m, t)

        def gpsimd(self, pool):
            W = self.width
            pool.memset(g_mask[:, :], 1.0).then_inc(S("g_mask"), 1)
            pool.wait_ge(S("g_mask"), before(1))
            pool.affine_select(out=g_mask[:, :], in_=g_mask[:, :], compare_op=ALU.is_gt, fill=0.0, base=0,
                               pattern=[[-1, P]], channel_multiplier=1).then_inc(S("g_mask"), 1)
            pool.wait_ge(S("g_cleared"), before(16 * z.nb))
            with pool.Fori(0, z.etiles) as k:
                pool.wait_ge(S("g_ix"), now(k))
                gate(pool)
                if self.table is not None:
                    pool.wait_ge(S("g_sum"), before(k))
                    gate(pool)
                    pool.indirect_dma_start(out=g_rows[:, 0:W], out_offset=None, in_=self.table,
                                            in_offset=bass.IndirectOffsetOnAxis(ap=g_ix[:, 0:1], axis=0)).then_inc(S("g_rows"), 16)
                pool.indirect_dma_start(out=g_old[:, 0:W], out_offset=None, in_=self.sums,
                                        in_offset=bass.IndirectOffsetOnAxis(ap=g_ix[:, 1:2], axis=0)).then_inc(S("g_old"), 16)
                pool.wait_ge(S("g_new"), now(k))
                gate(pool)
                pool.indirect_dma_start(out=self.sums, out_offset=bass.IndirectOffsetOnAxis(ap=g_ix[:, 2:3], axis=0),
                                        in_=g_new[:, 0:W], in_offset=None, bounds_check=z.rows - 1,
                                        oob_is_err=False).then_inc(S("g_put"), 16)
                pool.wait_ge(S("g_put"), landed("g_put", k))
                pool.sem_inc(S("g_stored"), 1)
            pool.sem_inc(S("g_all"), 1)

        def vector(self, ve):
            W = self.width
            V = nc.vector
            V.memset(store_a[0][:, 0:NT * W], 0.0).then_inc(S("g_zero"), 1)
            if self.table is None and self.direct is None:
                V.memset(g_rows[:, 0:W], 1.0).then_inc(S("g_zero"), 1)
            ve.wait_ge(S("g_mask"), before(2))
            with ve.Fori(0, z.etiles) as k:
                c = [0]

                def step(ins):
                    c[0] += 1
                    ins.then_inc(S("g_chain"), 1)
                    ve.wait_ge(S("g_chain"), before(k * 6 + c[0]))

                ve.wait_ge(S("g_stored"), before(k))
                ve.wait_ge(S("g_dst"), before(k * 16 + 16))
                ve.wait_ge(S("g_sum"), before(k))
                V.tensor_scalar(g_same[:, :], g_dst[:, :], dst_f[:, bass.ds(k, 1)], None, ALU.is_equal).then_inc(S("g_same"), 1)
                ve.wait_ge(S("g_same"), now(k))
                step(V.tensor_tensor(g_low[:, :], g_same[:, :], g_mask[:, :], ALU.mult))
                step(V.tensor_reduce(g_small[:, 0:1], g_low[:, :], AX.X, ALU.max))
                step(V.tensor_scalar(g_small[:, 1:2], dst_ix[:, bass.ds(k, 1)], 0.0, None, ALU.add))
                step(V.scalar_tensor_tensor(g_small[:, 2:3], g_small[:, 0:1], float(BIG), g_small[:, 1:2], ALU.mult, ALU.add))
                step(V.tensor_scalar(g_ix[:, 0:1], src_ix[:, bass.ds(k, 1)], 0.0, None, ALU.add))
                step(V.tensor_scalar(g_ix[:, 1:2], dst_ix[:, bass.ds(k, 1)], 0.0, None, ALU.add))
                V.tensor_copy(g_ix[:, 2:3], g_small[:, 2:3]).then_inc(S("g_ix"), 1)
                ve.wait_ge(S("g_sum"), now(k))
                ve.wait_ge(S("g_old"), landed("g_old", k))
                V.tensor_tensor(g_new[:, 0:W], ps[0][:, 0:W], g_old[:, 0:W], ALU.add).then_inc(S("g_new"), 1)

        def tensor(self, pe):
            W = self.width
            if self.table is None and self.direct is None:
                pe.wait_ge(S("g_zero"), before(2))
            with pe.Fori(0, z.etiles) as k:
                pe.wait_ge(S("g_same"), now(k))
                pe.wait_ge(S("g_new"), before(k))
                if self.table is not None or self.direct is not None:
                    pe.wait_ge(S("g_rows" if self.direct is None else "g_direct"), landed("g_rows" if self.direct is None else "g_direct", k))
                pe.matmul(ps[0][:, 0:W], g_same[:, :], g_rows[:, 0:W], start=True, stop=True).then_inc(S("g_sum"), 1)

    def pass_over(p):
        if p.table is not None:
            for u in range(2):
                carry(f"rows{u}", 16 * ET * (NB // 2))
            carry("g_rows", 16 * z.etiles)
        for name in ("g_old", "g_put"):
            carry(name, 16 * z.etiles)

    def both_ways(eng, general, windows):
        way = eng.value_load(flag[0:1, 0:1], min_val=0, max_val=1)
        with eng.If(way > 0):
            general()
        with eng.Else():
            windows()

    def bodies(eng, body, by=2, behind=2):
        n = (NB - behind) // by
        with eng.Fori(0, n) as it:
            for v in range(by):
                body(it * by + v, it * (by // 2) + v // 2, v % 2)
        for m in range(n * by, NB):
            body(m, m // 2, m % 2)

    def exists(m):
        return not isinstance(m, int) or m < NB

    def exists_before(m):
        return not isinstance(m, int) or m > 0

    def pre_of(q):
        return tmp[1][q][:, :]

    def later(m, i, u):
        return m + 1, i + u, 1 - u

    def gate(pool):
        pool.sem_inc(S("passed"), 1)

    def slot_rows(s, W, pitch):
        return ring[:, s * pitch:s * pitch + W]

    def gather_pool(pool, table, W, pitch, last_sum):
        def block(m, v, i, c):
            if v % 4 == 0:
                pool.wait_ge(S("ix"), landed("ix", c))
            if not isinstance(m, int) or m >= 2:
                pool.wait_ge(S(f"rows{v % 2}"), landed(f"rows{v % 2}", i - 1, ET))
            if not isinstance(m, int) or m >= RB:
                pool.wait_ge(S(last_sum), before(m - 5))
            gate(pool)
            for t in range(ET):
                at = v * ET + t
                pool.indirect_dma_start(
                    out=slot_rows(at, W, pitch), out_offset=None, in_=table,
                    in_offset=bass.IndirectOffsetOnAxis(ap=ix_now[:, at:at + 1], axis=0)).then_inc(S(f"rows{v % 2}"), 16)

        for m in range(min(RB, NB)):
            block(m, m, m // 2, m // 4)
        n = max(NB - RB, 0) // RB
        if n:
            with pool.Fori(1, n + 1) as it:
                for v in range(RB):
                    block(it * RB + v, v, it * (RB // 2) + v // 2, it * 2 + v // 4)
        for m in range((n + 1) * RB, NB):
            block(m, m % RB, m // 2, m // 4)

    def hot_matrices(at, q):
        return arena[:, at:at + HOT].rearrange("p (q k j n) -> p q k j n", q=2, k=2, j=GT)[:, q]

    def one_hots(ve, m, q, at):
        V = nc.vector
        V.tensor_tensor(hot_matrices(at, q),
                        iota[:, :].unsqueeze(1).unsqueeze(1).to_broadcast([P, 2, GT, P]),
                        window[:, :, bass.ds(m * NT + q * GT, GT)].unsqueeze(3).to_broadcast([P, 2, GT, P]),
                        ALU.is_equal).then_inc(S(f"hot{q}"), 1)

    def sums(pe, m, tiles, out, W, at):
        first, n = tiles[0], len(tiles)
        places = [nc.values_load_multi_w_load_instructions(
            slots[0:1, k, bass.ds(m * NT + first, n)], engines=(mybir.EngineType.PE,), min_val=0, max_val=RING - 1,
            skip_runtime_bounds_check_because="the table holds remainders by RING")[1] for k in range(2)]
        for j in tiles:
            for k in range(2):
                last = pe.matmul(out(j), hot_matrices(at, j // GT)[:, k, j % GT, :],
                                 ring[:, bass.ds(places[k][j - first] * W, W)], start=(k == 0), stop=(k == 1))
        return last

    def group(ap, q, W=D):
        return ap[:, q * GT * W:(q + 1) * GT * W]

    def tiles3(ap, W=D):
        return ap.rearrange("p (j w) -> p j w", w=W)

    def per_node(table, m, q):
        return table[:, bass.ds(m * NT + q * GT, GT)].unsqueeze(2).to_broadcast([P, GT, D])

    def row(b, W=D, n=GT):
        return b[:, :].unsqueeze(1).to_broadcast([P, n, W])

    def general_sums(u, W):
        return ring[:, u * NT * H:u * NT * H + NT * W]

    def norm_center(ve, m, pre, act_groups=()):
        V = nc.vector
        for q in range(2):
            ve.wait_ge(S(f"pre{q}"), now(m))
            V.tensor_reduce(stat[:, q, 0, :], tiles3(pre(q)), AX.X, ALU.add).then_inc(S(f"rs{q}"), 1)
        for q in range(2):
            ve.wait_ge(S(f"rs{q}"), now(m))
            if q in act_groups:
                ve.wait_ge(S(f"shift{q}"), before(m))
            V.tensor_scalar(stat[:, q, 1, :], stat[:, q, 0, :], -1.0 / D, None, ALU.mult).then_inc(S(f"nm{q}"), 1)
        for q in range(2):
            if q not in act_groups:
                ve.wait_ge(S(f"nm{q}"), now(m))
                V.tensor_tensor(tiles3(tmp[0][q][:, :]), tiles3(pre(q)),
                                stat[:, q, 1, :].unsqueeze(2).to_broadcast([P, GT, D]), ALU.add).then_inc(S(f"xc{q}"), 1)

    def norm_square(act, m, q, pre, by_act=False, adds=False):
        A = nc.scalar
        if by_act:
            act.wait_ge(S(f"nm{q}"), now(m))
            for j in range(GT):
                last = A.activation(store_a[1][:, (NT + q * GT + j) * D:(NT + q * GT + j + 1) * D], pre(q)[:, j * D:(j + 1) * D], ACT.Square,
                                    bias=stat[:, q, 1, j:j + 1], accum_out=stat[:, q, 2, j:j + 1])
            last.then_inc(S(f"vs{q}"), 1)
        elif adds:
            act.wait_ge(S(f"xc{q}"), now(m))
            act.wait_ge(S(f"sd{q}"), before(m))
            for j in range(GT):
                last = A.activation(sq[q][:, j * D:(j + 1) * D], tmp[0][q][:, j * D:(j + 1) * D], ACT.Square,
                                    accum_out=stat[:, q, 2, j:j + 1])
            last.then_inc(S(f"vs{q}"), 1)
        else:
            act.wait_ge(S(f"xc{q}"), now(m))
            act.wait_ge(S(f"vs{q}"), before(m))
            A.activation(sq[q][:, :], tmp[0][q][:, :], ACT.Square).then_inc(S(f"sq{q}"), 1)

    def norm_root(act, m):
        for q in range(2):
            act.wait_ge(S(f"vs{q}"), now(m))
            nc.scalar.activation(stat[:, q, 3, :], stat[:, q, 2, :], ACT.Sqrt, bias=eps_c[:, :], scale=1.0 / D).then_inc(S(f"sd{q}"), 1)

    def norm_apply(act, m, q, pre, to):
        act.wait_ge(S(f"shift{q}"), now(m))
        for j in range(GT):
            last = nc.scalar.activation(group(to, q)[:, j * D:(j + 1) * D], pre(q)[:, j * D:(j + 1) * D], ACT.Identity,
                                        bias=stat[:, q, 5, j:j + 1], scale=stat[:, q, 4, j:j + 1])
        last.then_inc(S(f"out{q}"), 1)

    def norm_var(ve, m, act_groups=()):
        for q in range(2):
            if q not in act_groups:
                ve.wait_ge(S(f"sq{q}"), now(m))
                nc.vector.tensor_reduce(stat[:, q, 2, :], tiles3(sq[q][:, :]), AX.X, ALU.add).then_inc(S(f"vs{q}"), 1)

    def norm_out(ve, m, to, act_groups=()):
        V = nc.vector
        for q in range(2):
            ve.wait_ge(S(f"sd{q}"), now(m))
            if q in act_groups:
                ve.wait_ge(S(f"out{q}"), before(m))
            V.reciprocal(stat[:, q, 4, :], stat[:, q, 3, :]).then_inc(S(f"rstd{q}"), 1)
        for q in range(2):
            ve.wait_ge(S(f"rstd{q}"), now(m))
            if q in act_groups:
                V.tensor_tensor(stat[:, q, 5, :], stat[:, q, 1, :], stat[:, q, 4, :], ALU.mult).then_inc(S(f"shift{q}"), 1)
            else:
                V.tensor_tensor(tiles3(group(to, q)), tiles3(tmp[0][q][:, :]),
                                stat[:, q, 4, :].unsqueeze(2).to_broadcast([P, GT, D]), ALU.mult).then_inc(S(f"out{q}"), 1)

    def stay_warm(pe, use, n):
        pe.wait_ge(S("warm"), before(use))
        for k in range(n):
            last = pe.matmul(ps[7][:, 0:P], ident[:, :], ident[:, :], start=(k == 0), stop=(k == n - 1))
        last.then_inc(S("warm"), 1)

    class Pass:
        ahead = 3
        double = True
        W = D
        pitch = D
        last_sum = "agg1"
        loads, stores, consumed = (), (), ()

        def __init__(self, number, table, general):
            self.number, self.table, self.gen = number, table, general

        def load_block(self, sp, m, u):
            for table, buf, W in self.loads:
                sp.dma_start(buf[u][:, 0:NT * W], block_of(table, m, W)).then_inc(S(f"in{u}"), 16)

        def load_sums(self, sp, m, u):
            sp.dma_start(general_sums(u, self.W), block_of(self.gen.sums, m, self.W)).then_inc(S(f"sums{u}"), 16)

        def load_index(self, sp, c):
            sp.dma_start(ix_now[:, bass.ds((c % 2) * IX, IX)], src_ix[:, bass.ds(c * IX, IX)]).then_inc(S("ix"), 16)

        def sync_rows_first(self, sp):
            self.load_index(sp, 0)

        def sync_rows(self, sp, m, i, u, v):
            if v % 4 == 0 and exists(m + 4):
                c = m // 4 if isinstance(m, int) else self.chunk
                if not isinstance(m, int) or m > 0:
                    sp.wait_ge(S(self.last_sum), before(m))
                sp.wait_ge(S("ix"), landed("ix", c))
                self.load_index(sp, c + 1)

        def sync_loop(self, sp, windows):
            if windows:
                self.sync_rows_first(sp)
            for u in range(2):
                self.load_block(sp, u, u)
                if not windows:
                    self.load_sums(sp, u, u)

            start_at_one(sp, self.other)

            def body(m, i, u, v):
                if windows:
                    self.sync_rows(sp, m, i, u, v)
                if exists(m + 2):
                    for name in self.consumed:
                        sp.wait_ge(S(name), now(m))
                    self.load_block(sp, m + 2, u)
                    if not windows:
                        self.load_sums(sp, m + 2, u)
                for table, buf, W, signals in self.stores:
                    for name in signals:
                        sp.wait_ge(S(name), now(m))
                    sp.dma_start(block_of(table, m, W), buf[u][:, 0:NT * W]).then_inc(S(f"put{u}"), 16)

            n = (NB - 4) // 4
            with sp.Fori(0, n) as it:
                self.chunk = it
                for v in range(4):
                    body(it * 4 + v, it * 2 + v // 2, v % 2, v)
            for m in range(n * 4, NB):
                body(m, m // 2, m % 2, m)
            for u in range(2):
                sp.wait_ge(S(f"put{u}"), before(16 * len(self.stores) * (NB // 2)))

        def inputs_in(self, eng, i, u):
            eng.wait_ge(S(f"in{u}"), landed(f"in{u}", i, len(self.loads)))

        def stored(self, eng, i, u):
            eng.wait_ge(S(f"put{u}"), before(i * 16 * len(self.stores)))

        def sums_here(self, ve, m, i, u, q, windows):
            if windows:
                ve.wait_ge(S(f"agg{q}"), now(m))
                return ps[q][:, 0:GT * D]
            ve.wait_ge(S(f"sums{u}"), landed(f"sums{u}", i))
            return group(general_sums(u, D), q)

        def rows_in(self, pe, i, u):
            pe.wait_ge(S(f"rows{u}"), landed(f"rows{u}", i, ET))

        def collect(self, pe, m, i, u, q):
            if not exists(m):
                return
            if q == 0:
                self.rows_in(pe, i, u)
            pe.wait_ge(S(f"hot{q}"), now(m))
            pe.wait_ge(S(f"mean{q}"), before(m))
            sums(pe, m, range(q * GT, q * GT + GT), lambda j: ps[q][:, (j % GT) * D:(j % GT + 1) * D],
                 D, self.hot_at(u)).then_inc(S(f"agg{q}"), 1)

        def hot_at(self, u):
            return RING_D + u * HOT if self.double else RING_H

        hot_used = ("agg0", "agg1")

        def hot(self, ve, m, u, q, windows):
            if windows and exists(m):
                back = 2 if self.double else 1
                if not isinstance(m, int) or m >= back:
                    ve.wait_ge(S(self.hot_used[q]), before(m + (1 - back)))
                one_hots(ve, m, q, self.hot_at(u))

        def hots(self, ve, m, u, windows):
            for q in range(2):
                self.hot(ve, m, u, q, windows)

        def hot_ahead(self, ve, m, u, q, windows):
            self.hot(ve, m + self.ahead, (u + self.ahead) % 2, q, windows)

        def hots_ahead(self, ve, m, u, windows):
            for q in range(2):
                self.hot_ahead(ve, m, u, q, windows)

        def take(self, ve, m, i, u, q, windows):
            pass

        def take_block(self, ve, m, i, u, windows):
            for q in range(2):
                self.take(ve, m, i, u, q, windows)

        def vector_loop(self, ve, windows):
            for m in range(self.ahead - 1):
                self.hots(ve, m, m, windows)
            self.take_block(ve, 0, 0, 0, windows)
            self.hots(ve, self.ahead - 1, (self.ahead - 1) % 2, windows)
            bodies(ve, lambda m, i, u: self.vector(ve, m, i, u, windows))

        def scalar_loop(self, act, windows):
            bodies(act, lambda m, i, u: self.scalar(act, m, i, u, windows))

        def tensor_loop(self, pe, windows):
            if windows:
                for q in range(2):
                    self.collect(pe, 0, 0, 0, q)
            bodies(pe, lambda m, i, u: self.tensor(pe, m, i, u, windows))

        def gpsimd_windows(self, pool):
            gather_pool(pool, self.table, self.W, self.pitch, self.last_sum)

        def emit(self):
            self.other = next_pass(self.number)
            with nc.Block() as block:

                @block.sync
                def _(sp):
                    def general():
                        self.gen.sync(sp)
                        sp.wait_ge(S("g_all"), now(0))
                        self.sync_loop(sp, False)

                    both_ways(sp, general, lambda: self.sync_loop(sp, True))

                @block.gpsimd
                def _(pool):
                    both_ways(pool, lambda: self.gen.gpsimd(pool), lambda: self.gpsimd_windows(pool))

                @block.vector
                def _(ve):
                    def general():
                        self.gen.vector(ve)
                        self.vector_loop(ve, False)

                    both_ways(ve, general, lambda: self.vector_loop(ve, True))

                @block.scalar
                def _(act):
                    both_ways(act, lambda: self.scalar_loop(act, False), lambda: self.scalar_loop(act, True))

                @block.tensor
                def _(pe):
                    def general():
                        self.gen.tensor(pe)
                        self.tensor_loop(pe, False)

                    both_ways(pe, general, lambda: self.tensor_loop(pe, True))

            pass_over(self)

    def pair_transposes(pe, src, bank):
        for r in range(GT // 2):
            last = pe.transpose(bank[:, r * P:(r + 1) * P], src[:, r * P:(r + 1) * P], ident[:, :])
        return last

    def pair_products(pe, lhs, w, bank):
        for r in range(GT // 2):
            last = pe.matmul(bank[:, r * P:(r + 1) * P], lhs[:, r * P:(r + 1) * P], w[:, :], start=True, stop=True)
        return last

    class Sage2(Pass):
        loads = ((s2_t, load_a, D), (a["x_rows"], load_b, D))
        stores = ((x1_t, store_a, D, ("out0", "out1")), (y1_t, store_b, D, ("y0", "y1")))
        consumed = ("pre0", "pre1")

        def take_block(self, ve, m, i, u, windows):
            V = nc.vector
            if not exists(m):
                return
            for q in range(2):
                agg = self.sums_here(ve, m, i, u, q, windows)
                ve.wait_ge(S(f"out{q}"), before(m))
                V.tensor_tensor(tiles3(tmp[0][q][:, :]), tiles3(agg), per_node(invdeg, m, q), ALU.mult).then_inc(S(f"mean{q}"), 1)
            self.inputs_in(ve, i, u)
            for q in range(2):
                ve.wait_ge(S(f"mean{q}"), now(m))
                V.tensor_tensor(tmp[1][q][:, :], tmp[0][q][:, :], group(load_a[u], q), ALU.add).then_inc(S(f"sum{q}"), 1)
            for q in range(2):
                ve.wait_ge(S(f"sum{q}"), now(m))
                V.scalar_tensor_tensor(tmp[1][q][:, :], tmp[1][q][:, :], 0.0, group(load_b[u], q), ALU.max, ALU.add).then_inc(S(f"pre{q}"), 1)
            norm_center(ve, m, pre_of)

        def vector(self, ve, m, i, u, windows):
            V = nc.vector
            self.stored(ve, i, u)
            norm_out(ve, m, store_a[u])
            self.take_block(ve, *later(m, i, u), windows)
            self.hots_ahead(ve, m, u, windows)
            for q in range(2):
                ve.wait_ge(S(f"mm{q}"), now(m))
                V.tensor_tensor(tiles3(group(store_b[u], q)), tiles3(ps[4 + q]), per_node(dis, m, q), ALU.mult).then_inc(S(f"y{q}"), 1)

        def scalar_loop(self, act, windows):
            for q in range(2):
                norm_square(act, 0, q, pre_of, adds=True)
            super().scalar_loop(act, windows)

        def scalar(self, act, m, i, u, windows):
            norm_root(act, m)
            for q in range(2):
                act.wait_ge(S(f"tr{q}"), now(m))
                act.wait_ge(S(f"mm{q}"), before(m))
                nc.scalar.activation(tp[q][:, :], ps[2 + q], ACT.Copy).then_inc(S(f"ev{q}"), 1)
            if exists(m + 1):
                for q in range(2):
                    norm_square(act, m + 1, q, pre_of, adds=True)

        def tensor(self, pe, m, i, u, windows):
            if windows:
                for q in range(2):
                    self.collect(pe, *later(m, i, u), q)
            for q in range(2):
                pe.wait_ge(S(f"out{q}"), now(m))
                pe.wait_ge(S(f"ev{q}"), before(m))
                pair_transposes(pe, group(store_a[u], q), ps[2 + q]).then_inc(S(f"tr{q}"), 1)
            for q in range(2):
                pe.wait_ge(S(f"ev{q}"), now(m))
                pe.wait_ge(S(f"y{q}"), before(m))
                pair_products(pe, tp[q], wg1, ps[4 + q]).then_inc(S(f"mm{q}"), 1)

    class Gcn1(Pass):
        loads = ((y1_t, load_b, D),)
        stores = ((y2_t, store_b, D, ("y0", "y1")),)
        consumed = ("mean0", "mean1")

        def take_block(self, ve, m, i, u, windows):
            V = nc.vector
            if not exists(m):
                return
            self.inputs_in(ve, i, u)
            for q in range(2):
                agg = self.sums_here(ve, m, i, u, q, windows)
                ve.wait_ge(S(f"pre{q}"), before(m))
                V.tensor_tensor(tmp[0][q][:, :], agg, group(load_b[u], q), ALU.add).then_inc(S(f"mean{q}"), 1)
            for q in range(2):
                ve.wait_ge(S(f"mean{q}"), now(m))
                ve.wait_ge(S(f"tr{q}"), before(m))
                V.tensor_tensor(tiles3(tmp[1][q][:, :]), tiles3(tmp[0][q][:, :]), per_node(dis, m, q), ALU.mult).then_inc(S(f"pre{q}"), 1)

        def vector(self, ve, m, i, u, windows):
            V = nc.vector
            self.take_block(ve, *later(m, i, u), windows)
            self.hots_ahead(ve, m, u, windows)
            self.stored(ve, i, u)
            for q in range(2):
                ve.wait_ge(S(f"mm{q}"), now(m))
                V.tensor_tensor(tiles3(group(store_b[u], q)), tiles3(ps[4 + q]), per_node(dis, m, q), ALU.mult).then_inc(S(f"y{q}"), 1)

        def scalar(self, act, m, i, u, windows):
            for q in range(2):
                act.wait_ge(S(f"tr{q}"), now(m))
                act.wait_ge(S(f"mm{q}"), before(m))
                nc.scalar.activation(tp[q][:, :], ps[2 + q], ACT.Relu, bias=bg1c[:, :]).then_inc(S(f"ev{q}"), 1)

        def tensor(self, pe, m, i, u, windows):
            if windows:
                self.collect(pe, *later(m, i, u), 0)
            for q in range(2):
                pe.wait_ge(S(f"pre{q}"), now(m))
                pe.wait_ge(S(f"ev{q}"), before(m))
                pair_transposes(pe, tmp[1][q], ps[2 + q]).then_inc(S(f"tr{q}"), 1)
            if windows:
                self.collect(pe, *later(m, i, u), 1)
            for q in range(2):
                pe.wait_ge(S(f"ev{q}"), now(m))
                pe.wait_ge(S(f"y{q}"), before(m))
                pair_products(pe, tp[q], wg2, ps[4 + q]).then_inc(S(f"mm{q}"), 1)

    class Gcn2(Pass):
        loads = ((y2_t, load_a, D), (x1_t, load_b, D))
        stores = ((x2_t, store_a, D, ("out0", "out1")),)
        consumed = ("mean0", "mean1", "sum0", "sum1")

        def pre(self, u):
            return lambda q: (tmp[1], sq)[u][q][:, :]

        def take_block(self, ve, m, i, u, windows):
            V = nc.vector
            if not exists(m):
                return
            self.inputs_in(ve, i, u)
            for q in range(2):
                agg = self.sums_here(ve, m, i, u, q, windows)
                ve.wait_ge(S(f"pre{q}"), before(m))
                V.tensor_tensor(tmp[0][q][:, :], agg, group(load_a[u], q), ALU.add).then_inc(S(f"mean{q}"), 1)
            for q in range(2):
                ve.wait_ge(S(f"mean{q}"), now(m))
                ve.wait_ge(S(f"out{q}"), before(m - 1) if exists_before(m) else before(0))
                V.tensor_tensor(tiles3(self.pre(u)(q)), tiles3(tmp[0][q][:, :]), per_node(dis, m, q), ALU.mult).then_inc(S(f"scaled{q}"), 1)
            for q in range(2):
                ve.wait_ge(S(f"scaled{q}"), now(m))
                V.tensor_tensor(tmp[0][q][:, :], self.pre(u)(q), group(load_b[u], q), ALU.add).then_inc(S(f"sum{q}"), 1)
            for q in range(2):
                ve.wait_ge(S(f"sum{q}"), now(m))
                V.tensor_tensor(tiles3(self.pre(u)(q)), tiles3(tmp[0][q][:, :]), row(bg2r), ALU.add).then_inc(S(f"pre{q}"), 1)
            if exists_before(m):
                norm_out(ve, m - 1, None, (0, 1))
            norm_center(ve, m, self.pre(u), (0, 1))

        def vector(self, ve, m, i, u, windows):
            self.take_block(ve, *later(m, i, u), windows)
            if not exists(m + 1):
                norm_out(ve, m, None, (0, 1))
            self.hots_ahead(ve, m, u, windows)

        def scalar_loop(self, act, windows):
            for q in range(2):
                norm_square(act, 0, q, self.pre(0), True)
            super().scalar_loop(act, windows)

        def scalar(self, act, m, i, u, windows):
            norm_root(act, m)
            self.stored(act, i, u)
            for q in range(2):
                norm_apply(act, m, q, self.pre(u), store_a[u])
            if exists(m + 1):
                for q in range(2):
                    norm_square(act, m + 1, q, self.pre(1 - u), True)

        def tensor(self, pe, m, i, u, windows):
            if windows:
                for q in range(2):
                    self.collect(pe, *later(m, i, u), q)
                    stay_warm(pe, m * 2 + q, 9)

    class Gin(Pass):
        loads = ((x2_t, load_b, D),)
        stores = ((x3_t, store_a, D, ("out0", "out1")),)
        consumed = ("pre0", "pre1")

        def take(self, ve, m, i, u, q, windows):
            if not exists(m):
                return
            self.inputs_in(ve, i, u)
            agg = self.sums_here(ve, m, i, u, q, windows)
            ve.wait_ge(S(f"tr{q}"), before(m))
            nc.vector.tensor_tensor(load_a[q][:, 0:GT * D], agg, group(load_b[u], q), ALU.add).then_inc(S(f"mean{q}"), 1)

        def vector(self, ve, m, i, u, windows):
            V = nc.vector
            for q in range(2):
                ve.wait_ge(S(f"mm{q}"), now(m))
                ve.wait_ge(S(f"out{q}"), before(m))
                V.tensor_tensor(tiles3(tmp[0][q][:, :]), tiles3(ps[6 + q]), row(bi2r), ALU.add).then_inc(S(f"sum{q}"), 1)
            for q in range(2):
                ve.wait_ge(S(f"last{q}"), now(m))
                V.scalar_tensor_tensor(tmp[1][q][:, :], group(load_b[u], q), 2.0, tmp[1][q][:, :], ALU.mult, ALU.add).then_inc(S(f"pre{q}"), 1)
            norm_center(ve, m, pre_of)
            for q in range(2):
                self.take(ve, *later(m, i, u), q, windows)
            self.hots_ahead(ve, m, u, windows)
            norm_var(ve, m)
            self.stored(ve, i, u)
            norm_out(ve, m, store_a[u])

        def first_layer(self, act, m):
            if not exists(m):
                return
            for q in range(2):
                act.wait_ge(S(f"tr{q}"), now(m))
                act.wait_ge(S(f"hid{q}"), before(m))
                nc.scalar.activation(tp[q][:, :], ps[2 + q], ACT.Copy).then_inc(S(f"ev{q}"), 1)
            for q in range(2):
                act.wait_ge(S(f"hid{q}"), now(m))
                act.wait_ge(S(f"mm{q}"), before(m))
                nc.scalar.activation(tq[q][:, :], ps[4 + q], ACT.Relu, bias=bi1c[:, :]).then_inc(S(f"relu{q}"), 1)

        def scalar_loop(self, act, windows):
            self.first_layer(act, 0)
            super().scalar_loop(act, windows)

        def scalar(self, act, m, i, u, windows):
            for q in range(2):
                act.wait_ge(S(f"sum{q}"), now(m))
                nc.scalar.activation(tmp[1][q][:, :], tmp[0][q][:, :], ACT.Relu).then_inc(S(f"last{q}"), 1)
            for q in range(2):
                norm_square(act, m, q, pre_of)
            self.first_layer(act, m + 1)
            norm_root(act, m)

        def tensor(self, pe, m, i, u, windows):
            for q in range(2):
                pe.wait_ge(S(f"mean{q}"), now(m))
                pe.wait_ge(S(f"ev{q}"), before(m))
                pair_transposes(pe, load_a[q], ps[2 + q]).then_inc(S(f"tr{q}"), 1)
            for q in range(2):
                pe.wait_ge(S(f"ev{q}"), now(m))
                pe.wait_ge(S(f"relu{q}"), before(m))
                pe.matmul(ps[4 + q], wi1[:, :], tp[q][:, :], start=True, stop=True).then_inc(S(f"hid{q}"), 1)
            for q in range(2):
                pe.wait_ge(S(f"relu{q}"), now(m))
                pe.wait_ge(S(f"sum{q}"), before(m))
                pair_products(pe, tq[q], wi2, ps[6 + q]).then_inc(S(f"mm{q}"), 1)
            if windows:
                for q in range(2):
                    self.collect(pe, *later(m, i, u), q)

    CT = 4

    def tile_transposes(pe, src, bank):
        for r in range(CT):
            last = pe.transpose(bank[:, r * P:(r + 1) * P], src[:, r * P:(r + 1) * P], ident[:, :])
        return last

    def tile_products(pe, lhs, w, bank):
        for r in range(CT):
            last = pe.matmul(bank[:, r * P:(r + 1) * P], lhs[:, r * P:(r + 1) * P], w, start=True, stop=True)
        return last

    class Chunks(Pass):
        last_sum = "agg3"
        hot_used = ("agg1", "agg3")

        def collect_chunk(self, pe, m, i, u, c):
            if not exists(m):
                return
            if c == 0:
                self.rows_in(pe, i, u)
            if c % 2 == 0:
                pe.wait_ge(S(f"hot{c // 2}"), now(m))
            pe.wait_ge(S(f"mean{c}"), before(m))
            W = self.pitch
            sums(pe, m, range(c * CT, c * CT + CT), lambda j: ps[c][:, (j % CT) * W:(j % CT + 1) * W],
                 W, self.hot_at(u)).then_inc(S(f"agg{c}"), 1)

        def collect(self, pe, m, i, u, q):
            for c in (2 * q, 2 * q + 1):
                self.collect_chunk(pe, m, i, u, c)

    class Sage0(Chunks):
        pitch = D + 1
        ahead = 2
        loads = (None,)
        stores = ((s1_t, store_a, H, ("s13",)), (n1_t, store_b, H, ("n13",)))
        consumed = ("hid3",)

        def load_block(self, sp, m, u):
            sp.dma_start(load_a[u][0:D, :], a["x_cols"][:, bass.ds(m * BN, BN)]).then_inc(S(f"in{u}"), 16)

        def take(self, ve, m, i, u, q, windows):
            if not exists(m):
                return
            V = nc.vector
            for c in (2 * q, 2 * q + 1):
                cols = lambda t: t[:, bass.ds(m * NT + c * CT, CT)]
                if windows:
                    ve.wait_ge(S(f"agg{c}"), now(m))
                    agg = tiles3(ps[c][:, 0:CT * (D + 1)], D + 1)
                    V.tensor_scalar(cols(deg).unsqueeze(2), agg[:, :, D:D + 1], 0.0, None, ALU.add).then_inc(S(f"deg{q}"), 1)
                    ve.wait_ge(S(f"deg{q}"), before(m * 2 + (c % 2 + 1)))
                    agg = agg[:, :, 0:D]
                else:
                    ve.wait_ge(S(f"sums{u}"), landed(f"sums{u}", i))
                    agg = tiles3(general_sums(u, D)[:, c * CT * D:(c + 1) * CT * D])
                V.tensor_scalar(stat[:, q, 0, 0:CT], cols(deg), 1.0, None, ALU.max).then_inc(S(f"least{q}"), 1)
                ve.wait_ge(S(f"least{q}"), before(m * 2 + (c % 2 + 1)))
                V.reciprocal(cols(invdeg), stat[:, q, 0, 0:CT]).then_inc(S(f"inv{q}"), 1)
                ve.wait_ge(S(f"inv{q}"), before(m * 2 + (c % 2 + 1)))
                ve.wait_ge(S(f"tr{c}"), before(m))
                V.tensor_tensor(tiles3(load_b[q][:, (c % 2) * CT * P:(c % 2 + 1) * CT * P], P)[:, :, D:P], agg,
                                cols(invdeg).unsqueeze(2).to_broadcast([P, CT, D]), ALU.mult).then_inc(S(f"mean{c}"), 1)

        def vector_loop(self, ve, windows):
            for q in range(2):
                nc.vector.memset(load_b[q][:, :], 0.0).then_inc(S("zeros"), 1)
            if windows:
                nc.vector.memset(tiles3(ring[:, 0:RING * (D + 1)], D + 1)[:, :, D:D + 1], 1.0).then_inc(S("zeros"), 1)
            ve.wait_ge(S("zeros"), before(3 if windows else 2))
            super().vector_loop(ve, windows)

        def vector(self, ve, m, i, u, windows):
            V = nc.vector

            def own(c):
                ve.wait_ge(S(f"nmm{c}"), now(m))
                V.tensor_tensor(tiles3(store_a[u][:, c * 512:(c + 1) * 512], H), tiles3(ps[7], H), row(b1r, H, CT), ALU.add).then_inc(S(f"s1{c}"), 1)

            self.stored(ve, i, u)
            for q in range(2):
                own(2 * q)
                self.hot_ahead(ve, m, u, q, windows)
                own(2 * q + 1)
                self.take(ve, *later(m, i, u), q, windows)

        def scalar(self, act, m, i, u, windows):
            A = nc.scalar
            self.stored(act, i, u)

            def evacuate(c):
                act.wait_ge(S(f"tr{c}"), now(m))
                A.activation(load_a[u][D:P, c * 512:(c + 1) * 512], ps[4][D:P, :], ACT.Copy).then_inc(S(f"ev{c}"), 1)

            def hidden(c):
                act.wait_ge(S(f"hid{c}"), now(m))
                act.wait_ge(S(f"nmm{(c + 2) % 4}"), now(m) if c >= 2 else before(m))
                A.activation(tp[c % 2][:, :], ps[5], ACT.Relu, bias=b0c[:, :]).then_inc(S(f"rel{c}"), 1)

            def neighbours(c):
                act.wait_ge(S(f"nmm{c}"), now(m))
                A.activation(store_b[u][:, c * 512:(c + 1) * 512], ps[6], ACT.Copy).then_inc(S(f"n1{c}"), 1)

            evacuate(0)
            for c in range(4):
                if c < 3:
                    evacuate(c + 1)
                hidden(c)
                if c >= 1:
                    neighbours(c - 1)
            neighbours(3)

        def tensor(self, pe, m, i, u, windows):
            def former(name, c):
                pe.wait_ge(S(f"{name}{(c + 3) % 4}"), now(m) if c else before(m))

            def turn(c):
                pe.wait_ge(S(f"mean{c}"), now(m))
                former("ev", c)
                tile_transposes(pe, load_b[c // 2][:, (c % 2) * 512:(c % 2 + 1) * 512], ps[4]).then_inc(S(f"tr{c}"), 1)

            def hidden(c):
                pe.wait_ge(S(f"ev{c}"), now(m))
                former("rel", c)
                pe.matmul(ps[5], w0[:, :], load_a[u][:, c * 512:(c + 1) * 512], start=True, stop=True).then_inc(S(f"hid{c}"), 1)

            def products(c):
                pe.wait_ge(S(f"rel{c}"), now(m))
                former("n1", c)
                tile_products(pe, tp[c % 2], w1[:, 0:H], ps[6])
                former("s1", c)
                tile_products(pe, tp[c % 2], w1[:, H:2 * H], ps[7]).then_inc(S(f"nmm{c}"), 1)

            def next_sums(c):
                if windows:
                    self.collect_chunk(pe, *later(m, i, u), c)

            turn(0)
            self.inputs_in(pe, i, u)
            turn(1)
            hidden(0)
            next_sums(0)
            turn(2)
            hidden(1)
            products(0)
            next_sums(1)
            turn(3)
            hidden(2)
            products(1)
            next_sums(2)
            hidden(3)
            products(2)
            next_sums(3)
            products(3)

    class Sage1(Chunks):
        W = H
        pitch = H
        ahead = 2
        double = False
        loads = ((s1_t, load_a, H),)
        stores = ((s2_t, store_a, D, ("s23",)), (n2_t, store_b, D, ("n23",)))
        consumed = ("mean3",)

        def take(self, ve, m, i, u, q, windows):
            if not exists(m):
                return
            self.inputs_in(ve, i, u)
            for c in (2 * q, 2 * q + 1):
                if windows:
                    ve.wait_ge(S(f"agg{c}"), now(m))
                    agg = ps[c]
                else:
                    ve.wait_ge(S(f"sums{u}"), landed(f"sums{u}", i))
                    agg = general_sums(u, H)[:, c * 512:(c + 1) * 512]
                ve.wait_ge(S(f"tr{c}"), before(m))
                for r in range(CT):
                    last = nc.vector.scalar_tensor_tensor(
                        tmp[c % 2][q][:, r * P:(r + 1) * P], agg[:, r * P:(r + 1) * P],
                        invdeg[:, bass.ds(m * NT + c * CT + r, 1)], load_a[u][:, (c * CT + r) * P:(c * CT + r + 1) * P],
                        ALU.mult, ALU.add)
                last.then_inc(S(f"mean{c}"), 1)

        def vector(self, ve, m, i, u, windows):
            self.stored(ve, i, u)
            for q in range(2):
                self.take(ve, *later(m, i, u), q, windows)
                self.hot_ahead(ve, m, u, q, windows)
                for c in (2 * q, 2 * q + 1):
                    ve.wait_ge(S(f"mm{c}"), now(m))
                    nc.vector.tensor_tensor(tiles3(store_a[u][:, c * 256:(c + 1) * 256]), tiles3(ps[6 + c % 2], H)[:, :, 0:D],
                                            row(b2r, D, CT), ALU.add).then_inc(S(f"s2{c}"), 1)

        def scalar(self, act, m, i, u, windows):
            A = nc.scalar
            self.stored(act, i, u)

            def hidden(c):
                act.wait_ge(S(f"tr{c}"), now(m))
                act.wait_ge(S(f"mm{c}"), before(m))
                A.activation((tp, tq)[c // 2][c % 2][:, :], ps[4 + c % 2], ACT.Relu).then_inc(S(f"rel{c}"), 1)

            def neighbours(c):
                act.wait_ge(S(f"s2{c}"), now(m))
                A.activation(tiles3(store_b[u][:, c * 256:(c + 1) * 256]), tiles3(ps[6 + c % 2], H)[:, :, D:H], ACT.Copy).then_inc(S(f"n2{c}"), 1)

            hidden(0)
            hidden(1)
            neighbours(0)
            neighbours(1)
            hidden(2)
            hidden(3)
            neighbours(2)
            neighbours(3)

        def tensor(self, pe, m, i, u, windows):
            def former(name, c):
                pe.wait_ge(S(f"{name}{(c + 2) % 4}"), now(m) if c >= 2 else before(m))

            for q in range(2):
                for c in (2 * q, 2 * q + 1):
                    pe.wait_ge(S(f"mean{c}"), now(m))
                    former("rel", c)
                    tile_transposes(pe, tmp[c % 2][q], ps[4 + c % 2]).then_inc(S(f"tr{c}"), 1)
                if windows:
                    self.collect(pe, *later(m, i, u), q)
                for c in (2 * q, 2 * q + 1):
                    pe.wait_ge(S(f"rel{c}"), now(m))
                    former("n2", c)
                    tile_products(pe, (tp, tq)[c // 2][c % 2], w2[:, :], ps[6 + c % 2]).then_inc(S(f"mm{c}"), 1)

    class Messages(Pass):

        def emit(self):
            other = next_pass(self.number)
            gathered = store_a
            with nc.Block() as block:

                @block.sync
                def _(sp):
                    start_at_one(sp, other)

                    def general():
                        def index(c):
                            for buf, ix in ((ix_now, src_ix), (ix_dst, dst_ix)):
                                sp.dma_start(buf[:, bass.ds((c % 2) * IX, IX)], ix[:, bass.ds(c * IX, IX)]).then_inc(S("ix"), 16)

                        def edges(m, u):
                            sp.dma_start(load_a[u][0:DE, 0:ET * P], a["edge_cols"][:, bass.ds(m * ET * P, ET * P)]).then_inc(S(f"in{u}"), 16)

                        index(0)
                        sp.wait_ge(S("zeros"), now(1))
                        for u in range(2):
                            edges(u, u)

                        def body(m, i, u, v, c):
                            if v % 4 == 0 and exists(m + 4):
                                sp.wait_ge(S("tr1"), before(m))
                                sp.wait_ge(S("ix"), landed("ix", c, 2))
                                index(c + 1)
                            if exists(m + 2):
                                sp.wait_ge(S("hid1"), now(m))
                                edges(m + 2, u)
                            sp.wait_ge(S("msg1"), now(m))
                            sp.dma_start(msg_t[bass.ds(m * ET * P, ET * P), :].rearrange("(p t) f -> p (t f)", p=P),
                                         store_b[u][:, 0:ET * D]).then_inc(S(f"put{u}"), 16)

                        n = (NB - 2) // 4
                        with sp.Fori(0, n) as it:
                            for v in range(4):
                                body(it * 4 + v, it * 2 + v // 2, v % 2, v, it)
                        for m in range(n * 4, NB):
                            body(m, m // 2, m % 2, m, m // 4)
                        for u in range(2):
                            sp.wait_ge(S(f"put{u}"), before(16 * (NB // 2)))

                    both_ways(sp, general, lambda: None)

                @block.gpsimd
                def _(pool):
                    def general():
                        def body(m, v, c):
                            if v % 4 == 0:
                                pool.wait_ge(S("ix"), landed("ix", c, 2))
                            for h in range(2):
                                pool.wait_ge(S(f"tr{h}"), before(m))
                                gate(pool)
                                for t in range(HT):
                                    for k, ix in enumerate((ix_now, ix_dst)):
                                        to, at = t * P + k * D, v * ET + h * HT + t
                                        pool.indirect_dma_start(
                                            out=gathered[h][:, to:to + D], out_offset=None, in_=x3_t,
                                            in_offset=bass.IndirectOffsetOnAxis(ap=ix[:, at:at + 1], axis=0)).then_inc(S(f"pair{h}"), 16)

                        if NB >= RB:
                            with pool.Fori(0, NB // RB) as it:
                                for v in range(RB):
                                    body(it * RB + v, v, it * 2 + v // 4)
                        for m in range(NB // RB * RB, NB):
                            body(m, m % RB, m // 4)

                    both_ways(pool, general, lambda: None)

                @block.vector
                def _(ve):
                    def general():
                        for u in range(2):
                            nc.vector.memset(load_a[u][:, :], 0.0).then_inc(S("zeros"), 1)

                        def body(m, i, u):
                            ve.wait_ge(S(f"put{u}"), before(i * 16))
                            for h in range(2):
                                ve.wait_ge(S(f"mm{h}"), now(m))
                                nc.vector.tensor_tensor(tiles3(store_b[u][:, h * HT * D:(h + 1) * HT * D]),
                                                        tiles3(ps[4 + h], P)[:, :, 0:D], row(bm2r, D, HT), ALU.add).then_inc(S(f"msg{h}"), 1)

                        bodies(ve, body)

                    both_ways(ve, general, lambda: None)

                @block.scalar
                def _(act):
                    def general():
                        def body(m, i, u):
                            for h in range(2):
                                act.wait_ge(S(f"tr{h}"), now(m))
                                nc.scalar.activation(tp[h][:, :], ps[h], ACT.Copy).then_inc(S(f"ev{h}"), 1)
                            for h in range(2):
                                act.wait_ge(S(f"hid{h}"), now(m))
                                nc.scalar.activation(tq[h][:, :], ps[2 + h], ACT.Relu, bias=bm1c[:, :]).then_inc(S(f"rel{h}"), 1)

                        bodies(act, body)

                    both_ways(act, general, lambda: None)

                @block.tensor
                def _(pe):
                    def general():
                        def body(m, i, u):
                            for h in range(2):
                                pe.wait_ge(S(f"pair{h}"), landed(f"pair{h}", m, 2 * HT))
                                pe.wait_ge(S(f"ev{h}"), before(m))
                                tile_transposes(pe, gathered[h], ps[h]).then_inc(S(f"tr{h}"), 1)
                            pe.wait_ge(S(f"in{u}"), landed(f"in{u}", i))
                            for h in range(2):
                                pe.wait_ge(S(f"ev{h}"), now(m))
                                pe.wait_ge(S(f"rel{h}"), before(m))
                                pe.matmul(ps[2 + h], wm1[:, :], tp[h][:, :], start=True, stop=False)
                                pe.matmul(ps[2 + h], wm1e[:, :], load_a[u][:, h * 512:(h + 1) * 512], start=False, stop=True).then_inc(S(f"hid{h}"), 1)
                            for h in range(2):
                                pe.wait_ge(S(f"rel{h}"), now(m))
                                pe.wait_ge(S(f"msg{h}"), before(m))
                                tile_products(pe, tq[h], wm2[:, :], ps[4 + h]).then_inc(S(f"mm{h}"), 1)

                        bodies(pe, body)

                    both_ways(pe, general, lambda: None)

    class Update(Pass):
        loads = ((x3_t, load_b, D),)
        stores = ((out, store_a, D, ("out0", "out1")),)
        consumed = ("pre0", "pre1")
        MINE = GT * P

        def pairs(self, u, h):
            return store_a[h][:, NT * D + u * 512:NT * D + (u + 1) * 512]

        def edges(self, u):
            return load_a[u][:, self.MINE:self.MINE + ET * P]

        def use(self, kind, c, m):
            return m + 2 if kind == "m" else m * 2 + c // 2

        def wait_former(self, eng, signal, kind, c, m, windows):
            s = c % 2
            if kind == "m":
                eng.wait_ge(S(f"m{signal}{s}"), before(m + 2))
                if not isinstance(m, int) or m > 0:
                    eng.wait_ge(S(f"u{signal}{s}"), before(m * 2))
            elif c >= 2:
                eng.wait_ge(S(f"u{signal}{s}"), now(m * 2))
            elif windows and exists(m + 2):
                eng.wait_ge(S(f"m{signal}{s}"), now(m + 2))
            else:
                eng.wait_ge(S(f"u{signal}{s}"), before(m * 2))

        def load_index(self, sp, c):
            for buf, ix in ((ix_now, src_ix), (ix_dst, dst_ix)):
                sp.dma_start(buf[:, bass.ds((c % 2) * IX, IX)], ix[:, bass.ds(c * IX, IX)]).then_inc(S("ix"), 16)

        def load_edges(self, sp, n, u):
            sp.dma_start(self.edges(u)[0:DE, :], a["edge_cols"][:, bass.ds(n * ET * P, ET * P)]).then_inc(S(f"edges{u}"), 16)

        def sync_rows_first(self, sp):
            self.load_index(sp, 0)
            sp.wait_ge(S("zeros"), now(1))
            for u in range(2):
                self.load_edges(sp, u, u)
            sp.wait_ge(S("mhid1"), now(0))
            self.load_edges(sp, 2, 0)

        def sync_rows(self, sp, m, i, u, v):
            if exists(m + 3):
                sp.wait_ge(S("mhid1"), now(m + 1))
                self.load_edges(sp, m + 3, 1 - u)
            if v % 4 == 0 and exists(m + 4):
                c = m // 4 if isinstance(m, int) else self.chunk
                sp.wait_ge(S("agg1"), before(m))
                sp.wait_ge(S("ix"), landed("ix", c, 2))
                self.load_index(sp, c + 1)

        def gpsimd_windows(self, pool):
            def block(m, v, i, c):
                u = v % 2
                if v % 4 == 0:
                    pool.wait_ge(S("ix"), landed("ix", c, 2))
                if not isinstance(m, int) or m >= 2:
                    pool.wait_ge(S(f"pair{u}"), landed(f"pair{u}", i - 1, 2 * ET))
                    for h in range(2):
                        pool.wait_ge(S(f"mtr{h}"), before(m - 1))
                gate(pool)
                for h in range(2):
                    for t in range(HT):
                        for k, ix in enumerate((ix_now, ix_dst)):
                            to, at = t * P + k * D, v * ET + h * HT + t
                            pool.indirect_dma_start(
                                out=self.pairs(u, h)[:, to:to + D], out_offset=None, in_=x3_t,
                                in_offset=bass.IndirectOffsetOnAxis(ap=ix[:, at:at + 1], axis=0)).then_inc(S(f"pair{u}"), 16)

            for m in range(min(RB, NB)):
                block(m, m, m // 2, m // 4)
            n = max(NB - RB, 0) // RB
            if n:
                with pool.Fori(1, n + 1) as it:
                    for v in range(RB):
                        block(it * RB + v, v, it * (RB // 2) + v // 2, it * 2 + v // 4)
            for m in range((n + 1) * RB, NB):
                block(m, m % RB, m // 2, m // 4)

        def message(self, ve, m, h):
            n = m + 2
            ve.wait_ge(S(f"mmm{h}"), now(n))
            nc.vector.tensor_tensor(tiles3(ring[:, bass.ds((n % RB) * (ET * D) + h * HT * D, HT * D)]),
                                    tiles3(ps[6 + h], P)[:, :, 0:D], row(bm2r, D, HT), ALU.add).then_inc(S(f"msum{h}"), 1)

        def messages(self, ve, m, windows):
            if windows and exists(m + 2):
                for h in range(2):
                    self.message(ve, m, h)

        def take(self, ve, m, i, u, q, windows):
            if not exists(m):
                return
            agg = self.sums_here(ve, m, i, u, q, windows)
            for s in range(2):
                ve.wait_ge(S(f"utr{s}"), before(m * 2))
            nc.vector.tensor_copy(tiles3(load_a[q][:, 0:self.MINE], P)[:, :, D:P], tiles3(agg)).then_inc(S(f"mean{q}"), 1)

        def vector_loop(self, ve, windows):
            for u in range(2):
                nc.vector.memset(self.edges(u), 0.0).then_inc(S("zeros"), 1)
            for m in range(self.ahead - 1):
                self.hots(ve, m, m, windows)
            for m in (-2, -1):
                self.messages(ve, m, windows)
            self.take_block(ve, 0, 0, 0, windows)
            self.hots(ve, self.ahead - 1, (self.ahead - 1) % 2, windows)
            self.messages(ve, 0, windows)
            bodies(ve, lambda m, i, u: self.vector(ve, m, i, u, windows), behind=4)

        def vector(self, ve, m, i, u, windows):
            V = nc.vector
            self.inputs_in(ve, i, u)
            for q in range(2):
                ve.wait_ge(S(f"out{q}"), before(m))
                for c in (2 * q, 2 * q + 1):
                    ve.wait_ge(S(f"umm{c % 2}"), now(self.use("u", c, m)))
                    V.tensor_tensor(tiles3(tmp[0][q][:, (c % 2) * 256:(c % 2 + 1) * 256]),
                                    tiles3(ps[6 + c % 2], P)[:, :, 0:D], row(bu2r, D, CT), ALU.add).then_inc(S(f"usum{c % 2}"), 1)
            self.take_block(ve, *later(m, i, u), windows)
            for q in range(2):
                ve.wait_ge(S("usum1"), now(m * 2 + q))
                ve.wait_ge(S(f"xc{q}"), before(m))
                V.tensor_tensor(tmp[1][q][:, :], tmp[0][q][:, :], group(load_b[u], q), ALU.add).then_inc(S(f"pre{q}"), 1)
            norm_center(ve, m, pre_of)
            self.hot_ahead(ve, m, u, 0, windows)
            self.messages(ve, m + 1, windows)
            self.hot_ahead(ve, m, u, 1, windows)
            norm_var(ve, m)
            self.stored(ve, i, u)
            norm_out(ve, m, store_a[u])

        def own(self, act, m, i, u):
            if not exists(m):
                return
            self.inputs_in(act, i, u)
            for q in range(2):
                for s in range(2):
                    act.wait_ge(S(f"utr{s}"), before(m * 2))
                nc.scalar.activation(tiles3(load_a[q][:, 0:self.MINE], P)[:, :, 0:D], tiles3(group(load_b[u], q)), ACT.Copy).then_inc(S(f"own{q}"), 1)

        def turned(self, act, kind, c, m, windows):
            n, s = self.use(kind, c, m), c % 2
            act.wait_ge(S(f"{kind}tr{s}"), now(n))
            self.wait_former(act, "hid", kind, c, m, windows)
            nc.scalar.activation(tp[s][:, :], ps[2 + s], ACT.Copy).then_inc(S(f"{kind}ev{s}"), 1)

        def bent(self, act, kind, c, m, windows):
            n, s = self.use(kind, c, m), c % 2
            act.wait_ge(S(f"{kind}hid{s}"), now(n))
            self.wait_former(act, "mm", kind, c, m, windows)
            nc.scalar.activation(tq[s][:, :], ps[4 + s], ACT.Relu, bias=(bm1c if kind == "m" else bu1c)[:, :]).then_inc(S(f"{kind}rel{s}"), 1)

        def message_units(self, act, m, windows):
            if windows and exists(m + 2):
                for h in range(2):
                    self.turned(act, "m", h, m, windows)
                for h in range(2):
                    self.bent(act, "m", h, m, windows)

        def scalar_loop(self, act, windows):
            for m in (-2, -1):
                self.message_units(act, m, windows)
            self.own(act, 0, 0, 0)
            self.message_units(act, 0, windows)
            bodies(act, lambda m, i, u: self.scalar(act, m, i, u, windows), behind=4)

        def scalar(self, act, m, i, u, windows):
            self.turned(act, "u", 0, m, windows)
            for c in range(4):
                if c < 3:
                    self.turned(act, "u", c + 1, m, windows)
                self.bent(act, "u", c, m, windows)
            self.own(act, *later(m, i, u))
            self.message_units(act, m + 1, windows)
            for q in range(2):
                norm_square(act, m, q, pre_of)
            norm_root(act, m)

        def turn(self, pe, kind, c, m, i, u, windows):
            n, s = self.use(kind, c, m), c % 2
            if kind == "m":
                pe.wait_ge(S(f"pair{u}"), landed(f"pair{u}", i + 1, 2 * ET))
                source = self.pairs(u, c)
            else:
                pe.wait_ge(S(f"mean{c // 2}"), now(m))
                pe.wait_ge(S(f"own{c // 2}"), now(m))
                source = load_a[c // 2][:, s * 512:(s + 1) * 512]
            self.wait_former(pe, "ev", kind, c, m, windows)
            tile_transposes(pe, source, ps[2 + s]).then_inc(S(f"{kind}tr{s}"), 1)

        def hidden(self, pe, kind, c, m, i, u, windows):
            n, s = self.use(kind, c, m), c % 2
            pe.wait_ge(S(f"{kind}ev{s}"), now(n))
            self.wait_former(pe, "rel", kind, c, m, windows)
            if kind == "m":
                pe.wait_ge(S(f"edges{u}"), landed(f"edges{u}", i + 1))
                pe.matmul(ps[4 + s], wm1[:, :], tp[s][:, :], start=True, stop=False)
                pe.matmul(ps[4 + s], wm1e[:, :], self.edges(u)[:, c * 512:(c + 1) * 512], start=False, stop=True).then_inc(S(f"mhid{s}"), 1)
            else:
                pe.matmul(ps[4 + s], wu1[:, :], tp[s][:, :], start=True, stop=True).then_inc(S(f"uhid{s}"), 1)

        def products(self, pe, kind, c, m, windows):
            n, s = self.use(kind, c, m), c % 2
            pe.wait_ge(S(f"{kind}rel{s}"), now(n))
            self.wait_former(pe, "sum", kind, c, m, windows)
            tile_products(pe, tq[s], (wm2 if kind == "m" else wu2)[:, :], ps[6 + s]).then_inc(S(f"{kind}mm{s}"), 1)

        def rows_in(self, pe, m):
            for h in range(2):
                pe.wait_ge(S(f"msum{h}"), now(m))

        def collect(self, pe, m, i, u, q):
            if not exists(m):
                return
            if q == 0:
                self.rows_in(pe, m)
            pe.wait_ge(S(f"hot{q}"), now(m))
            pe.wait_ge(S(f"mean{q}"), before(m))
            sums(pe, m, range(q * GT, q * GT + GT), lambda j: ps[q][:, (j % GT) * D:(j % GT + 1) * D],
                 D, self.hot_at(u)).then_inc(S(f"agg{q}"), 1)

        def tensor_loop(self, pe, windows):
            if windows:
                for m in (-2, -1):
                    for h in range(2):
                        self.turn(pe, "m", h, m, -1, m + 2, windows)
                    for h in range(2):
                        self.hidden(pe, "m", h, m, -1, m + 2, windows)
                    for h in range(2):
                        self.products(pe, "m", h, m, windows)
                for q in range(2):
                    self.collect(pe, 0, 0, 0, q)
            bodies(pe, lambda m, i, u: self.tensor(pe, m, i, u, windows))

        def tensor(self, pe, m, i, u, windows):
            both = windows and exists(m + 2)
            if both:
                for h in range(2):
                    self.turn(pe, "m", h, m, i, u, windows)
                for h in range(2):
                    self.hidden(pe, "m", h, m, i, u, windows)
                self.products(pe, "m", 0, m, windows)
            if windows:
                self.collect(pe, *later(m, i, u), 0)
            if both:
                self.products(pe, "m", 1, m, windows)
            for c in range(2):
                self.turn(pe, "u", c, m, i, u, windows)
            if windows:
                self.collect(pe, *later(m, i, u), 1)
            for c in range(4):
                self.hidden(pe, "u", c, m, i, u, windows)
                if c < 2:
                    self.turn(pe, "u", c + 2, m, i, u, windows)
                if c >= 1:
                    self.products(pe, "u", c - 1, m, windows)
            self.products(pe, "u", 3, m, windows)

    def roots(number):
        other = next_pass(number)
        T = z.tiles
        above, root, quot = store_a[0][:, 0:T], store_a[1][:, 0:T], store_b[0][:, 0:T]
        with nc.Block() as block:

            @block.sync
            def _(sp):
                start_at_one(sp, other)

            @block.scalar
            def _(act):
                act.wait_ge(S("above"), now(0))
                nc.scalar.activation(root, above, ACT.Sqrt).then_inc(S("root"), 1)

            @block.vector
            def _(ve):
                V = nc.vector
                V.tensor_scalar(above, deg[:, :], 1.0, None, ALU.add).then_inc(S("above"), 1)
                ve.wait_ge(S("root"), now(0))
                V.reciprocal(quot, root).then_inc(S("inverse"), 1)
                ve.wait_ge(S("inverse"), now(0))
                V.tensor_tensor(quot, quot, above, ALU.mult).then_inc(S("quotient"), 1)
                ve.wait_ge(S("quotient"), now(0))
                V.tensor_tensor(quot, quot, root, ALU.add).then_inc(S("twice"), 1)
                ve.wait_ge(S("twice"), now(0))
                V.reciprocal(above, quot).then_inc(S("half"), 1)
                ve.wait_ge(S("half"), now(0))
                V.tensor_scalar(dis[:, :], above, 2.0, None, ALU.mult).then_inc(S("dis"), 1)
                ve.wait_ge(S("dis"), now(0))

    class Degrees(Pass):
        loads = ()
        stores = ()

        def emit(self):
            other = next_pass(self.number)
            with nc.Block() as block:

                @block.sync
                def _(sp):
                    start_at_one(sp, other)

                    def general():
                        self.gen.sync(sp)
                        sp.wait_ge(S("g_all"), now(0))
                        with sp.Fori(0, NB) as m:
                            sp.wait_ge(S("deg"), before(m))
                            self.load_sums(sp, m, 0)
                        sp.wait_ge(S("deg"), now(NB - 1))

                    both_ways(sp, general, lambda: None)

                @block.gpsimd
                def _(pool):
                    both_ways(pool, lambda: self.gen.gpsimd(pool), lambda: None)

                @block.vector
                def _(ve):
                    def general():
                        self.gen.vector(ve)
                        with ve.Fori(0, NB) as m:
                            ve.wait_ge(S("sums0"), landed("sums0", m))
                            nc.vector.tensor_scalar(deg[:, bass.ds(m * NT, NT)], tiles3(general_sums(0, D))[:, :, 0], 0.0, None, ALU.add).then_inc(S("deg"), 1)

                    both_ways(ve, general, lambda: None)

                @block.tensor
                def _(pe):
                    both_ways(pe, lambda: self.gen.tensor(pe), lambda: None)

            pass_over(self)

    with ctx:
        setup()
        Degrees(1, None, General(sums_t, D)).emit()
        Sage0(2, a["x_rows"], General(sums_t, D, table=a["x_rows"])).emit()
        roots(3)
        Sage1(4, n1_t, General(sums2_t, H, table=n1_t)).emit()
        Sage2(5, n2_t, General(sums_t, D, table=n2_t)).emit()
        Gcn1(6, y1_t, General(sums_t, D, table=y1_t)).emit()
        Gcn2(7, y2_t, General(sums_t, D, table=y2_t)).emit()
        Gin(8, x2_t, General(sums_t, D, table=x2_t)).emit()
        Messages(9, x3_t, None).emit()
        Update(10, None, General(sums_t, D, direct=msg_t)).emit()


OUT_ROWS = (100000, D)
WEIGHTS = ["L0_gnn_ws0", "L0_gnn_wn0", "L0_gnn_b0", "L0_gnn_ws1", "L0_gnn_wn1", "L0_gnn_b1", "L0_gnn_ws2", "L0_gnn_wn2",
           "L0_gnn_b2", "L1_gnn_W1", "L1_gnn_b1", "L1_gnn_W2", "L1_gnn_b2", "L2_gnn_W1", "L2_gnn_b1", "L2_gnn_W2", "L2_gnn_b2",
           "L3_gnn_mW1", "L3_gnn_mb1", "L3_gnn_mW2", "L3_gnn_mb2", "L3_gnn_uW1", "L3_gnn_ub1", "L3_gnn_uW2", "L3_gnn_ub2"]


def kernel(**inputs):
    import numpy as np
    import concourse.bacc as bacc
    from concourse.bass_utils import run_bass_kernel_spmd as run

    x, src, dst, edge = (np.asarray(inputs[n]) for n in ("x", "src", "dst", "edge_attr_32"))
    z = Sizes(x.shape[0], src.shape[0])
    E = z.etiles * P
    x_pad = np.zeros((z.rows, D), x.dtype)
    x_pad[BN:BN + z.nodes] = x
    x_rows = np.ascontiguousarray(x_pad.reshape(z.nb, NT, P, D).transpose(0, 2, 1, 3)).reshape(z.rows, D)
    x_cols = np.ascontiguousarray(x_pad.T)
    src_pad = np.zeros(E, np.int32)
    src_pad[:z.edges] = src
    dst_pad = np.full(E + P, z.pad_node, np.int32)
    dst_pad[:z.edges] = dst
    by_tile = lambda v: np.ascontiguousarray(v.reshape(z.etiles, P).T)
    edge_pad = np.zeros((DE, E), edge.dtype)
    edge_pad[:, :z.edges] = edge.T
    arrays = {
        "x_rows": x_rows, "x_cols": x_cols, "edge_cols": edge_pad,
        "src_pt": by_tile(src_pad), "dst_pt": by_tile(dst_pad[:E]), "dstn_pt": by_tile(dst_pad[1:E + 1]),
        "dst_rows": dst_pad.reshape(z.etiles + 1, P),
    }
    for n in WEIGHTS:
        arrays[n] = np.ascontiguousarray(inputs[n])
    nc = bacc.Bacc("TRN2", target_bir_lowering=False, num_devices=1)
    a = {n: nc.dram_tensor(n, v.shape, mybir.dt.from_np(v.dtype), kind="ExternalInput").ap() for n, v in arrays.items()}
    out = nc.dram_tensor("out", [z.rows, D], F32, kind="ExternalOutput").ap()
    build(nc, z, a, out)
    r = run(nc, [arrays], core_ids=[0])
    got = np.asarray(r.results[0]["out"]).reshape(z.nb, P, NT, D).transpose(0, 2, 1, 3).reshape(z.rows, D)
    return np.ascontiguousarray(got[BN:BN + z.nodes])
```
